# Optimizing a Trainium2 kernel written in Bass

```python
import numpy as np
import jax
import jax.numpy as jnp

def _softmax(x, axis=-1):
    return jax.nn.softmax(x, axis=axis)

def _gelu(x):
    return jax.nn.gelu(x, approximate=True)

def _silu(x):
    return jax.nn.silu(x)

def _sigmoid(x):
    return jax.nn.sigmoid(x)

def _layernorm(x, axis=-1, eps=1e-05):
    m = jnp.mean(x, axis=axis, keepdims=True)
    v = jnp.var(x, axis=axis, keepdims=True)
    return (x - m) / jnp.sqrt(v + eps)

def _scatter_add(tgt, idx, src, axis=0):
    return tgt.at[idx].add(src)

def _segment_sum(src, seg, n):
    return jax.ops.segment_sum(src, seg, n)
kernel_name = 'mk_decoder_postln_d4_seqx_r8_6c4b97'

def setup_inputs(seed: int=0):
    np.random.seed(seed)
    _w = jnp.asarray

    def _rec_inputs():
        import jax
        import jax.numpy as jnp
        _rk = jax.random.key(seed)
        x = 7.22e-05 + 1 * jax.random.normal(jax.random.fold_in(_rk, 1), (128, 64, 128), jnp.float32)
        _lenS = 64 - jax.random.randint(jax.random.fold_in(_rk, 7), (128,), 0, max(1, 64 // 4) + 1, jnp.int32)
        _lenS2 = 64 - jax.random.randint(jax.random.fold_in(_rk, 8), (128,), 0, max(1, 64 // 4) + 1, jnp.int32)
        _ctx_1024P = jax.random.normal(jax.random.fold_in(_rk, 11), (128, 16, 128), jnp.float32)
        _ctx_1024c = jax.random.dirichlet(jax.random.fold_in(_rk, 511), 0.3 * jnp.ones((16,), jnp.float32), (128, 64))
        _ctx_1024t = jnp.einsum('bsk,bkd->bsd', _ctx_1024c, _ctx_1024P)
        _ctx_1024t = _ctx_1024t * jax.lax.rsqrt(jnp.mean(jnp.square(_ctx_1024t)) + 1e-12) * 0.953939
        ctx_1024 = 4.13588e-05 + 0.999923 * (_ctx_1024t + 0.3 * jax.random.normal(jax.random.fold_in(_rk, 611), (128, 64, 128), jnp.float32))
        itok_Bx1xSx1_0_63 = jax.random.randint(jax.random.fold_in(_rk, 13), (128, 1, 64, 1), 0, 64, jnp.int32)
        _validS = jnp.arange(64)[None, :] < _lenS[:, None]
        _validS2 = jnp.arange(64)[None, :] < _lenS2[:, None]
        _causal = jnp.tril(jnp.ones((64, 64), dtype=bool))
        mask_BxS2_ik0 = jnp.where(jnp.broadcast_to(_validS2[:, :], (128, 64)), 0, 1).astype(jnp.int32)
        return (x, ctx_1024, itok_Bx1xSx1_0_63, mask_BxS2_ik0)
    x, ctx_1024, itok_Bx1xSx1_0_63, mask_BxS2_ik0 = _rec_inputs()

    def _L0_attn_setup():
        import jax, jax.numpy as jnp
        import numpy as np
        import math
        D_MODEL = 128
        NUM_HEADS = 16
        THETA = 10000.0

        def _rope(x, theta):
            n, d_k = (x.shape[-2], x.shape[-1])
            powers = jnp.arange(0, d_k, 2, dtype=jnp.float32) / d_k
            freqs = 1.0 / theta ** powers
            t = jnp.arange(n, dtype=jnp.float32)
            angles = jnp.outer(t, freqs)
            cos = jnp.cos(angles).astype(x.dtype)
            sin = jnp.sin(angles).astype(x.dtype)
            x_even = x[..., 0::2]
            x_odd = x[..., 1::2]
            rot_even = x_even * cos - x_odd * sin
            rot_odd = x_even * sin + x_odd * cos
            return jnp.stack([rot_even, rot_odd], axis=-1).reshape(x.shape)
        key = jax.random.key(seed)
        ks = jax.random.split(key, 5)
        B, N, D = (2, 256, D_MODEL)
        std = math.sqrt(2.0 / (D + D))
        x = jax.random.normal(ks[0], (B, N, D), dtype=jnp.float32)
        wq = jax.random.normal(ks[1], (D, D), dtype=jnp.float32) * std
        wk = jax.random.normal(ks[2], (D, D), dtype=jnp.float32) * std
        wv = jax.random.normal(ks[3], (D, D), dtype=jnp.float32) * std
        wo = jax.random.normal(ks[4], (D, D), dtype=jnp.float32) * std
        return {'x': x, 'wq': wq, 'wk': wk, 'wv': wv, 'wo': wo}
    _L0_attn_all = _L0_attn_setup()
    _L0_attn_in = {k: v for k, v in _L0_attn_all.items() if k in ('wq', 'wk', 'wv', 'wo')}
    del _L0_attn_all

    def _L0_xattn_setup():
        import jax, jax.numpy as jnp
        import numpy as np
        B, S, E, H = (4, 256, 128, 16)
        HD = E // H
        EPS = 1.1920928955078125e-07

        def _rmsnorm(x, w):
            ms = jnp.mean(x * x, axis=-1, keepdims=True)
            return x * jax.lax.rsqrt(ms + EPS) * w

        def _rope(x, start_pos=0):
            seq_len = x.shape[-2]
            inv_freq = 1.0 / 10000.0 ** (jnp.arange(0, HD, 2, dtype=jnp.float32) / HD)
            t = jnp.arange(start_pos, start_pos + seq_len, dtype=jnp.float32)
            freqs = t[:, None] * inv_freq[None, :]
            cos = jnp.cos(freqs)[None, None]
            sin = jnp.sin(freqs)[None, None]
            x1 = x[..., 0::2]
            x2 = x[..., 1::2]
            o1 = x1 * cos - x2 * sin
            o2 = x1 * sin + x2 * cos
            return jnp.stack((o1, o2), axis=-1).reshape(x.shape)
        key = jax.random.key(seed)
        k1, k2, k3, k4 = jax.random.split(key, 4)
        lim = 1.0 / np.sqrt(E)
        return {'q': jax.random.normal(k1, (B, S, E), jnp.float32), 'k': jax.random.normal(k2, (B, S, E), jnp.float32), 'v': jax.random.normal(k3, (B, S, E), jnp.float32), 'q_norm_w': jnp.ones((HD,), jnp.float32), 'k_norm_w': jnp.ones((HD,), jnp.float32), 'proj_w': jax.random.uniform(k4, (E, E), jnp.float32, -lim, lim), 'proj_b': jnp.zeros((E,), jnp.float32)}
    _L0_xattn_all = _L0_xattn_setup()
    _L0_xattn_in = {k: v for k, v in _L0_xattn_all.items() if k in ('q_norm_w', 'k_norm_w', 'proj_w', 'proj_b')}
    del _L0_xattn_all

    def _L0_ffn_setup():
        import jax, jax.numpy as jnp
        import numpy as np
        S, B, H = (256, 1, 128)
        E, K, F = (8, 2, 176)
        key = jax.random.key(seed)
        k1, k2, k3, k4 = jax.random.split(key, 4)
        return {'hidden_states': jax.random.normal(k1, (S, B, H), jnp.float32), 'router_weight': jax.random.normal(k2, (H, E), jnp.float32) * 0.02, 'w1': jax.random.normal(k3, (E, H, 2 * F), jnp.float32) * 0.02, 'w2': jax.random.normal(k4, (E, F, H), jnp.float32) * 0.02}
    _L0_ffn_all = _L0_ffn_setup()
    _L0_ffn_in = {k: v for k, v in _L0_ffn_all.items() if k in ('router_weight', 'w1', 'w2')}
    del _L0_ffn_all

    def _L1_attn_setup():
        import jax, jax.numpy as jnp
        import numpy as np
        HIDDEN = 128
        NUM_HEADS = 16
        HEAD_DIM = 64
        NUM_KV_HEADS = 4

        def _xavier(key, out_dim, in_dim):
            limit = jnp.sqrt(6.0 / (in_dim + out_dim)).astype(jnp.float32)
            return jax.random.uniform(key, (out_dim, in_dim), jnp.float32, -limit, limit)
        key = jax.random.key(seed)
        kx, kq, kk, kv, ko = jax.random.split(key, 5)
        return {'hidden_states': jax.random.normal(kx, (2, 256, HIDDEN), jnp.float32), 'Wq': _xavier(kq, NUM_HEADS * HEAD_DIM, HIDDEN), 'Wk': _xavier(kk, NUM_KV_HEADS * HEAD_DIM, HIDDEN), 'Wv': _xavier(kv, NUM_KV_HEADS * HEAD_DIM, HIDDEN), 'Wo': _xavier(ko, HIDDEN, NUM_HEADS * HEAD_DIM)}
    _L1_attn_all = _L1_attn_setup()
    _L1_attn_in = {k: v for k, v in _L1_attn_all.items() if k in ('Wq', 'Wk', 'Wv', 'Wo')}
    del _L1_attn_all

    def _L1_xattn_setup():
        import jax, jax.numpy as jnp
        import numpy as np
        B, S, D, H = (2, 256, 128, 16)
        HD = D // H

        def _split_heads(x):
            Bb, Ss, Dd = x.shape
            return x.reshape(Bb, Ss, H, HD).transpose(0, 2, 1, 3)
        key0 = jax.random.key(seed)
        ks = jax.random.split(key0, 12)
        scale = 1.0 / np.sqrt(D)
        inp = {'query': jax.random.normal(ks[0], (B, S, D), jnp.float32), 'key': jax.random.normal(ks[1], (B, S, D), jnp.float32), 'value': jax.random.normal(ks[2], (B, S, D), jnp.float32), 'mask': jax.random.randint(ks[3], (B, S), 0, 2, jnp.int32), 'Wq': jax.random.normal(ks[4], (D, D), jnp.float32) * scale, 'bq': jnp.zeros((D,), jnp.float32), 'Wk': jax.random.normal(ks[5], (D, D), jnp.float32) * scale, 'bk': jnp.zeros((D,), jnp.float32), 'Wv': jax.random.normal(ks[6], (D, D), jnp.float32) * scale, 'bv': jnp.zeros((D,), jnp.float32), 'Wo': jax.random.normal(ks[7], (D, D), jnp.float32) * scale, 'bo': jnp.zeros((D,), jnp.float32)}
        return inp
    _L1_xattn_all = _L1_xattn_setup()
    _L1_xattn_in = {k: v for k, v in _L1_xattn_all.items() if k in ('Wq', 'bq', 'Wk', 'bk', 'Wv', 'bv', 'Wo', 'bo')}
    del _L1_xattn_all

    def _L1_ffn_setup():
        import jax, jax.numpy as jnp
        import numpy as np
        NHEAD = 16
        NUM_GROUPS = 4
        EXPERTS_PER_GROUP = 2
        LN_EPS = 1e-05

        def _layernorm(x, g, b):
            mu = jnp.mean(x, axis=-1, keepdims=True)
            var = jnp.mean(jnp.square(x - mu), axis=-1, keepdims=True)
            return (x - mu) * jax.lax.rsqrt(var + LN_EPS) * g + b

        def _mha(x, wi, bi, wo, bo):
            B, S, D = x.shape
            hd = D // NHEAD
            qkv = x @ wi.T + bi
            q, k, v = jnp.split(qkv, 3, axis=-1)

            def heads(t):
                return t.reshape(B, S, NHEAD, hd).transpose(0, 2, 1, 3)
            q, k, v = (heads(q), heads(k), heads(v))
            scores = jnp.einsum('bhqd,bhkd->bhqk', q, k) / jnp.sqrt(jnp.asarray(hd, x.dtype))
            attn = jax.nn.softmax(scores, axis=-1)
            o = jnp.einsum('bhqk,bhkd->bhqd', attn, v)
            o = o.transpose(0, 2, 1, 3).reshape(B, S, D)
            return o @ wo.T + bo

        def _hier_moe(x, w_group, b_group, w_expert, b_expert, w1, b1, w2, b2):
            B, S, D = x.shape
            xt = x.reshape(B * S, D)
            T = xt.shape[0]
            E = NUM_GROUPS * EXPERTS_PER_GROUP
            gp = jax.nn.softmax(xt @ w_group + b_group, axis=-1)
            g_idx = jnp.argmax(gp, axis=-1)
            g_prob = jnp.max(gp, axis=-1)
            elog = jnp.einsum('td,gde->tge', xt, w_expert) + b_expert
            ep = jax.nn.softmax(elog, axis=-1)
            ep_sel = jnp.take_along_axis(ep, g_idx[:, None, None], axis=1)[:, 0, :]
            e_idx_local = jnp.argmax(ep_sel, axis=-1)
            e_prob = jnp.max(ep_sel, axis=-1)
            flat_e = g_idx * EXPERTS_PER_GROUP + e_idx_local
            combine = jax.nn.one_hot(flat_e, E, dtype=xt.dtype) * (g_prob * e_prob)[:, None]
            h = jax.nn.relu(jnp.einsum('td,edf->etf', xt, w1) + b1[:, None, :])
            y = jnp.einsum('etf,efd->etd', h, w2) + b2[:, None, :]
            out = jnp.einsum('te,etd->td', combine, y)
            return out.reshape(B, S, D)
        key = jax.random.key(seed)
        ks = jax.random.split(key, 8)
        B, S, D, F = (2, 128, 128, 256)
        G, Epg = (NUM_GROUPS, EXPERTS_PER_GROUP)
        E = G * Epg
        sc = lambda fan: 1.0 / np.sqrt(fan)
        return {'x': jax.random.normal(ks[0], (B, S, D), jnp.float32), 'in_proj_w': jax.random.normal(ks[1], (3 * D, D), jnp.float32) * sc(D), 'in_proj_b': jnp.zeros((3 * D,), jnp.float32), 'out_proj_w': jax.random.normal(ks[2], (D, D), jnp.float32) * sc(D), 'out_proj_b': jnp.zeros((D,), jnp.float32), 'ln1_g': jnp.ones((D,), jnp.float32), 'ln1_b': jnp.zeros((D,), jnp.float32), 'ln2_g': jnp.ones((D,), jnp.float32), 'ln2_b': jnp.zeros((D,), jnp.float32), 'w_group': jax.random.normal(ks[3], (D, G), jnp.float32) * sc(D), 'b_group': jnp.zeros((G,), jnp.float32), 'w_expert': jax.random.normal(ks[4], (G, D, Epg), jnp.float32) * sc(D), 'b_expert': jnp.zeros((G, Epg), jnp.float32), 'w1': jax.random.normal(ks[5], (E, D, F), jnp.float32) * sc(D), 'b1': jnp.zeros((E, F), jnp.float32), 'w2': jax.random.normal(ks[6], (E, F, D), jnp.float32) * sc(F), 'b2': jnp.zeros((E, D), jnp.float32)}
    _L1_ffn_all = _L1_ffn_setup()
    _L1_ffn_in = {k: v for k, v in _L1_ffn_all.items() if k in ('in_proj_w', 'in_proj_b', 'out_proj_w', 'out_proj_b', 'ln1_g', 'ln1_b', 'ln2_g', 'ln2_b', 'w_group', 'b_group', 'w_expert', 'b_expert', 'w1', 'b1', 'w2', 'b2')}
    del _L1_ffn_all

    def _L2_attn_setup():
        import jax, jax.numpy as jnp
        import numpy as np
        HIDDEN = 128
        N_HEADS = 16
        WINDOW = 64
        ROPE_BASE = 10000.0
        BATCH = 1
        SEQ = 1024

        def _rope(x, base=ROPE_BASE):
            B, S, D = x.shape
            half = D // 2
            inv_freq = 1.0 / base ** (jnp.arange(half, dtype=jnp.float32) / half)
            ang = jnp.arange(S, dtype=jnp.float32)[:, None] * inv_freq[None, :]
            cos, sin = (jnp.cos(ang), jnp.sin(ang))
            x1, x2 = (x[..., :half], x[..., half:])
            return jnp.concatenate([x1 * cos - x2 * sin, x1 * sin + x2 * cos], axis=-1)

        def _banded_attention(q, k, v, window):
            B, H, S, Dh = q.shape
            Wb = window
            nb = S // Wb
            scale = 1.0 / jnp.sqrt(jnp.asarray(Dh, q.dtype))
            qb = q.reshape(B, H, nb, Wb, Dh)
            kb = k.reshape(B, H, nb, Wb, Dh)
            vb = v.reshape(B, H, nb, Wb, Dh)
            zpad = [(0, 0), (0, 0), (1, 0), (0, 0), (0, 0)]
            k_prev = jnp.pad(kb, zpad)[:, :, :nb]
            v_prev = jnp.pad(vb, zpad)[:, :, :nb]
            k_ctx = jnp.concatenate([k_prev, kb], axis=3)
            v_ctx = jnp.concatenate([v_prev, vb], axis=3)
            scores = jnp.einsum('bhnqd,bhnkd->bhnqk', qb, k_ctx) * scale
            i = jnp.arange(Wb)[:, None]
            j = jnp.arange(2 * Wb)[None, :]
            band = (j >= i) & (j <= i + Wb)
            kv_glob = (jnp.arange(nb)[:, None, None] - 1) * Wb + j[None]
            mask = band[None] & (kv_glob >= 0)
            scores = jnp.where(mask[None, None], scores, jnp.finfo(scores.dtype).min)
            probs = jax.nn.softmax(scores, axis=-1)
            out = jnp.einsum('bhnqk,bhnkd->bhnqd', probs, v_ctx)
            return out.reshape(B, H, S, Dh)
        key = jax.random.key(seed)
        ks = jax.random.split(key, 9)
        s = 1.0 / np.sqrt(HIDDEN)
        return {'hidden_state': jax.random.normal(ks[0], (BATCH, SEQ, HIDDEN), jnp.float32), 'Wq': jax.random.uniform(ks[1], (HIDDEN, HIDDEN), jnp.float32, -s, s), 'bq': jnp.zeros((HIDDEN,), jnp.float32), 'Wk': jax.random.uniform(ks[2], (HIDDEN, HIDDEN), jnp.float32, -s, s), 'bk': jnp.zeros((HIDDEN,), jnp.float32), 'Wv': jax.random.uniform(ks[3], (HIDDEN, HIDDEN), jnp.float32, -s, s), 'bv': jnp.zeros((HIDDEN,), jnp.float32), 'Wo': jax.random.uniform(ks[4], (HIDDEN, HIDDEN), jnp.float32, -s, s), 'bo': jnp.zeros((HIDDEN,), jnp.float32)}
    _L2_attn_all = _L2_attn_setup()
    _L2_attn_in = {k: v for k, v in _L2_attn_all.items() if k in ('Wq', 'bq', 'Wk', 'bk', 'Wv', 'bv', 'Wo', 'bo')}
    del _L2_attn_all

    def _L2_xattn_setup():
        import jax, jax.numpy as jnp
        import numpy as np
        D_MODEL = 128
        N_HEADS = 16
        D_K = D_MODEL // N_HEADS
        key = jax.random.key(seed)
        ks = jax.random.split(key, 11)
        B, S = (4, 256)
        inp = {'q': jax.random.normal(ks[0], (B, S, D_MODEL), dtype=jnp.float32), 'k': jax.random.normal(ks[1], (B, S, D_MODEL), dtype=jnp.float32), 'v': jax.random.normal(ks[2], (B, S, D_MODEL), dtype=jnp.float32)}
        scale = 1.0 / np.sqrt(D_MODEL)
        for i, name in enumerate(['Wq', 'Wk', 'Wv', 'Wo']):
            inp[name] = jax.random.normal(ks[3 + i], (D_MODEL, D_MODEL), dtype=jnp.float32) * scale
            inp['b' + name[1:]] = jnp.zeros((D_MODEL,), dtype=jnp.float32)
        return inp
    _L2_xattn_all = _L2_xattn_setup()
    _L2_xattn_in = {k: v for k, v in _L2_xattn_all.items() if k in ('Wq', 'bq', 'Wk', 'bk', 'Wv', 'bv', 'Wo', 'bo')}
    del _L2_xattn_all

    def _L2_ffn_setup():
        import jax, jax.numpy as jnp
        import numpy as np
        MICRO_BATCHES = 2
        TOP_K = 2
        NUM_EXPERTS = 8
        B, S, D = (4, 512, 128)
        H = 4 * D
        key = jax.random.key(seed)
        ks = jax.random.split(key, 8)
        s = 0.02
        return {'x': jax.random.normal(ks[0], (B, S, D), jnp.float32), 'ln_scale': jnp.ones((D,), jnp.float32), 'ln_bias': jnp.zeros((D,), jnp.float32), 'attn_w': jax.random.normal(ks[1], (D, D), jnp.float32) * s, 'attn_b': jnp.zeros((D,), jnp.float32), 'gate_w': jax.random.normal(ks[2], (NUM_EXPERTS, D), jnp.float32) * s, 'w1': jax.random.normal(ks[3], (NUM_EXPERTS, D, H), jnp.float32) * s, 'b1': jnp.zeros((NUM_EXPERTS, H), jnp.float32), 'w2': jax.random.normal(ks[4], (NUM_EXPERTS, H, D), jnp.float32) * s, 'b2': jnp.zeros((NUM_EXPERTS, D), jnp.float32), 'next_w': jax.random.normal(ks[5], (D, D), jnp.float32) * s, 'next_b': jnp.zeros((D,), jnp.float32)}
    _L2_ffn_all = _L2_ffn_setup()
    _L2_ffn_in = {k: v for k, v in _L2_ffn_all.items() if k in ('ln_scale', 'ln_bias', 'attn_w', 'attn_b', 'gate_w', 'w1', 'b1', 'w2', 'b2', 'next_w', 'next_b')}
    del _L2_ffn_all

    def _L3_attn_setup():
        import jax, jax.numpy as jnp
        import numpy as np
        C_CONST = 8.0
        EPS = 1e-06
        K = 4

        def rmsnorm(x, w):
            var = jnp.mean(x * x, axis=-1, keepdims=True)
            return x * jax.lax.rsqrt(var + EPS) * w

        def causal_depthwise_conv(x, conv_w, conv_b):
            B, S, D = x.shape
            xp = jnp.pad(x, ((0, 0), (K - 1, 0), (0, 0)))
            out = conv_b
            for k in range(K):
                out = out + conv_w[k] * xp[:, k:k + S, :]
            return out

        def rg_lru(x, Wi, Wa, lam):
            r = jax.nn.sigmoid(jnp.einsum('bsd,de->bse', x, Wa))
            i = jax.nn.sigmoid(jnp.einsum('bsd,de->bse', x, Wi))
            log_a = -C_CONST * jax.nn.softplus(lam) * r
            a = jnp.exp(log_a)
            b = jnp.sqrt(jnp.maximum(1.0 - a * a, 1e-12)) * (i * x)

            def comb(e1, e2):
                a1, b1 = e1
                a2, b2 = e2
                return (a1 * a2, a2 * b1 + b2)
            _, h = jax.lax.associative_scan(comb, (a, b), axis=1)
            return h
        key = jax.random.key(seed)
        ks = jax.random.split(key, 16)
        B, S, D, H = (4, 256, 128, 512)
        s = 0.02
        return {'x': jax.random.normal(ks[0], (B, S, D), jnp.float32), 'norm1_w': jnp.ones((D,), jnp.float32), 'Wx': jax.random.normal(ks[1], (D, D), jnp.float32) * s, 'Wy': jax.random.normal(ks[2], (D, D), jnp.float32) * s, 'conv_w': jax.random.normal(ks[3], (K, D), jnp.float32) * s, 'conv_b': jnp.zeros((D,), jnp.float32), 'Wi': jax.random.normal(ks[4], (D, D), jnp.float32) * s, 'Wa': jax.random.normal(ks[5], (D, D), jnp.float32) * s, 'lam': jax.random.normal(ks[6], (D,), jnp.float32) * 0.5, 'Wo': jax.random.normal(ks[7], (D, D), jnp.float32) * s, 'norm2_w': jnp.ones((D,), jnp.float32), 'Wg': jax.random.normal(ks[8], (D, H), jnp.float32) * s, 'Wu': jax.random.normal(ks[9], (D, H), jnp.float32) * s, 'Wd': jax.random.normal(ks[10], (H, D), jnp.float32) * s}
    _L3_attn_all = _L3_attn_setup()
    _L3_attn_in = {k: v for k, v in _L3_attn_all.items() if k in ('norm1_w', 'Wx', 'Wy', 'conv_w', 'conv_b', 'Wi', 'Wa', 'lam', 'Wo', 'norm2_w', 'Wg', 'Wu', 'Wd')}
    del _L3_attn_all

    def _L3_xattn_setup():
        import jax, jax.numpy as jnp
        import numpy as np
        HEADS = 16
        WINDOW = 32
        D_MODEL = 128

        def _ln(x, g, b, eps=1e-05):
            m = jnp.mean(x, -1, keepdims=True)
            var = jnp.mean((x - m) ** 2, -1, keepdims=True)
            return (x - m) * jax.lax.rsqrt(var + eps) * g + b

        def _proj(x, g, b, W, bias):
            return _ln(x, g, b) @ W.T + bias

        def _bucket(x, pad_value):
            L = x.shape[-2]
            n = WINDOW * -(-L // WINDOW)
            pads = [(0, 0)] * x.ndim
            pads[-2] = (0, n - L)
            x = jnp.pad(x, pads, constant_values=pad_value)
            return x.reshape(*x.shape[:-2], n // WINDOW, WINDOW, x.shape[-1])

        def _unfold(x, pad_value):
            pads = [(0, 0)] * x.ndim
            pads[-3] = (1, 0)
            prev = jnp.pad(x, pads, constant_values=pad_value)[..., :-1, :, :]
            return jnp.concatenate([prev, x], axis=-2)

        def _rotary(x):
            S, d = (x.shape[-2], x.shape[-1])
            inv = 1.0 / 10000.0 ** (jnp.arange(0, d, 2, dtype=jnp.float32) / d)
            freqs = jnp.arange(S, dtype=jnp.float32)[:, None] * inv[None, :]
            freqs = jnp.repeat(freqs, 2, axis=-1)
            cos, sin = (jnp.cos(freqs).astype(x.dtype), jnp.sin(freqs).astype(x.dtype))
            xp = x.reshape(*x.shape[:-1], d // 2, 2)
            xr = jnp.stack([-xp[..., 1], xp[..., 0]], axis=-1).reshape(x.shape)
            return x * cos + xr * sin

        def _forward(q, k, v, cell, ln_q_w, ln_q_b, w_q, b_q, ln_k_w, ln_k_b, w_k, b_k, ln_v_w, ln_v_b, w_v, b_v, ln_o_w, ln_o_b, w_o, b_o):
            B, L, D = q.shape
            hd = D // HEADS

            def split_heads(x):
                return x.reshape(B, L, HEADS, hd).transpose(0, 2, 1, 3)
            qh = split_heads(_proj(q, ln_q_w, ln_q_b, w_q, b_q))
            kh = split_heads(_proj(k, ln_k_w, ln_k_b, w_k, b_k))
            vh = split_heads(_proj(v, ln_v_w, ln_v_b, w_v, b_v))
            bq = _bucket(qh, -1.0)
            bk = _unfold(_bucket(kh, -1.0), -1.0)
            bv = _unfold(_bucket(vh, -1.0), -1.0)
            nb = bq.shape[2]
            n = nb * WINDOW
            i = _bucket(jnp.arange(n, dtype=jnp.int32)[:, None], -1)
            j = jnp.swapaxes(_unfold(i, -1), -1, -2)
            mask = (i >= j) & (j != -1)
            req = _bucket(cell, -1)
            rek = jnp.swapaxes(_unfold(req, -1), -1, -2)
            mask = mask & (req == rek)
            bq = _rotary(bq)
            bk = _rotary(bk)
            p = jnp.einsum('bhnqd,bhnkd->bhnqk', bq, bk) / jnp.sqrt(jnp.asarray(hd, bq.dtype))
            p = jnp.where(mask, p, jnp.finfo(p.dtype).min)
            a = jax.nn.softmax(p, axis=-1)
            o = jnp.einsum('bhnqk,bhnkd->bhnqd', a, bv)
            o = o.reshape(B, HEADS, n, hd)[:, :, :L]
            o = o.transpose(0, 2, 1, 3).reshape(B, L, D)
            return _proj(o, ln_o_w, ln_o_b, w_o, b_o)
        key = jax.random.key(seed)
        ks = jax.random.split(key, 10)
        B, L, D = (2, 512, D_MODEL)
        inp = {'q': jax.random.normal(ks[0], (B, L, D), dtype=jnp.float32), 'k': jax.random.normal(ks[1], (B, L, D), dtype=jnp.float32), 'v': jax.random.normal(ks[2], (B, L, D), dtype=jnp.float32), 'cell': jnp.sort(jax.random.randint(ks[3], (B, 1, L, 1), 0, 64, dtype=jnp.int32), axis=2)}
        for idx, name in enumerate(['q', 'k', 'v', 'o']):
            inp[f'ln_{name}_w'] = jnp.ones((D,), jnp.float32)
            inp[f'ln_{name}_b'] = jnp.zeros((D,), jnp.float32)
            inp[f'w_{name}'] = jax.random.normal(ks[4 + idx], (D, D), dtype=jnp.float32) * 0.02
            inp[f'b_{name}'] = jnp.zeros((D,), jnp.float32)
        return inp
    _L3_xattn_all = _L3_xattn_setup()
    _L3_xattn_in = {k: v for k, v in _L3_xattn_all.items() if k in ('ln_q_w', 'ln_q_b', 'w_q', 'b_q', 'ln_k_w', 'ln_k_b', 'w_k', 'b_k', 'ln_v_w', 'ln_v_b', 'w_v', 'b_v', 'ln_o_w', 'ln_o_b', 'w_o', 'b_o')}
    del _L3_xattn_all

    def _L3_ffn_setup():
        import jax, jax.numpy as jnp
        import numpy as np
        DIM = 128

        def _reference_tuple_inner(x, W_r, W_k, W_v, mu_r, mu_k):
            B, T, C = x.shape
            x_prev = jnp.concatenate([jnp.zeros((B, 1, C), x.dtype), x[:, :-1, :]], axis=1)
            xr = mu_r * x + (1.0 - mu_r) * x_prev
            xk = mu_k * x + (1.0 - mu_k) * x_prev
            r = jax.nn.sigmoid(jnp.einsum('btc,dc->btd', xr, W_r))
            k = jnp.einsum('btc,dc->btd', xk, W_k)
            k_act = jnp.square(jax.nn.relu(k))
            out = r * jnp.einsum('btc,dc->btd', k_act, W_v)
            new_state = x[:, -1, :]
            return (out, new_state)
        key = jax.random.key(seed)
        ks = jax.random.split(key, 6)
        B, T, C = (8, 256, DIM)
        x = jax.random.normal(ks[0], (B, T, C), dtype=jnp.float32)
        s = 1.0 / np.sqrt(C)
        W_r = jax.random.uniform(ks[1], (C, C), jnp.float32, -s, s)
        W_k = jax.random.uniform(ks[2], (C, C), jnp.float32, -s, s)
        W_v = jax.random.uniform(ks[3], (C, C), jnp.float32, -s, s)
        mu_r = jax.random.uniform(ks[4], (C,), jnp.float32)
        mu_k = jax.random.uniform(ks[5], (C,), jnp.float32)
        return {'x': x, 'W_r': W_r, 'W_k': W_k, 'W_v': W_v, 'mu_r': mu_r, 'mu_k': mu_k}
    _L3_ffn_all = _L3_ffn_setup()
    _L3_ffn_in = {k: v for k, v in _L3_ffn_all.items() if k in ('W_r', 'W_k', 'W_v', 'mu_r', 'mu_k')}
    del _L3_ffn_all
    return {'x': x, 'ctx_1024': ctx_1024, 'itok_Bx1xSx1_0_63': itok_Bx1xSx1_0_63, 'mask_BxS2_ik0': mask_BxS2_ik0, 'L0_attn_wq': _L0_attn_in['wq'], 'L0_attn_wk': _L0_attn_in['wk'], 'L0_attn_wv': _L0_attn_in['wv'], 'L0_attn_wo': _L0_attn_in['wo'], 'L0_xattn_q_norm_w': _L0_xattn_in['q_norm_w'], 'L0_xattn_k_norm_w': _L0_xattn_in['k_norm_w'], 'L0_xattn_proj_w': _L0_xattn_in['proj_w'], 'L0_xattn_proj_b': _L0_xattn_in['proj_b'], 'L0_ffn_router_weight': _L0_ffn_in['router_weight'], 'L0_ffn_w1': _L0_ffn_in['w1'], 'L0_ffn_w2': _L0_ffn_in['w2'], 'L1_attn_Wq': _L1_attn_in['Wq'], 'L1_attn_Wk': _L1_attn_in['Wk'], 'L1_attn_Wv': _L1_attn_in['Wv'], 'L1_attn_Wo': _L1_attn_in['Wo'], 'L1_xattn_Wq': _L1_xattn_in['Wq'], 'L1_xattn_bq': _L1_xattn_in['bq'], 'L1_xattn_Wk': _L1_xattn_in['Wk'], 'L1_xattn_bk': _L1_xattn_in['bk'], 'L1_xattn_Wv': _L1_xattn_in['Wv'], 'L1_xattn_bv': _L1_xattn_in['bv'], 'L1_xattn_Wo': _L1_xattn_in['Wo'], 'L1_xattn_bo': _L1_xattn_in['bo'], 'L1_ffn_in_proj_w': _L1_ffn_in['in_proj_w'], 'L1_ffn_in_proj_b': _L1_ffn_in['in_proj_b'], 'L1_ffn_out_proj_w': _L1_ffn_in['out_proj_w'], 'L1_ffn_out_proj_b': _L1_ffn_in['out_proj_b'], 'L1_ffn_ln1_g': _L1_ffn_in['ln1_g'], 'L1_ffn_ln1_b': _L1_ffn_in['ln1_b'], 'L1_ffn_ln2_g': _L1_ffn_in['ln2_g'], 'L1_ffn_ln2_b': _L1_ffn_in['ln2_b'], 'L1_ffn_w_group': _L1_ffn_in['w_group'], 'L1_ffn_b_group': _L1_ffn_in['b_group'], 'L1_ffn_w_expert': _L1_ffn_in['w_expert'], 'L1_ffn_b_expert': _L1_ffn_in['b_expert'], 'L1_ffn_w1': _L1_ffn_in['w1'], 'L1_ffn_b1': _L1_ffn_in['b1'], 'L1_ffn_w2': _L1_ffn_in['w2'], 'L1_ffn_b2': _L1_ffn_in['b2'], 'L2_attn_Wq': _L2_attn_in['Wq'], 'L2_attn_bq': _L2_attn_in['bq'], 'L2_attn_Wk': _L2_attn_in['Wk'], 'L2_attn_bk': _L2_attn_in['bk'], 'L2_attn_Wv': _L2_attn_in['Wv'], 'L2_attn_bv': _L2_attn_in['bv'], 'L2_attn_Wo': _L2_attn_in['Wo'], 'L2_attn_bo': _L2_attn_in['bo'], 'L2_xattn_Wq': _L2_xattn_in['Wq'], 'L2_xattn_bq': _L2_xattn_in['bq'], 'L2_xattn_Wk': _L2_xattn_in['Wk'], 'L2_xattn_bk': _L2_xattn_in['bk'], 'L2_xattn_Wv': _L2_xattn_in['Wv'], 'L2_xattn_bv': _L2_xattn_in['bv'], 'L2_xattn_Wo': _L2_xattn_in['Wo'], 'L2_xattn_bo': _L2_xattn_in['bo'], 'L2_ffn_ln_scale': _L2_ffn_in['ln_scale'], 'L2_ffn_ln_bias': _L2_ffn_in['ln_bias'], 'L2_ffn_attn_w': _L2_ffn_in['attn_w'], 'L2_ffn_attn_b': _L2_ffn_in['attn_b'], 'L2_ffn_gate_w': _L2_ffn_in['gate_w'], 'L2_ffn_w1': _L2_ffn_in['w1'], 'L2_ffn_b1': _L2_ffn_in['b1'], 'L2_ffn_w2': _L2_ffn_in['w2'], 'L2_ffn_b2': _L2_ffn_in['b2'], 'L2_ffn_next_w': _L2_ffn_in['next_w'], 'L2_ffn_next_b': _L2_ffn_in['next_b'], 'L3_attn_norm1_w': _L3_attn_in['norm1_w'], 'L3_attn_Wx': _L3_attn_in['Wx'], 'L3_attn_Wy': _L3_attn_in['Wy'], 'L3_attn_conv_w': _L3_attn_in['conv_w'], 'L3_attn_conv_b': _L3_attn_in['conv_b'], 'L3_attn_Wi': _L3_attn_in['Wi'], 'L3_attn_Wa': _L3_attn_in['Wa'], 'L3_attn_lam': _L3_attn_in['lam'], 'L3_attn_Wo': _L3_attn_in['Wo'], 'L3_attn_norm2_w': _L3_attn_in['norm2_w'], 'L3_attn_Wg': _L3_attn_in['Wg'], 'L3_attn_Wu': _L3_attn_in['Wu'], 'L3_attn_Wd': _L3_attn_in['Wd'], 'L3_xattn_ln_q_w': _L3_xattn_in['ln_q_w'], 'L3_xattn_ln_q_b': _L3_xattn_in['ln_q_b'], 'L3_xattn_w_q': _L3_xattn_in['w_q'], 'L3_xattn_b_q': _L3_xattn_in['b_q'], 'L3_xattn_ln_k_w': _L3_xattn_in['ln_k_w'], 'L3_xattn_ln_k_b': _L3_xattn_in['ln_k_b'], 'L3_xattn_w_k': _L3_xattn_in['w_k'], 'L3_xattn_b_k': _L3_xattn_in['b_k'], 'L3_xattn_ln_v_w': _L3_xattn_in['ln_v_w'], 'L3_xattn_ln_v_b': _L3_xattn_in['ln_v_b'], 'L3_xattn_w_v': _L3_xattn_in['w_v'], 'L3_xattn_b_v': _L3_xattn_in['b_v'], 'L3_xattn_ln_o_w': _L3_xattn_in['ln_o_w'], 'L3_xattn_ln_o_b': _L3_xattn_in['ln_o_b'], 'L3_xattn_w_o': _L3_xattn_in['w_o'], 'L3_xattn_b_o': _L3_xattn_in['b_o'], 'L3_ffn_W_r': _L3_ffn_in['W_r'], 'L3_ffn_W_k': _L3_ffn_in['W_k'], 'L3_ffn_W_v': _L3_ffn_in['W_v'], 'L3_ffn_mu_r': _L3_ffn_in['mu_r'], 'L3_ffn_mu_k': _L3_ffn_in['mu_k']}

def reference(x, ctx_1024, itok_Bx1xSx1_0_63, mask_BxS2_ik0, L0_attn_wq, L0_attn_wk, L0_attn_wv, L0_attn_wo, L0_xattn_q_norm_w, L0_xattn_k_norm_w, L0_xattn_proj_w, L0_xattn_proj_b, L0_ffn_router_weight, L0_ffn_w1, L0_ffn_w2, L1_attn_Wq, L1_attn_Wk, L1_attn_Wv, L1_attn_Wo, L1_xattn_Wq, L1_xattn_bq, L1_xattn_Wk, L1_xattn_bk, L1_xattn_Wv, L1_xattn_bv, L1_xattn_Wo, L1_xattn_bo, L1_ffn_in_proj_w, L1_ffn_in_proj_b, L1_ffn_out_proj_w, L1_ffn_out_proj_b, L1_ffn_ln1_g, L1_ffn_ln1_b, L1_ffn_ln2_g, L1_ffn_ln2_b, L1_ffn_w_group, L1_ffn_b_group, L1_ffn_w_expert, L1_ffn_b_expert, L1_ffn_w1, L1_ffn_b1, L1_ffn_w2, L1_ffn_b2, L2_attn_Wq, L2_attn_bq, L2_attn_Wk, L2_attn_bk, L2_attn_Wv, L2_attn_bv, L2_attn_Wo, L2_attn_bo, L2_xattn_Wq, L2_xattn_bq, L2_xattn_Wk, L2_xattn_bk, L2_xattn_Wv, L2_xattn_bv, L2_xattn_Wo, L2_xattn_bo, L2_ffn_ln_scale, L2_ffn_ln_bias, L2_ffn_attn_w, L2_ffn_attn_b, L2_ffn_gate_w, L2_ffn_w1, L2_ffn_b1, L2_ffn_w2, L2_ffn_b2, L2_ffn_next_w, L2_ffn_next_b, L3_attn_norm1_w, L3_attn_Wx, L3_attn_Wy, L3_attn_conv_w, L3_attn_conv_b, L3_attn_Wi, L3_attn_Wa, L3_attn_lam, L3_attn_Wo, L3_attn_norm2_w, L3_attn_Wg, L3_attn_Wu, L3_attn_Wd, L3_xattn_ln_q_w, L3_xattn_ln_q_b, L3_xattn_w_q, L3_xattn_b_q, L3_xattn_ln_k_w, L3_xattn_ln_k_b, L3_xattn_w_k, L3_xattn_b_k, L3_xattn_ln_v_w, L3_xattn_ln_v_b, L3_xattn_w_v, L3_xattn_b_v, L3_xattn_ln_o_w, L3_xattn_ln_o_b, L3_xattn_w_o, L3_xattn_b_o, L3_ffn_W_r, L3_ffn_W_k, L3_ffn_W_v, L3_ffn_mu_r, L3_ffn_mu_k):
    import jax
    import jax.numpy as jnp

    def _L0_attn_ref(x, wq, wk, wv, wo):
        import jax, jax.numpy as jnp
        import numpy as np
        import math
        D_MODEL = 128
        NUM_HEADS = 16
        THETA = 10000.0

        def _rope(x, theta):
            n, d_k = (x.shape[-2], x.shape[-1])
            powers = jnp.arange(0, d_k, 2, dtype=jnp.float32) / d_k
            freqs = 1.0 / theta ** powers
            t = jnp.arange(n, dtype=jnp.float32)
            angles = jnp.outer(t, freqs)
            cos = jnp.cos(angles).astype(x.dtype)
            sin = jnp.sin(angles).astype(x.dtype)
            x_even = x[..., 0::2]
            x_odd = x[..., 1::2]
            rot_even = x_even * cos - x_odd * sin
            rot_odd = x_even * sin + x_odd * cos
            return jnp.stack([rot_even, rot_odd], axis=-1).reshape(x.shape)
        B, N, D = x.shape
        H = NUM_HEADS
        d_k = D // H

        def split_heads(t):
            return t.reshape(B, N, H, d_k).transpose(0, 2, 1, 3)
        Q = split_heads(x @ wq.T)
        K = split_heads(x @ wk.T)
        V = split_heads(x @ wv.T)
        Q = _rope(Q, THETA)
        K = _rope(K, THETA)
        scale = 1.0 / math.sqrt(d_k)
        scores = jnp.einsum('bhqd,bhkd->bhqk', Q, K) * scale
        causal_mask = jnp.triu(jnp.ones((N, N), dtype=bool), k=1)
        scores = jnp.where(causal_mask, -jnp.inf, scores)
        attn = jax.nn.softmax(scores, axis=-1)
        out = jnp.einsum('bhqk,bhkd->bhqd', attn, V)
        out = out.transpose(0, 2, 1, 3).reshape(B, N, D)
        return out @ wo.T

    def _L0_xattn_ref(q, k, v, q_norm_w, k_norm_w, proj_w, proj_b):
        import jax, jax.numpy as jnp
        import numpy as np
        B, S, E, H = (4, 256, 128, 16)
        HD = E // H
        EPS = 1.1920928955078125e-07

        def _rmsnorm(x, w):
            ms = jnp.mean(x * x, axis=-1, keepdims=True)
            return x * jax.lax.rsqrt(ms + EPS) * w

        def _rope(x, start_pos=0):
            seq_len = x.shape[-2]
            inv_freq = 1.0 / 10000.0 ** (jnp.arange(0, HD, 2, dtype=jnp.float32) / HD)
            t = jnp.arange(start_pos, start_pos + seq_len, dtype=jnp.float32)
            freqs = t[:, None] * inv_freq[None, :]
            cos = jnp.cos(freqs)[None, None]
            sin = jnp.sin(freqs)[None, None]
            x1 = x[..., 0::2]
            x2 = x[..., 1::2]
            o1 = x1 * cos - x2 * sin
            o2 = x1 * sin + x2 * cos
            return jnp.stack((o1, o2), axis=-1).reshape(x.shape)
        b, s, _ = q.shape
        scale = HD ** (-0.5)
        qh = q.reshape(b, s, H, HD).transpose(0, 2, 1, 3)
        kh = k.reshape(b, s, H, HD).transpose(0, 2, 1, 3)
        vh = v.reshape(b, s, H, HD).transpose(0, 2, 1, 3)
        qh = _rope(_rmsnorm(qh, q_norm_w))
        kh = _rope(_rmsnorm(kh, k_norm_w))
        scores = jnp.einsum('bhqd,bhkd->bhqk', qh, kh) * scale
        attn = jax.nn.softmax(scores, axis=-1)
        ctx = jnp.einsum('bhqk,bhkd->bhqd', attn, vh)
        ctx = ctx.transpose(0, 2, 1, 3).reshape(b, s, E)
        return ctx @ proj_w.T + proj_b

    def _L0_ffn_ref(hidden_states, router_weight, w1, w2):
        import jax, jax.numpy as jnp
        import numpy as np
        S, B, H = (256, 1, 128)
        E, K, F = (8, 2, 176)
        s, b, h = hidden_states.shape
        x = hidden_states.reshape(-1, h)
        logits = x @ router_weight
        probs = jax.nn.softmax(logits, axis=-1)
        _, topk_idx = jax.lax.top_k(probs, K)
        routing_map = jax.nn.one_hot(topk_idx, E, dtype=probs.dtype).sum(axis=1)
        local_probs = probs * routing_map
        y = jnp.einsum('th,ehf->tef', x, w1)
        y1, y2 = jnp.split(y, 2, axis=-1)
        g = jax.nn.silu(y1) * y2
        o = jnp.einsum('tef,efh->teh', g, w2)
        out = jnp.einsum('teh,te->th', o, local_probs)
        return out.reshape(s, b, h)

    def _L1_attn_ref(hidden_states, Wq, Wk, Wv, Wo):
        import jax, jax.numpy as jnp
        import numpy as np
        HIDDEN = 128
        NUM_HEADS = 16
        HEAD_DIM = 64
        NUM_KV_HEADS = 4

        def _xavier(key, out_dim, in_dim):
            limit = jnp.sqrt(6.0 / (in_dim + out_dim)).astype(jnp.float32)
            return jax.random.uniform(key, (out_dim, in_dim), jnp.float32, -limit, limit)
        B, S, _ = hidden_states.shape
        q = (hidden_states @ Wq.T).reshape(B, S, NUM_HEADS, HEAD_DIM).transpose(0, 2, 1, 3)
        k = (hidden_states @ Wk.T).reshape(B, S, NUM_KV_HEADS, HEAD_DIM).transpose(0, 2, 1, 3)
        v = (hidden_states @ Wv.T).reshape(B, S, NUM_KV_HEADS, HEAD_DIM).transpose(0, 2, 1, 3)
        n_rep = NUM_HEADS // NUM_KV_HEADS
        if n_rep > 1:
            k = jnp.repeat(k, n_rep, axis=1)
            v = jnp.repeat(v, n_rep, axis=1)
        scale = HEAD_DIM ** (-0.5)
        scores = jnp.einsum('bhqd,bhkd->bhqk', q, k) * scale
        causal = jnp.triu(jnp.full((S, S), -jnp.inf, dtype=scores.dtype), k=1)
        scores = scores + causal[None, None]
        probs = jax.nn.softmax(scores, axis=-1)
        out = jnp.einsum('bhqk,bhkd->bhqd', probs, v)
        out = out.transpose(0, 2, 1, 3).reshape(B, S, NUM_HEADS * HEAD_DIM)
        return out @ Wo.T

    def _L1_xattn_ref(query, key, value, mask, Wq, bq, Wk, bk, Wv, bv, Wo, bo):
        import jax, jax.numpy as jnp
        import numpy as np
        B, S, D, H = (2, 256, 128, 16)
        HD = D // H

        def _split_heads(x):
            Bb, Ss, Dd = x.shape
            return x.reshape(Bb, Ss, H, HD).transpose(0, 2, 1, 3)
        q = _split_heads(query @ Wq.T + bq)
        k = _split_heads(key @ Wk.T + bk)
        v = _split_heads(value @ Wv.T + bv)
        scores = jnp.einsum('bhqd,bhkd->bhqk', q, k) / np.sqrt(HD).astype(np.float32)
        scores = jnp.where(mask[:, None, None, :] == 0, jnp.float32(-1000000000.0), scores)
        attn = jax.nn.softmax(scores, axis=-1)
        x = jnp.einsum('bhqk,bhkd->bhqd', attn, v)
        x = x.transpose(0, 2, 1, 3).reshape(query.shape[0], query.shape[1], D)
        return x @ Wo.T + bo

    def _L1_ffn_ref(x, in_proj_w, in_proj_b, out_proj_w, out_proj_b, ln1_g, ln1_b, ln2_g, ln2_b, w_group, b_group, w_expert, b_expert, w1, b1, w2, b2):
        import jax, jax.numpy as jnp
        import numpy as np
        NHEAD = 16
        NUM_GROUPS = 4
        EXPERTS_PER_GROUP = 2
        LN_EPS = 1e-05

        def _layernorm(x, g, b):
            mu = jnp.mean(x, axis=-1, keepdims=True)
            var = jnp.mean(jnp.square(x - mu), axis=-1, keepdims=True)
            return (x - mu) * jax.lax.rsqrt(var + LN_EPS) * g + b

        def _mha(x, wi, bi, wo, bo):
            B, S, D = x.shape
            hd = D // NHEAD
            qkv = x @ wi.T + bi
            q, k, v = jnp.split(qkv, 3, axis=-1)

            def heads(t):
                return t.reshape(B, S, NHEAD, hd).transpose(0, 2, 1, 3)
            q, k, v = (heads(q), heads(k), heads(v))
            scores = jnp.einsum('bhqd,bhkd->bhqk', q, k) / jnp.sqrt(jnp.asarray(hd, x.dtype))
            attn = jax.nn.softmax(scores, axis=-1)
            o = jnp.einsum('bhqk,bhkd->bhqd', attn, v)
            o = o.transpose(0, 2, 1, 3).reshape(B, S, D)
            return o @ wo.T + bo

        def _hier_moe(x, w_group, b_group, w_expert, b_expert, w1, b1, w2, b2):
            B, S, D = x.shape
            xt = x.reshape(B * S, D)
            T = xt.shape[0]
            E = NUM_GROUPS * EXPERTS_PER_GROUP
            gp = jax.nn.softmax(xt @ w_group + b_group, axis=-1)
            g_idx = jnp.argmax(gp, axis=-1)
            g_prob = jnp.max(gp, axis=-1)
            elog = jnp.einsum('td,gde->tge', xt, w_expert) + b_expert
            ep = jax.nn.softmax(elog, axis=-1)
            ep_sel = jnp.take_along_axis(ep, g_idx[:, None, None], axis=1)[:, 0, :]
            e_idx_local = jnp.argmax(ep_sel, axis=-1)
            e_prob = jnp.max(ep_sel, axis=-1)
            flat_e = g_idx * EXPERTS_PER_GROUP + e_idx_local
            combine = jax.nn.one_hot(flat_e, E, dtype=xt.dtype) * (g_prob * e_prob)[:, None]
            h = jax.nn.relu(jnp.einsum('td,edf->etf', xt, w1) + b1[:, None, :])
            y = jnp.einsum('etf,efd->etd', h, w2) + b2[:, None, :]
            out = jnp.einsum('te,etd->td', combine, y)
            return out.reshape(B, S, D)
        attn_out = _mha(x, in_proj_w, in_proj_b, out_proj_w, out_proj_b)
        x = _layernorm(x + attn_out, ln1_g, ln1_b)
        moe_out = _hier_moe(x, w_group, b_group, w_expert, b_expert, w1, b1, w2, b2)
        x = _layernorm(x + moe_out, ln2_g, ln2_b)
        return x

    def _L2_attn_ref(hidden_state, Wq, bq, Wk, bk, Wv, bv, Wo, bo):
        import jax, jax.numpy as jnp
        import numpy as np
        HIDDEN = 128
        N_HEADS = 16
        WINDOW = 64
        ROPE_BASE = 10000.0
        BATCH = 1
        SEQ = 1024

        def _rope(x, base=ROPE_BASE):
            B, S, D = x.shape
            half = D // 2
            inv_freq = 1.0 / base ** (jnp.arange(half, dtype=jnp.float32) / half)
            ang = jnp.arange(S, dtype=jnp.float32)[:, None] * inv_freq[None, :]
            cos, sin = (jnp.cos(ang), jnp.sin(ang))
            x1, x2 = (x[..., :half], x[..., half:])
            return jnp.concatenate([x1 * cos - x2 * sin, x1 * sin + x2 * cos], axis=-1)

        def _banded_attention(q, k, v, window):
            B, H, S, Dh = q.shape
            Wb = window
            nb = S // Wb
            scale = 1.0 / jnp.sqrt(jnp.asarray(Dh, q.dtype))
            qb = q.reshape(B, H, nb, Wb, Dh)
            kb = k.reshape(B, H, nb, Wb, Dh)
            vb = v.reshape(B, H, nb, Wb, Dh)
            zpad = [(0, 0), (0, 0), (1, 0), (0, 0), (0, 0)]
            k_prev = jnp.pad(kb, zpad)[:, :, :nb]
            v_prev = jnp.pad(vb, zpad)[:, :, :nb]
            k_ctx = jnp.concatenate([k_prev, kb], axis=3)
            v_ctx = jnp.concatenate([v_prev, vb], axis=3)
            scores = jnp.einsum('bhnqd,bhnkd->bhnqk', qb, k_ctx) * scale
            i = jnp.arange(Wb)[:, None]
            j = jnp.arange(2 * Wb)[None, :]
            band = (j >= i) & (j <= i + Wb)
            kv_glob = (jnp.arange(nb)[:, None, None] - 1) * Wb + j[None]
            mask = band[None] & (kv_glob >= 0)
            scores = jnp.where(mask[None, None], scores, jnp.finfo(scores.dtype).min)
            probs = jax.nn.softmax(scores, axis=-1)
            out = jnp.einsum('bhnqk,bhnkd->bhnqd', probs, v_ctx)
            return out.reshape(B, H, S, Dh)
        B, S, D = hidden_state.shape
        Dh = D // N_HEADS
        q = hidden_state @ Wq.T + bq
        k = hidden_state @ Wk.T + bk
        v = hidden_state @ Wv.T + bv
        q = _rope(q)
        k = _rope(k)
        split = lambda x: x.reshape(B, S, N_HEADS, Dh).transpose(0, 2, 1, 3)
        out = _banded_attention(split(q), split(k), split(v), WINDOW)
        out = out.transpose(0, 2, 1, 3).reshape(B, S, D)
        return out @ Wo.T + bo

    def _L2_xattn_ref(q, k, v, Wq, bq, Wk, bk, Wv, bv, Wo, bo):
        import jax, jax.numpy as jnp
        import numpy as np
        D_MODEL = 128
        N_HEADS = 16
        D_K = D_MODEL // N_HEADS
        B, S, _ = q.shape

        def split_heads(x):
            return x.reshape(B, -1, N_HEADS, D_K).transpose(0, 2, 1, 3)
        qh = split_heads(q @ Wq.T + bq)
        kh = split_heads(k @ Wk.T + bk)
        vh = split_heads(v @ Wv.T + bv)
        scores = jnp.einsum('bhqd,bhkd->bhqk', qh, kh) / jnp.sqrt(jnp.float32(D_K))
        attn = jax.nn.softmax(scores, axis=-1)
        out = jnp.einsum('bhqk,bhkd->bhqd', attn, vh)
        out = out.transpose(0, 2, 1, 3).reshape(B, -1, D_MODEL)
        return out @ Wo.T + bo

    def _L2_ffn_ref(x, ln_scale, ln_bias, attn_w, attn_b, gate_w, w1, b1, w2, b2, next_w, next_b):
        import jax, jax.numpy as jnp
        import numpy as np
        MICRO_BATCHES = 2
        TOP_K = 2
        NUM_EXPERTS = 8
        B, S, D = (4, 512, 128)
        H = 4 * D
        b, s, d = x.shape
        flat = x.reshape(b * s, d)
        mu = jnp.mean(flat, axis=-1, keepdims=True)
        var = jnp.mean((flat - mu) ** 2, axis=-1, keepdims=True)
        xn = (flat - mu) * jax.lax.rsqrt(var + 1e-05) * ln_scale + ln_bias
        x_attn = xn @ attn_w.T + attn_b + flat
        logits = x_attn @ gate_w.T
        _vals, _idx = jax.lax.top_k(logits, TOP_K)
        e = w1.shape[0]
        n = b * s // (MICRO_BATCHES * e)
        xe = x_attn.reshape(MICRO_BATCHES, e, n, d)
        h = jax.nn.gelu(jnp.einsum('mend,edh->menh', xe, w1) + b1[None, :, None, :], approximate=False)
        eo = jnp.einsum('menh,ehd->mend', h, w2) + b2[None, :, None, :]
        eo = eo.reshape(b * s, d)
        out = jax.nn.gelu(eo @ next_w.T + next_b, approximate=False)
        return out.reshape(b, s, d)

    def _L3_attn_ref(x, norm1_w, Wx, Wy, conv_w, conv_b, Wi, Wa, lam, Wo, norm2_w, Wg, Wu, Wd):
        import jax, jax.numpy as jnp
        import numpy as np
        C_CONST = 8.0
        EPS = 1e-06
        K = 4

        def rmsnorm(x, w):
            var = jnp.mean(x * x, axis=-1, keepdims=True)
            return x * jax.lax.rsqrt(var + EPS) * w

        def causal_depthwise_conv(x, conv_w, conv_b):
            B, S, D = x.shape
            xp = jnp.pad(x, ((0, 0), (K - 1, 0), (0, 0)))
            out = conv_b
            for k in range(K):
                out = out + conv_w[k] * xp[:, k:k + S, :]
            return out

        def rg_lru(x, Wi, Wa, lam):
            r = jax.nn.sigmoid(jnp.einsum('bsd,de->bse', x, Wa))
            i = jax.nn.sigmoid(jnp.einsum('bsd,de->bse', x, Wi))
            log_a = -C_CONST * jax.nn.softplus(lam) * r
            a = jnp.exp(log_a)
            b = jnp.sqrt(jnp.maximum(1.0 - a * a, 1e-12)) * (i * x)

            def comb(e1, e2):
                a1, b1 = e1
                a2, b2 = e2
                return (a1 * a2, a2 * b1 + b2)
            _, h = jax.lax.associative_scan(comb, (a, b), axis=1)
            return h
        t = rmsnorm(x, norm1_w)
        xb = jnp.einsum('bsd,de->bse', t, Wx)
        xb = causal_depthwise_conv(xb, conv_w, conv_b)
        h = rg_lru(xb, Wi, Wa, lam)
        yb = jax.nn.gelu(jnp.einsum('bsd,de->bse', t, Wy))
        mix = jnp.einsum('bsd,de->bse', h * yb, Wo)
        h1 = x + mix
        u = rmsnorm(h1, norm2_w)
        ffn = jnp.einsum('bsh,hd->bsd', jax.nn.gelu(jnp.einsum('bsd,dh->bsh', u, Wg)) * jnp.einsum('bsd,dh->bsh', u, Wu), Wd)
        return h1 + ffn

    def _L3_xattn_ref(q, k, v, cell, ln_q_w, ln_q_b, w_q, b_q, ln_k_w, ln_k_b, w_k, b_k, ln_v_w, ln_v_b, w_v, b_v, ln_o_w, ln_o_b, w_o, b_o):
        import jax, jax.numpy as jnp
        import numpy as np
        HEADS = 16
        WINDOW = 32
        D_MODEL = 128

        def _ln(x, g, b, eps=1e-05):
            m = jnp.mean(x, -1, keepdims=True)
            var = jnp.mean((x - m) ** 2, -1, keepdims=True)
            return (x - m) * jax.lax.rsqrt(var + eps) * g + b

        def _proj(x, g, b, W, bias):
            return _ln(x, g, b) @ W.T + bias

        def _bucket(x, pad_value):
            L = x.shape[-2]
            n = WINDOW * -(-L // WINDOW)
            pads = [(0, 0)] * x.ndim
            pads[-2] = (0, n - L)
            x = jnp.pad(x, pads, constant_values=pad_value)
            return x.reshape(*x.shape[:-2], n // WINDOW, WINDOW, x.shape[-1])

        def _unfold(x, pad_value):
            pads = [(0, 0)] * x.ndim
            pads[-3] = (1, 0)
            prev = jnp.pad(x, pads, constant_values=pad_value)[..., :-1, :, :]
            return jnp.concatenate([prev, x], axis=-2)

        def _rotary(x):
            S, d = (x.shape[-2], x.shape[-1])
            inv = 1.0 / 10000.0 ** (jnp.arange(0, d, 2, dtype=jnp.float32) / d)
            freqs = jnp.arange(S, dtype=jnp.float32)[:, None] * inv[None, :]
            freqs = jnp.repeat(freqs, 2, axis=-1)
            cos, sin = (jnp.cos(freqs).astype(x.dtype), jnp.sin(freqs).astype(x.dtype))
            xp = x.reshape(*x.shape[:-1], d // 2, 2)
            xr = jnp.stack([-xp[..., 1], xp[..., 0]], axis=-1).reshape(x.shape)
            return x * cos + xr * sin

        def _forward(q, k, v, cell, ln_q_w, ln_q_b, w_q, b_q, ln_k_w, ln_k_b, w_k, b_k, ln_v_w, ln_v_b, w_v, b_v, ln_o_w, ln_o_b, w_o, b_o):
            B, L, D = q.shape
            hd = D // HEADS

            def split_heads(x):
                return x.reshape(B, L, HEADS, hd).transpose(0, 2, 1, 3)
            qh = split_heads(_proj(q, ln_q_w, ln_q_b, w_q, b_q))
            kh = split_heads(_proj(k, ln_k_w, ln_k_b, w_k, b_k))
            vh = split_heads(_proj(v, ln_v_w, ln_v_b, w_v, b_v))
            bq = _bucket(qh, -1.0)
            bk = _unfold(_bucket(kh, -1.0), -1.0)
            bv = _unfold(_bucket(vh, -1.0), -1.0)
            nb = bq.shape[2]
            n = nb * WINDOW
            i = _bucket(jnp.arange(n, dtype=jnp.int32)[:, None], -1)
            j = jnp.swapaxes(_unfold(i, -1), -1, -2)
            mask = (i >= j) & (j != -1)
            req = _bucket(cell, -1)
            rek = jnp.swapaxes(_unfold(req, -1), -1, -2)
            mask = mask & (req == rek)
            bq = _rotary(bq)
            bk = _rotary(bk)
            p = jnp.einsum('bhnqd,bhnkd->bhnqk', bq, bk) / jnp.sqrt(jnp.asarray(hd, bq.dtype))
            p = jnp.where(mask, p, jnp.finfo(p.dtype).min)
            a = jax.nn.softmax(p, axis=-1)
            o = jnp.einsum('bhnqk,bhnkd->bhnqd', a, bv)
            o = o.reshape(B, HEADS, n, hd)[:, :, :L]
            o = o.transpose(0, 2, 1, 3).reshape(B, L, D)
            return _proj(o, ln_o_w, ln_o_b, w_o, b_o)
        return _forward(q, k, v, cell, ln_q_w, ln_q_b, w_q, b_q, ln_k_w, ln_k_b, w_k, b_k, ln_v_w, ln_v_b, w_v, b_v, ln_o_w, ln_o_b, w_o, b_o)

    def _L3_ffn_ref(x, W_r, W_k, W_v, mu_r, mu_k):
        import jax, jax.numpy as jnp
        import numpy as np
        DIM = 128

        def _reference_tuple_inner(x, W_r, W_k, W_v, mu_r, mu_k):
            B, T, C = x.shape
            x_prev = jnp.concatenate([jnp.zeros((B, 1, C), x.dtype), x[:, :-1, :]], axis=1)
            xr = mu_r * x + (1.0 - mu_r) * x_prev
            xk = mu_k * x + (1.0 - mu_k) * x_prev
            r = jax.nn.sigmoid(jnp.einsum('btc,dc->btd', xr, W_r))
            k = jnp.einsum('btc,dc->btd', xk, W_k)
            k_act = jnp.square(jax.nn.relu(k))
            out = r * jnp.einsum('btc,dc->btd', k_act, W_v)
            new_state = x[:, -1, :]
            return (out, new_state)
        return _reference_tuple_inner(x, W_r, W_k, W_v, mu_r, mu_k)[0]
    x = _layernorm(x + _L0_attn_ref(x, L0_attn_wq, L0_attn_wk, L0_attn_wv, L0_attn_wo), axis=-1)
    x = _layernorm(x + _L0_xattn_ref(x, ctx_1024, ctx_1024, L0_xattn_q_norm_w, L0_xattn_k_norm_w, L0_xattn_proj_w, L0_xattn_proj_b), axis=-1)
    x = _layernorm(x + _L0_ffn_ref(x, L0_ffn_router_weight, L0_ffn_w1, L0_ffn_w2), axis=-1)
    x = _layernorm(x + _L1_attn_ref(x, L1_attn_Wq, L1_attn_Wk, L1_attn_Wv, L1_attn_Wo), axis=-1)
    x = _layernorm(x + _L1_xattn_ref(x, ctx_1024, ctx_1024, mask_BxS2_ik0, L1_xattn_Wq, L1_xattn_bq, L1_xattn_Wk, L1_xattn_bk, L1_xattn_Wv, L1_xattn_bv, L1_xattn_Wo, L1_xattn_bo), axis=-1)
    x = _layernorm(x + _L1_ffn_ref(x, L1_ffn_in_proj_w, L1_ffn_in_proj_b, L1_ffn_out_proj_w, L1_ffn_out_proj_b, L1_ffn_ln1_g, L1_ffn_ln1_b, L1_ffn_ln2_g, L1_ffn_ln2_b, L1_ffn_w_group, L1_ffn_b_group, L1_ffn_w_expert, L1_ffn_b_expert, L1_ffn_w1, L1_ffn_b1, L1_ffn_w2, L1_ffn_b2), axis=-1)
    x = _layernorm(x + _L2_attn_ref(x, L2_attn_Wq, L2_attn_bq, L2_attn_Wk, L2_attn_bk, L2_attn_Wv, L2_attn_bv, L2_attn_Wo, L2_attn_bo), axis=-1)
    x = _layernorm(x + _L2_xattn_ref(x, ctx_1024, ctx_1024, L2_xattn_Wq, L2_xattn_bq, L2_xattn_Wk, L2_xattn_bk, L2_xattn_Wv, L2_xattn_bv, L2_xattn_Wo, L2_xattn_bo), axis=-1)
    x = _layernorm(x + _L2_ffn_ref(x, L2_ffn_ln_scale, L2_ffn_ln_bias, L2_ffn_attn_w, L2_ffn_attn_b, L2_ffn_gate_w, L2_ffn_w1, L2_ffn_b1, L2_ffn_w2, L2_ffn_b2, L2_ffn_next_w, L2_ffn_next_b), axis=-1)
    x = _layernorm(x + _L3_attn_ref(x, L3_attn_norm1_w, L3_attn_Wx, L3_attn_Wy, L3_attn_conv_w, L3_attn_conv_b, L3_attn_Wi, L3_attn_Wa, L3_attn_lam, L3_attn_Wo, L3_attn_norm2_w, L3_attn_Wg, L3_attn_Wu, L3_attn_Wd), axis=-1)
    x = _layernorm(x + _L3_xattn_ref(x, ctx_1024, ctx_1024, itok_Bx1xSx1_0_63, L3_xattn_ln_q_w, L3_xattn_ln_q_b, L3_xattn_w_q, L3_xattn_b_q, L3_xattn_ln_k_w, L3_xattn_ln_k_b, L3_xattn_w_k, L3_xattn_b_k, L3_xattn_ln_v_w, L3_xattn_ln_v_b, L3_xattn_w_v, L3_xattn_b_v, L3_xattn_ln_o_w, L3_xattn_ln_o_b, L3_xattn_w_o, L3_xattn_b_o), axis=-1)
    x = _layernorm(x + _L3_ffn_ref(x, L3_ffn_W_r, L3_ffn_W_k, L3_ffn_W_v, L3_ffn_mu_r, L3_ffn_mu_k), axis=-1)
    return x

_drawn_inputs = setup_inputs


def setup_inputs(seed=0):
    import zlib

    import numpy as np

    out = dict(_drawn_inputs(seed))
    spreads = {'L0_xattn_q_norm_w': (1.0, 0.6),
     'L0_xattn_k_norm_w': (1.0, 0.6),
     'L0_xattn_proj_b': (0.0, 0.1),
     'L1_xattn_bq': (0.0, 0.314),
     'L1_xattn_bk': (0.0, 2.0),
     'L1_xattn_bv': (0.0, 0.1),
     'L1_xattn_bo': (0.0, 0.1),
     'L1_ffn_in_proj_b': (0.0, 0.1),
     'L1_ffn_out_proj_b': (0.0, 0.1),
     'L1_ffn_ln1_g': (1.0, 0.2),
     'L1_ffn_ln1_b': (0.0, 0.1),
     'L1_ffn_ln2_g': (1.0, 0.2),
     'L1_ffn_ln2_b': (0.0, 0.1),
     'L1_ffn_b_group': (0.0, 0.1),
     'L1_ffn_b_expert': (0.0, 0.627),
     'L1_ffn_b1': (0.0, 0.681),
     'L1_ffn_b2': (0.0, 0.461),
     'L2_attn_bq': (0.0, 0.8),
     'L2_attn_bk': (0.0, 0.8),
     'L2_attn_bv': (0.0, 0.1),
     'L2_attn_bo': (0.0, 0.1),
     'L2_xattn_bq': (0.0, 0.414),
     'L2_xattn_bk': (0.0, 2.0),
     'L2_xattn_bv': (0.0, 0.1),
     'L2_xattn_bo': (0.0, 0.1),
     'L2_ffn_ln_scale': (1.0, 0.6),
     'L2_ffn_ln_bias': (0.0, 0.8),
     'L2_ffn_attn_b': (0.0, 0.8),
     'L2_ffn_b1': (0.0, 0.8),
     'L2_ffn_b2': (0.0, 0.714),
     'L2_ffn_next_b': (0.0, 0.529),
     'L3_attn_norm1_w': (1.0, 0.6),
     'L3_attn_conv_b': (0.0, 0.8),
     'L3_attn_norm2_w': (1.0, 0.6),
     'L3_xattn_ln_q_w': (1.0, 0.6),
     'L3_xattn_ln_q_b': (0.0, 0.8),
     'L3_xattn_b_q': (0.0, 2.0),
     'L3_xattn_ln_k_w': (1.0, 0.6),
     'L3_xattn_ln_k_b': (0.0, 0.8),
     'L3_xattn_b_k': (0.0, 2.0),
     'L3_xattn_ln_v_w': (1.0, 0.2),
     'L3_xattn_ln_v_b': (0.0, 0.43),
     'L3_xattn_b_v': (0.0, 0.1),
     'L3_xattn_ln_o_w': (1.0, 0.2),
     'L3_xattn_ln_o_b': (0.0, 0.414),
     'L3_xattn_b_o': (0.0, 0.1)}
    factors = {'L0_ffn_router_weight': 8.0,
     'L0_ffn_w1': 8.0,
     'L0_ffn_w2': 8.0,
     'L2_attn_Wq': 5.132,
     'L2_attn_Wk': 5.116,
     'L2_ffn_attn_w': 8.0,
     'L2_ffn_w1': 8.0,
     'L2_ffn_w2': 8.0,
     'L2_ffn_next_w': 4.416,
     'L3_attn_Wx': 8.0,
     'L3_attn_Wy': 8.0,
     'L3_attn_conv_w': 8.0,
     'L3_attn_Wi': 8.0,
     'L3_attn_Wa': 8.0,
     'L3_attn_lam': 8.0,
     'L3_attn_Wo': 8.0,
     'L3_attn_Wg': 8.0,
     'L3_attn_Wu': 8.0,
     'L3_attn_Wd': 8.0,
     'L3_xattn_w_q': 8.0,
     'L3_xattn_w_k': 8.0,
     'L3_ffn_mu_r': 7.919}
    for name, (base, spread) in spreads.items():
        noise = np.random.default_rng([zlib.crc32(name.encode()), seed]).standard_normal(out[name].shape)
        drawn = base * np.exp(spread * noise) if base else spread * noise
        out[name] = jnp.asarray(drawn.astype(out[name].dtype))
    for name, factor in factors.items():
        out[name] = (out[name] * factor).astype(out[name].dtype)
    return out
```

```python
from contextlib import ExitStack

import numpy as np

import concourse.bass as bass
from concourse import mybir

NB, SEQ, D = 128, 64, 128
HEADS, HD = 16, 8
P = 128
TOK = NB * SEQ
TILES = TOK // P
PAIRS = TILES // 2
BATCH = 512
NBATCH = TOK // BATCH
KVH, GD = 4, 64
HP = HEADS // 2
VW = 2 * HD + 2
LN_EPS = 1e-5
RMS_EPS = 1.1920928955078125e-07
NEG = -1e30

F32, BF16, I32 = mybir.dt.float32, mybir.dt.bfloat16, mybir.dt.int32
ALU, ACT, AX = mybir.AluOpType, mybir.ActivationFunctionType, mybir.AxisListType.X

SQ = ["I", "SWAP", "L0q", "L0qs", "L0k", "L0ks", "L0v", "L0o", "L0xo",
      "L1xq", "L1xk", "L1xv", "L1xo", "L1fq", "L1fk", "L1fv", "L1fo",
      "L2q", "L2qs", "L2k", "L2ks", "L2v", "L2o", "L2xq", "L2xk", "L2xv", "L2xo",
      "L3xq", "L3xqs", "L3xk", "L3xks", "L3xv", "L3xo",
      "L2fa", "L2fn", "L3Wx", "L3Wy", "L3Wi", "L3Wa", "L3Wo", "L3fr", "L3fk", "L3fv"]
COL = ["qn", "qns", "kn", "kns", "L1bq", "L1bk", "L1bv", "L1fbq", "L1fbk", "L1fbv",
       "L2bq", "L2bqs", "L2bk", "L2bks", "L2bv", "L2xbq", "L2xbk", "L2xbv",
       "L3bq", "L3bqs", "L3bk", "L3bks", "L3gq", "L3aq", "L3gk", "L3ak", "L3gv", "L3av", "L3go", "L3ao", "L3bv",
       "L2fab", "L2fnb", "n1", "n2", "cb", "lam", "c0", "c1", "c2", "c3", "mur", "muk", "L2g", "L2b"]
ROW = ["L0xb", "L1xb", "L1fb", "L2b", "L2xb", "L3b", "g1", "b1", "g2", "b2"]


class Signal:

    def __init__(self, ctx, nc, name):
        self.sem, self.base = ctx.enter_context(nc.semaphore(name)), 0


class Signals(dict):

    def __init__(self, ctx, nc):
        super().__init__()
        self.ctx, self.nc = ctx, nc

    def __missing__(self, name):
        self[name] = Signal(self.ctx, self.nc, name)
        return self[name]

    def advance(self, given, when=True):
        for name, n in given.items():
            if when:
                self[name].base += n


def after(count):
    return not isinstance(count, int) or count > 0


def pace(eng, S):
    eng.sem_inc(S["paced"].sem, 1)


class Memory(ExitStack):

    def __init__(self, nc, layer):
        super().__init__()
        self.nc, self.layer = nc, layer

    def sb(self, name, shape, dt=F32):
        return self.enter_context(self.nc.sbuf_tensor(f"{self.layer}_{name}", shape, dt))

    def pb(self, name, shape, dt=F32):
        return self.enter_context(self.nc.psum_tensor(f"{self.layer}_{name}", shape, dt))


class At:

    def __init__(self, i, c, n=TILES):
        self.i, self.c, self.n = i, c, n
        self.ok = i is not None or 0 <= c < n
        self.t = c if i is None else i * 4 + c
        self.par = c % 2
        self.u = (c // 2) % 2

    def __add__(self, k):
        return At(self.i, self.c + k, self.n)

    def __sub__(self, k):
        return self + (-k)

    @property
    def p(self):
        return self.c // 2 if self.i is None else self.i * 2 + self.c // 2


def pipeline(eng, slot, ahead=3):
    first, turns = 8, 13
    for c in range(-ahead, first):
        slot(At(None, c))
    with eng.Fori(0, turns) as i:
        for c in range(4):
            slot(At(i, first + c))
    for c in range(first + 4 * turns, TILES + 6):
        slot(At(None, c))


def build(nc, io, out):
    ctx = ExitStack()
    with ctx:
        S = Signals(ctx, nc)

        def sb(name, shape, dt=F32):
            return ctx.enter_context(nc.sbuf_tensor(name, shape, dt))

        def pb(name, shape, dt=F32):
            return ctx.enter_context(nc.psum_tensor(name, shape, dt))

        X = sb("X", [P, TILES, D])
        W = sb("W", [P, len(SQ), D])
        col = sb("col", [P, len(COL)])
        row = sb("row", [P, len(ROW), D])
        rope = sb("rope", [P, 6, SEQ])
        idb = sb("idb", [P, P], BF16)
        causal = sb("causal", [P, SEQ], BF16)
        maskk = sb("maskk", [P, TILES, SEQ], BF16)
        stat = sb("stat", [P, TILES, HEADS])
        stat2 = sb("stat2", [P, TILES, HEADS])
        wp = sb("wp", [P, 6, D])
        colx = sb("colx", [P, 8])
        rowx = sb("rowx", [P, 2, D])
        colb = sb("colb", [P, 2, D])
        half = sb("half", [P, 4])
        zeros = sb("zeros", [P, 1])
        eps = sb("eps", [P, 4])
        cellq = sb("cellq", [P, TILES], I32)
        ident = W[:, SQ.index("I"), :]
        Wm = lambda n: W[:, SQ.index(n), :]
        C = lambda n: col[:, COL.index(n):COL.index(n) + 1]
        R = lambda n: row[:, ROW.index(n), :]

        mem0 = Memory(nc, "setup")
        causal32 = mem0.sb("causal32", [P, SEQ])
        with nc.Block() as block:
            @block.sync
            def _(sp):
                for dst, src in ((W[:, :, :], io["W"]), (X[:, :, :], io["x"].rearrange("(t p) d -> p t d", p=P)),
                                 (col[:, :], io["col"]), (rope[:, :, :], io["rope"])):
                    sp.dma_start(dst, src).then_inc(S["loaded"].sem, 16)
                sp.dma_start(row[:, :, :], io["row"].partition_broadcast(P)).then_inc(S["loaded"].sem, 16)
                sp.dma_start(causal32[:, :], io["causal"]).then_inc(S["loaded"].sem, 16)
                sp.wait_ge(S["loaded"].sem, 6 * 16)

            @block.vector
            def _(v):
                nc.vector.memset(half[:, :], -0.5)
                nc.vector.memset(zeros[:, :], 0.0)
                nc.vector.memset(eps[:, :], LN_EPS)
                v.wait_ge(S["loaded"].sem, S["loaded"].base + 6 * 16)
                nc.vector.tensor_copy(idb[:, :], ident)
                nc.vector.tensor_copy(causal[:, :], causal32[:, :])
        mem0.close()

        def attention(L, q, k, v, o, qs=None, ks=None, gq=None, gqs=None, gk=None, gks=None, bq=None, bqs=None, bk=None, bks=None, bv=None, bo=None,
                      cq=0, ck=0, cross=False, norm=None, mask=None, keymask=False, ln_o=False, affine=None):
            mem = Memory(nc, L)
            XS = mem.sb("XS", [P, 2, 2, D])
            CS = mem.sb("CS", [P, 2, 2, D])
            XR = mem.sb("XR", [P, 2, 2, D])
            XT = mem.sb("XT", [P, 2, 2 * P])
            CT = mem.sb("CT", [P, 2, 2 * P])
            CR = mem.sb("CR", [P, 2, 2 * P])
            CN = mem.sb("CN", [P, 2, 2, D])
            RA = mem.sb("RA", [P, 2, 2, 2 * P])
            MI = mem.sb("MI", [P, 2, 2 * P], I32)
            MF = mem.sb("MF", [P, 2, 2 * P])
            QT = mem.sb("QT", [P, 2, 2 * P])
            KT = mem.sb("KT", [P, 2, 2 * P])
            KB = mem.sb("KB", [P, 2, HEADS, 4, SEQ])
            VB = mem.sb("VB", [P, 2, 4, HP, VW])
            PR = mem.sb("PR", [P, 2, HEADS, SEQ])
            PT = mem.sb("PT", [P, 2, HP, P])
            mx = mem.sb("mx", [P, 2, HEADS])
            rden = mem.sb("rden", [P, 2, HP, 2])
            ON = mem.sb("ON", [P, 2, D])
            OT = mem.sb("OT", [P, 2, P])
            RB = mem.sb("RB", [P, 2, 2, D])
            st6 = mem.sb("st6", [P, 2, 6])
            mv = mem.sb("mv", [P, 2, 2, 2])
            rs = mem.sb("rs", [P, 2, 2, 2])
            st6o = mem.sb("st6o", [P, 2, 6])
            mvo = mem.sb("mvo", [P, 2, 2])
            rso = mem.sb("rso", [P, 2, 2])
            OL = mem.sb("OL", [P, 2, D])

            psS = mem.pb("psS", [P, 2, HEADS, SEQ])
            psP = mem.pb("psP", [P, 2, 4, P])
            psF = mem.pb("psF", [P, 512])
            psB = mem.pb("psB", [P, 512])
            psO, psOT, psJ = psB[:, 0:HP * VW], psB[:, 256:384], psB[:, 384:512]
            scale = HD ** -0.5
            steps = ["tx"] + (["tc"] if cross and norm else []) + ["k", "q", "v"]
            NS = len(steps)
            NF = NS + 1
            e = 1 if ln_o else 0
            sidx = {s: n for n, s in enumerate(steps)}
            zero = zeros[:, 0:1]
            raw = cross and norm != "ln"

            def front_done(eng, p, step):
                eng.wait_ge(S["front_out"].sem, S["front_out"].base + p * NF + (NF if step == "v" else sidx[step] + 1))

            def wait_front(eng, p, step):
                eng.wait_ge(S["front"].sem, S["front"].base + p * NS + sidx[step] + 1)


            with nc.Block() as block:
                @block.vector
                def _(dv):
                    nc.vector.memset(VB[:, :, :, :, :], 0.0).then_inc(S["zeroed"].sem, 1)
                    nc.vector.memset(KB[:, 0, :, :, :], 0.0)
                    dv.wait_ge(S["zeroed"].sem, S["zeroed"].base + 1)
                    nc.vector.memset(VB[0:64, :, :, :, 2 * HD:2 * HD + 1], 1.0)
                    nc.vector.memset(VB[64:128, :, :, :, 2 * HD + 1:VW], 1.0)

                @block.gpsimd
                def _(g):
                    nc.gpsimd.memset(KB[:, 1, :, :, :], 0.0)
            S.advance(dict(zeroed=1))
            src = (CR if norm is None else CT) if cross else XT
            srcv = (CR if raw else CT) if cross else XT
            bias_row = rowx[:, 0, :] if bv is not None or ln_o else bo
            if bv is not None and not ln_o:
                with nc.Block() as block:
                    @block.vector
                    def _(dv):
                        nc.vector.tensor_scalar(colb[:, 0, :], ident, 0.0, bv, ALU.mult, ALU.add).then_inc(S["prep"].sem, 1)
                        dv.wait_ge(S["prep_pe"].sem, S["prep_pe"].base + 1)
                        nc.vector.tensor_tensor(rowx[:, 0, :], psJ, bo, ALU.add)

                    @block.tensor
                    def _(pe):
                        pe.wait_ge(S["prep"].sem, S["prep"].base + 1)
                        nc.tensor.matmul(psJ, colb[:, 0, :], o, start=True, stop=True).then_inc(S["prep_pe"].sem, 1)
                S["prep"].base += 1
                S["prep_pe"].base += 1

            def parity_wait(eng, name, K, each):
                if K.i is None and K.c < 0:
                    return
                n = K.c // 4 if K.i is None else K.i + K.c // 4
                eng.wait_ge(S[f"{name}{K.u}"].sem, S[f"{name}{K.u}"].base + (n + 1) * each)

            def parity_sem(name, K):
                return S[f"{name}{K.u}"].sem

            def xrow(t):
                return X[:, t, :] if isinstance(t, int) else X[:, bass.ds(t, 1), :].rearrange("p a d -> p (a d)")

            heads = lambda ap: ap.rearrange("p t (h d) -> p (t h) d", d=HD)

            with nc.Block() as block:
                @block.sync
                def _(sp):
                    def slot(T):
                        N = T + 4
                        if T.par == 0 and N.ok:
                            if raw:
                                if after((N.p - 2) * NS + NS):
                                    sp.wait_ge(S["front"].sem, S["front"].base + (N.p - 2) * NS + NS)
                                sp.dma_start(CR[:, N.u, :], io["ctxT"][:, bass.ds(N.p * 256, 256)]).then_inc(parity_sem("ctx_in", N), 16)
                            if cross and norm:
                                if after(N.p - 1):
                                    sp.wait_ge(S["ctx_normed"].sem, S["ctx_normed"].base + N.p - 1)
                                sp.dma_start(CS[:, N.u, :, :], io["ctx"][bass.ds(N.p * 256, 256), :].rearrange("(t p) d -> p t d", p=P)).then_inc(parity_sem("rows_in", N), 16)
                            if keymask:
                                if after(N.p - 1):
                                    sp.wait_ge(S["mask_used"].sem, S["mask_used"].base + N.p - 1)
                                sp.dma_start(MI[:, N.u, :], io["mask"][bass.ds(N.p * 256, 256)].partition_broadcast(P)).then_inc(parity_sem("mask_in", N), 16)
                        K = T + 2
                        if T.par == 0 and K.ok:
                            if ks is not None:
                                sp.wait_ge(S["k_roped"].sem, S["k_roped"].base + K.p + 1)
                            else:
                                front_done(sp, K.p, "k")
                            if after(2 * K.p - 2):
                                sp.wait_ge(S["scores"].sem, S["scores"].base + 2 * K.p - 2)
                            for h in range(HEADS):
                                sp.dma_start(KB[HD * h:HD * h + HD, K.u, h, :, :].rearrange("p s k -> p (s k)"), KT[HD * h:HD * h + HD, K.u, :]).then_inc(parity_sem("keys_in", K), 16)
                    pipeline(sp, slot, 4)

                @block.gpsimd
                def _(g):
                    def normalise(N, dst, src_, st, between, done):
                        if norm == "rms":
                            r = st[:, bass.ds(N.t, 2), :].rearrange("p t h -> p (t h)").unsqueeze(2).to_broadcast([P, 2 * HEADS, HD])
                            nc.gpsimd.tensor_tensor(heads(dst), heads(src_), r, ALU.mult).then_inc(done.sem, 1)
                        else:
                            nc.gpsimd.tensor_tensor(dst, src_, st[:, bass.ds(N.t, 2), 0:1].to_broadcast([P, 2, D]), ALU.subtract).then_inc(between.sem, 1)
                            g.wait_ge(between.sem, between.base + N.p + 1)
                            nc.gpsimd.tensor_tensor(dst, dst, st[:, bass.ds(N.t, 2), 1:2].to_broadcast([P, 2, D]), ALU.mult).then_inc(done.sem, 1)

                    def slot(T):
                        N = T + 2
                        if T.par == 0 and N.ok:
                            if ks is not None:
                                front_done(g, N.p, "k")
                                parity_wait(g, "keys_in", N - 4, 256)
                                nc.gpsimd.tensor_tensor(KT[:, N.u], RA[:, 0, 0], RA[:, 0, 1], ALU.add).then_inc(S["k_roped"].sem, 1)
                        K = T + 1
                        if T.par == 1 and K.ok and qs is not None:
                            front_done(g, K.p, "q")
                            if after(2 * K.p - 2):
                                g.wait_ge(S["scores"].sem, S["scores"].base + 2 * K.p - 2)
                            nc.gpsimd.tensor_tensor(QT[:, K.u], RA[:, 1, 0], RA[:, 1, 1], ALU.add).then_inc(S["q_roped"].sem, 1)
                        N = T + 3
                        if T.par == 1 and N.ok:
                            if after((N.p - 2) * NS + 1):
                                g.wait_ge(S["front"].sem, S["front"].base + (N.p - 2) * NS + 1)
                            xin = X[:, bass.ds(N.t, 2), :]
                            if norm:
                                normalise(N, XS[:, N.u], xin, stat, S["x_centred"], S["xs"])
                            else:
                                nc.gpsimd.tensor_copy(XS[:, N.u], xin).then_inc(S["xs"].sem, 1)
                            if cross and norm:
                                parity_wait(g, "rows_in", N, 16)
                                if after((N.p - 2) * NS + 2):
                                    g.wait_ge(S["front"].sem, S["front"].base + (N.p - 2) * NS + 2)
                                normalise(N, CN[:, N.u], CS[:, N.u], stat2, S["ctx_centred"], S["ctx_normed"])
                        A = T - 2
                        if A.par == 0 and A.ok and bias_row is not None:
                            if after(2 * (A.p - 1)):
                                g.wait_ge(S["res"].sem, S["res"].base + 2 * (A.p - 1))
                            nc.gpsimd.tensor_tensor(XR[:, A.u], X[:, bass.ds(A.t, 2), :], bias_row.unsqueeze(1).to_broadcast([P, 2, D]), ALU.add).then_inc(S["xres"].sem, 1)
                        A = T - 3
                        if ln_o and A.ok:
                            g.wait_ge(S["o_stats"].sem, S["o_stats"].base + A.t + 1)
                            if after(A.t - 1):
                                g.wait_ge(S["o_ready"].sem, S["o_ready"].base + A.t - 1)
                            nc.gpsimd.tensor_tensor(rso[:, A.par, 0:1], mvo[:, A.par, 1:2], eps[:, 0:1], ALU.add).then_inc(S["o_eps"].sem, 1)
                            g.wait_ge(S["o_eps"].sem, S["o_eps"].base + A.t + 1)
                            nc.gpsimd.tensor_tensor(rso[:, A.par, 1:2], rso[:, A.par, 0:1], half[:, 0:1], ALU.pow).then_inc(S["o_rstd"].sem, 1)
                        F = T - 4 - e
                        if F.par == 1 and F.ok:
                            g.wait_ge(S["stats"].sem, S["stats"].base + F.t + 1)
                            if after(F.p - 1):
                                g.wait_ge(S["out_rows"].sem, S["out_rows"].base + F.p - 1)
                            nc.gpsimd.tensor_tensor(rs[:, F.u, 0, :], mv[:, F.u, :, 1], eps[:, 0:2], ALU.add).then_inc(S["var_eps"].sem, 1)
                            g.wait_ge(S["var_eps"].sem, S["var_eps"].base + F.p + 1)
                            nc.gpsimd.tensor_tensor(rs[:, F.u, 1, :], rs[:, F.u, 0, :], half[:, 0:2], ALU.pow).then_inc(S["rstd"].sem, 1)
                    pipeline(g, slot)

                @block.tensor
                def _(pe):
                    def front(N, step):
                        if after(N.p * NF + sidx[step]):
                            pe.wait_ge(S["front_out"].sem, S["front_out"].base + N.p * NF + sidx[step])
                        if step == "tx":
                            pe.wait_ge(S["xs"].sem, S["xs"].base + N.p + 1)
                            for a in range(2):
                                m = nc.tensor.transpose(psF[:, a * P:a * P + P], XS[:, N.u, a, :], ident)
                        if step == "tc":
                            pe.wait_ge(S["ctx_normed"].sem, S["ctx_normed"].base + N.p + 1)
                            for a in range(2):
                                m = nc.tensor.transpose(psF[:, a * P:a * P + P], CN[:, N.u, a, :], ident)
                        if step in ("k", "q"):
                            s_, w, ws = (src, k, ks) if step == "k" else (XT, q, qs)
                            if raw:
                                parity_wait(pe, "ctx_in", N, 16)
                            m = nc.tensor.matmul(psF[:, 0:256], w, s_[:, N.u, :], start=True, stop=True)
                            if ws is not None:
                                m = nc.tensor.matmul(psF[:, 256:512], ws, s_[:, N.u, :], start=True, stop=True)
                        if step == "v":
                            for s in range(4):
                                for a in range(2):
                                    m = nc.tensor.matmul(psF[64 * a:64 * a + 64, s * D:s * D + D], srcv[:, N.u, s * SEQ:(s + 1) * SEQ], v, start=True, stop=True)
                        m.then_inc(S["front"].sem, 1)

                    def slot(T):
                        N, K, M = T + 2, T + 1, T + 3
                        if T.par == 0 and N.ok:
                            front(N, "k")
                        if T.par == 1 and K.ok:
                            front(K, "q")
                        def scores(hh):
                            if qs is not None:
                                pe.wait_ge(S["q_roped"].sem, S["q_roped"].base + T.p + 1)
                            else:
                                front_done(pe, T.p, "q")
                            parity_wait(pe, "keys_in", T, 256)
                            if after(T.t - 1):
                                pe.wait_ge(S["shifted"].sem, S["shifted"].base + T.t - 1)
                            if mask is not None:
                                mk = mask(T).unsqueeze(1).to_broadcast([P, 8, SEQ])
                                nc.tensor.matmul(psS[:, T.par, 8 * hh:8 * hh + 8, :], idb[:, :], mk, start=True, stop=False, skip_group_check=True)
                            for s in range(2):
                                q4 = 2 * T.par + s
                                m = nc.tensor.matmul(psS[64 * s:64 * s + 64, T.par, 8 * hh:8 * hh + 8, :],
                                                     QT[:, T.u, q4 * SEQ:(q4 + 1) * SEQ], KB[:, T.u, 8 * hh:8 * hh + 8, q4, :],
                                                     start=mask is None, stop=True, skip_group_check=True)
                            if hh == 1:
                                m.then_inc(S["scores"].sem, 1)

                        if T.ok:
                            scores(0)
                        A = T - 3 - e
                        if A.ok:
                            pe.wait_ge(S["normed"].sem, S["normed"].base + (T.t - 2 if T.i is not None else min(T.c - 2, TILES)))
                            if ln_o:
                                pe.wait_ge(S["o_ready"].sem, S["o_ready"].base + A.t + 1)
                            nc.tensor.transpose(psOT, (OL if ln_o else ON)[:, A.par, :], ident).then_inc(S["o_turned"].sem, 1)
                        if T.ok:
                            scores(1)
                        A = T - 3 - e
                        if A.ok:
                            pe.wait_ge(S["ot"].sem, S["ot"].base + A.t + 1)
                            nc.tensor.matmul(psJ, OT[:, A.par, :], o, start=True, stop=True).then_inc(S["proj"].sem, 1)
                        A = T - 1
                        if A.ok:
                            pe.wait_ge(S["probs"].sem, S["probs"].base + A.t + 1)
                            for hb, freed, turned in ((0, S["pt_a"], S["turned_a"]), (1, S["pt_b"], S["turned_b"])):
                                if after(A.t):
                                    pe.wait_ge(freed.sem, freed.base + A.t)
                                for j in range(4):
                                    b = hb * 4 + j
                                    m = nc.tensor.transpose(psP[:, hb, j, :], PR[:, A.par, 2 * b:2 * b + 2, :].rearrange("p h k -> p (h k)"), ident)
                                m.then_inc(turned.sem, 1)
                        if T.par == 1 and K.ok:
                            front(K, "v")
                        A = T - 2
                        if A.ok:
                            pe.wait_ge(S["pt_a"].sem, S["pt_a"].base + A.t + 1)
                            pe.wait_ge(S["pt_b"].sem, S["pt_b"].base + A.t + 1)
                            front_done(pe, A.p, "v")
                            if after(A.t - e):
                                pe.wait_ge(S["res"].sem, S["res"].base + A.t - e)
                            for b in range(HP):
                                for s in range(2):
                                    m = nc.tensor.matmul(psO[64 * s:64 * s + 64, b * VW:(b + 1) * VW], PT[:, A.par, b, 64 * s:64 * s + 64],
                                                         VB[:, A.u, 2 * A.par + s, b, :], start=True, stop=True)
                            m.then_inc(S["pv"].sem, 1)
                        if T.par == 1 and M.ok:
                            front(M, "tx")
                            if "tc" in steps:
                                front(M, "tc")
                    pipeline(pe, slot)

                @block.scalar
                def _(act):
                    def slot(T):
                        N, K, M = T + 2, T + 1, T + 3
                        if T.par == 0 and N.ok and ks is None and not keymask:
                            wait_front(act, N.p, "k")
                            parity_wait(act, "keys_in", N - 4, 256)
                            nc.scalar.activation(KT[:, N.u, :], psF[:, 0:256], ACT.Identity, bias=bk if bk is not None else zero).then_inc(S["front_out"].sem, 1)
                        if T.par == 1 and K.ok and qs is None:
                            wait_front(act, K.p, "q")
                            if after(2 * K.p - 2):
                                act.wait_ge(S["scores"].sem, S["scores"].base + 2 * K.p - 2)
                            nc.scalar.activation(QT[:, K.u, :], psF[:, 0:256], ACT.Identity, bias=bq if bq is not None else zero).then_inc(S["front_out"].sem, 1)
                        A = T - 3 - e
                        if A.ok:
                            act.wait_ge(S["o_turned"].sem, S["o_turned"].base + A.t + 1)
                            if after(A.t - 1):
                                act.wait_ge(S["proj"].sem, S["proj"].base + A.t - 1)
                            nc.scalar.activation(OT[:, A.par, :], psOT, ACT.Copy).then_inc(S["ot"].sem, 1)
                        A = T - 1
                        if A.ok:
                            act.wait_ge(S["turned_a"].sem, S["turned_a"].base + A.t + 1)
                            if after(A.t - 1):
                                act.wait_ge(S["pv"].sem, S["pv"].base + A.t - 1)
                            nc.scalar.activation(PT[:, A.par, 0:4, :], psP[:, 0], ACT.Copy).then_inc(S["pt_a"].sem, 1)
                        if T.ok:
                            act.wait_ge(S["shifted"].sem, S["shifted"].base + T.t + 1)
                            nc.scalar.activation(PR[:, T.par], PR[:, T.par], ACT.Exp, scale=scale).then_inc(S["probs"].sem, 1)
                        if T.par == 1 and K.ok:
                            wait_front(act, K.p, "v")
                            if after(2 * (K.p - 1)):
                                act.wait_ge(S["pv"].sem, S["pv"].base + 2 * (K.p - 1))
                            nc.scalar.activation(VB[0:64, K.u, :, :, 0:HD].rearrange("p s b d -> p (s b) d"),
                                                 psF[0:64, :].rearrange("p (b h d) -> p b h d", h=2, d=HD)[:, :, 0, :], ACT.Copy).then_inc(S["front_out"].sem, 1)
                        if T.par == 1 and M.ok:
                            wait_front(act, M.p, "tx")
                            if after((M.p - 2) * NS + (sidx["q"] + 1 if cross else NS)):
                                act.wait_ge(S["front"].sem, S["front"].base + (M.p - 2) * NS + (sidx["q"] + 1 if cross else NS))
                            nc.scalar.activation(XT[:, M.u, :], psF[:, 0:256], ACT.Copy).then_inc(S["front_out"].sem, 1)
                            if "tc" in steps:
                                wait_front(act, M.p, "tc")
                                if after((M.p - 2) * NS + NS):
                                    act.wait_ge(S["front"].sem, S["front"].base + (M.p - 2) * NS + NS)
                                nc.scalar.activation(CT[:, M.u, :], psF[:, 0:256], ACT.Copy).then_inc(S["front_out"].sem, 1)
                    pipeline(act, slot)

                @block.vector
                def _(dv):
                    def rope_parts(N, step, parts, tab, n, roped):
                        wait_front(dv, N.p, step)
                        if after(N.p):
                            dv.wait_ge(roped.sem, roped.base + N.p)
                        by_seq = lambda ap: ap.rearrange("p (s k) -> p s k", s=4)
                        for j, (vec, op) in enumerate(parts):
                            table = rope[:, tab + j, :].unsqueeze(1).to_broadcast([P, 4, SEQ])
                            m = nc.vector.scalar_tensor_tensor(by_seq(RA[:, n, j]), by_seq(psF[:, 256 * j:256 * j + 256]), vec, table, op, ALU.mult)
                        m.then_inc(S["front_out"].sem, 1)

                    def part(g_, b_):
                        return (g_, ALU.mult) if g_ is not None else (b_ if b_ is not None else zero, ALU.add)

                    def slot(T):
                        N, K = T + 2, T + 1
                        A = T - 4
                        if ln_o and A.ok:
                            dv.wait_ge(S["o_rstd"].sem, S["o_rstd"].base + A.t + 1)
                            if after(A.t - 1):
                                dv.wait_ge(S["o_turned"].sem, S["o_turned"].base + A.t - 1)
                            nc.vector.tensor_scalar(OL[:, A.par, :], ON[:, A.par, :], mvo[:, A.par, 0:1], rso[:, A.par, 1:2], ALU.subtract, ALU.mult).then_inc(S["o_ready"].sem, 1)
                        A = T - 3
                        if A.ok:
                            dv.wait_ge(S["pv"].sem, S["pv"].base + A.t + 1)
                            o3 = psO.rearrange("p (b c) -> p b c", c=VW)
                            nc.vector.reciprocal(rden[:, A.par], o3[:, :, 2 * HD:VW]).then_inc(S["recip"].sem, 1)
                            dv.wait_ge(S["recip"].sem, S["recip"].base + A.t + 1)
                            if after(A.t - 1):
                                dv.wait_ge((S["o_ready"] if ln_o else S["o_turned"]).sem, (S["o_ready"] if ln_o else S["o_turned"]).base + A.t - 1)
                            nc.vector.tensor_tensor(ON[:, A.par, :].rearrange("p (b h d) -> p b h d", h=2, d=HD),
                                                    o3[:, :, 0:2 * HD].rearrange("p b (h d) -> p b h d", h=2),
                                                    rden[:, A.par].unsqueeze(3).to_broadcast([P, HP, 2, HD]), ALU.mult).then_inc(S["normed"].sem, 1)
                            if ln_o:
                                dv.wait_ge(S["normed"].sem, S["normed"].base + A.t + 1)
                                nc.vector.tensor_tensor(ON[:, A.par, :], ON[:, A.par, :], rowx[:, 1, :], ALU.add).then_inc(S["o_sum"].sem, 1)
                                dv.wait_ge(S["o_sum"].sem, S["o_sum"].base + A.t + 1)
                                nc.vector.bn_stats(st6o[:, A.par, :], ON[:, A.par, :]).then_inc(S["o_bn"].sem, 1)
                                dv.wait_ge(S["o_bn"].sem, S["o_bn"].base + A.t + 1)
                                pace(nc.vector, S)
                                nc.vector.bn_aggr(mvo[:, A.par, :], st6o[:, A.par, :]).then_inc(S["o_stats"].sem, 1)
                        if T.par == 0 and N.ok:
                            if ks is not None:
                                rope_parts(N, "k", (part(gk, bk), part(gks, bks)), ck, 0, S["k_roped"])
                            elif keymask:
                                wait_front(dv, N.p, "k")
                                dv.wait_ge(S["mask_used"].sem, S["mask_used"].base + N.p + 1)
                                parity_wait(dv, "keys_in", N - 4, 256)
                                nc.vector.scalar_tensor_tensor(KT[:, N.u, :], psF[:, 0:256], bk, MF[:, N.u, :], ALU.add, ALU.mult).then_inc(S["front_out"].sem, 1)
                        if T.par == 1 and K.ok and qs is not None:
                            rope_parts(K, "q", (part(gq, bq), part(gqs, bqs)), cq, 1, S["q_roped"])
                        if T.ok:
                            dv.wait_ge(S["scores"].sem, S["scores"].base + T.t + 1)
                            nc.vector.tensor_reduce(mx[:, T.par, :], psS[:, T.par], AX, ALU.max).then_inc(S["maxed"].sem, 1)
                        J = T - 3 - e
                        if J.ok:
                            dv.wait_ge(S["proj"].sem, S["proj"].base + J.t + 1)
                            if bias_row is not None:
                                dv.wait_ge(S["xres"].sem, S["xres"].base + J.p + 1)
                            res = XR[:, J.u, J.par, :] if bias_row is not None else xrow(J.t)
                            if after(J.p - 1):
                                dv.wait_ge(S["out_rows"].sem, S["out_rows"].base + J.p - 1)
                            nc.vector.tensor_tensor(RB[:, J.u, J.par, :], psJ, res, ALU.add).then_inc(S["res"].sem, 1)
                        if T.ok:
                            dv.wait_ge(S["maxed"].sem, S["maxed"].base + T.t + 1)
                            if after(T.t - 1):
                                dv.wait_ge(S["turned_b"].sem, S["turned_b"].base + T.t - 1)
                            nc.vector.tensor_tensor(PR[:, T.par], psS[:, T.par], mx[:, T.par, :].unsqueeze(2).to_broadcast([P, HEADS, SEQ]), ALU.subtract).then_inc(S["shifted"].sem, 1)
                        if J.ok:
                            dv.wait_ge(S["res"].sem, S["res"].base + J.t + 1)
                            nc.vector.bn_stats(st6[:, J.par, :], RB[:, J.u, J.par, :]).then_inc(S["bn"].sem, 1)
                        A = T - 1
                        if A.ok:
                            dv.wait_ge(S["turned_b"].sem, S["turned_b"].base + A.t + 1)
                            if after(A.t - 1):
                                dv.wait_ge(S["pv"].sem, S["pv"].base + A.t - 1)
                            nc.vector.tensor_copy(PT[:, A.par, 4:8, :], psP[:, 1]).then_inc(S["pt_b"].sem, 1)
                        if J.ok:
                            dv.wait_ge(S["bn"].sem, S["bn"].base + J.t + 1)
                            pace(nc.vector, S)
                            nc.vector.bn_aggr(mv[:, J.u, J.par, :], st6[:, J.par, :]).then_inc(S["stats"].sem, 1)
                        A = T - 5 - e
                        if A.par == 1 and A.ok:
                            dv.wait_ge(S["rstd"].sem, S["rstd"].base + A.p + 1)
                            for a in range(2):
                                xo = xrow((A - 1 + a).t)
                                m = nc.vector.tensor_scalar(xo, RB[:, A.u, a, :], mv[:, A.u, a, 0:1], rs[:, A.u, 1, a:a + 1], ALU.subtract, ALU.mult)
                                if affine is not None:
                                    m.then_inc(S["unscaled"].sem, 1)
                                    dv.wait_ge(S["unscaled"].sem, S["unscaled"].base + 2 * A.t - 1 + 2 * a)
                                    nc.vector.tensor_tensor(xo, xo, affine[0], ALU.mult).then_inc(S["unscaled"].sem, 1)
                                    dv.wait_ge(S["unscaled"].sem, S["unscaled"].base + 2 * A.t + 2 * a)
                                    m = nc.vector.tensor_tensor(xo, xo, affine[1], ALU.add)
                            m.then_inc(S["out_rows"].sem, 1)
                        if T.par == 1 and K.ok:
                            wait_front(dv, K.p, "v")
                            if after(2 * (K.p - 1)):
                                dv.wait_ge(S["pv"].sem, S["pv"].base + 2 * (K.p - 1))
                            nc.vector.tensor_copy(VB[64:128, K.u, :, :, HD:2 * HD].rearrange("p s b d -> p (s b) d"),
                                                  psF[64:128, :].rearrange("p (b h d) -> p b h d", h=2, d=HD)[:, :, 1, :]).then_inc(S["front_out"].sem, 1)
                        M = T + 3
                        if T.par == 1 and M.ok and keymask:
                            parity_wait(dv, "mask_in", M, 16)
                            nc.vector.tensor_scalar(MF[:, M.u, :], MI[:, M.u, :], 0.0, None, ALU.not_equal).then_inc(S["mask_used"].sem, 1)
                    pipeline(dv, slot)

            S.advance(dict(front=NS * PAIRS, front_out=NF * PAIRS, keys_in0=256 * PAIRS // 2, keys_in1=256 * PAIRS // 2))
            S.advance(dict.fromkeys(("xs", "rstd", "var_eps", "out_rows"), PAIRS))
            S.advance(dict.fromkeys(("scores", "shifted", "maxed", "probs", "pt_a", "pt_b", "turned_a", "turned_b", "pv", "normed",
                                     "recip", "ot", "o_turned", "proj", "res", "bn", "stats"), TILES))
            S.advance(dict.fromkeys(("q_roped",), PAIRS), qs is not None)
            S.advance(dict.fromkeys(("k_roped",), PAIRS), ks is not None)
            S.advance(dict.fromkeys(("xres",), PAIRS), bias_row is not None)
            S.advance(dict(mask_used=PAIRS, mask_in0=8 * PAIRS, mask_in1=8 * PAIRS), keymask)
            S.advance(dict(ctx_in0=8 * PAIRS, ctx_in1=8 * PAIRS), raw)
            S.advance(dict(rows_in0=8 * PAIRS, rows_in1=8 * PAIRS, ctx_normed=PAIRS), cross and norm is not None)
            S.advance(dict(x_centred=PAIRS), norm == "ln")
            S.advance(dict(unscaled=2 * TILES), affine is not None)
            S.advance(dict(ctx_centred=PAIRS), norm == "ln" and cross)
            S.advance(dict.fromkeys(("o_sum", "o_bn", "o_stats", "o_eps", "o_rstd", "o_ready"), TILES), ln_o)
            mem.close()

        def store():
            with nc.Block() as block:
                @block.sync
                def _(sp):
                    sp.dma_start(out.rearrange("(t p) d -> p t d", p=P), X[:, :, :]).then_inc(S["stored"].sem, 16)
                    sp.wait_ge(S["stored"].sem, 16)

        def key_masks(which):
            mem = Memory(nc, "masks_" + which)
            MK = mem.sb("MK", [P, TILES * SEQ // 4], I32)
            KEEP = mem.sb("KEEP", [P, TILES * SEQ // 4])
            n = 4
            w = TILES // n
            src = io["mask"] if which == "mask" else io["cell"]
            with nc.Block() as block:
                @block.sync
                def _(sp):
                    if which == "cell":
                        sp.dma_start(cellq[:, :], io["cellT"]).then_inc(S["mask_rows"].sem, 16)
                    for r in range(n):
                        if r:
                            sp.wait_ge(S["mask_made"].sem, S["mask_made"].base + r)
                        for s in range(2):
                            rows = src.rearrange("(t s k) -> s t k", s=2, k=SEQ)[s, r * w:(r + 1) * w, :]
                            sp.dma_start(MK[64 * s:64 * s + 64, 0:w * SEQ].rearrange("p (t k) -> p t k", k=SEQ),
                                         rows.partition_broadcast(64)).then_inc(S["mask_rows"].sem, 16)

                @block.vector
                def _(dv):
                    own = 16 if which == "cell" else 0
                    for r in range(n):
                        dv.wait_ge(S["mask_rows"].sem, S["mask_rows"].base + own + 32 * (r + 1))
                        mk = MK[:, 0:w * SEQ].rearrange("p (t k) -> p t k", k=SEQ)
                        keep = KEEP[:, :].rearrange("p (t k) -> p t k", k=SEQ)
                        if which == "mask":
                            nc.vector.tensor_scalar(keep, mk, 0.0, None, ALU.not_equal).then_inc(S["mask_keep"].sem, 1)
                        else:
                            nc.vector.tensor_tensor(keep, mk, cellq[:, r * w:(r + 1) * w].unsqueeze(2).to_broadcast([P, w, SEQ]), ALU.is_equal).then_inc(S["mask_keep"].sem, 1)
                        dv.wait_ge(S["mask_keep"].sem, S["mask_keep"].base + r + 1)
                        out_ = maskk[:, r * w:(r + 1) * w, :]
                        nc.vector.tensor_scalar(out_, keep, 1.0, -NEG, ALU.subtract, ALU.mult).then_inc(S["mask_neg"].sem, 1)
                        dv.wait_ge(S["mask_neg"].sem, S["mask_neg"].base + r + 1)
                        if which == "cell":
                            nc.vector.tensor_tensor(out_, out_, causal[:, :].unsqueeze(1).to_broadcast([P, w, SEQ]), ALU.add).then_inc(S["mask_made"].sem, 1)
                        else:
                            nc.vector.tensor_copy(keep, keep).then_inc(S["mask_made"].sem, 1)
            S.advance(dict(mask_rows=32 * n + (16 if which == "cell" else 0), mask_made=n, mask_neg=n, mask_keep=n))
            mem.close()

        def source_stats(norm):
            n = 8
            w = TILES // n
            mem = Memory(nc, "stats_" + norm)
            chunk = mem.sb("chunk", [P, w, D])
            sq = mem.sb("sq", [P, w, D])
            bn = mem.sb("bn", [P, w, 6])
            with nc.Block() as block:
                @block.sync
                def _(sp):
                    for r in range(n):
                        if after(2 * r):
                            sp.wait_ge(S["chunk_used"].sem, S["chunk_used"].base + 2 * r)
                        sp.dma_start(chunk[:, :, :], io["ctx"][r * w * P:(r + 1) * w * P, :].rearrange("(t p) d -> p t d", p=P)).then_inc(S["chunk_in"].sem, 16)

                @block.vector
                def _(dv):
                    k = 0
                    for r in range(n):
                        for src_, st in ((X[:, r * w:(r + 1) * w, :], stat), (chunk[:, :, :], stat2)):
                            if st is stat2:
                                dv.wait_ge(S["chunk_in"].sem, S["chunk_in"].base + 16 * (r + 1))
                            dst = st[:, r * w:(r + 1) * w, :]
                            if after(k):
                                dv.wait_ge(S["chunk_used"].sem, S["chunk_used"].base + k)
                            k += 1
                            if norm == "rms":
                                nc.vector.tensor_tensor(sq[:, :, :], src_, src_, ALU.mult).then_inc(S["squared"].sem, 1)
                                dv.wait_ge(S["squared"].sem, S["squared"].base + k)
                                nc.vector.tensor_reduce(dst.rearrange("p t h -> p (t h)"), sq[:, :, :].rearrange("p t (h d) -> p (t h) d", d=HD), AX, ALU.add).then_inc(S["chunk_used"].sem, 1)
                            else:
                                for j in range(w):
                                    m = nc.vector.bn_stats(bn[:, j, :], src_[:, j, :])
                                m.then_inc(S["squared"].sem, 1)
                                dv.wait_ge(S["squared"].sem, S["squared"].base + k)
                                for j in range(w):
                                    m = nc.vector.bn_aggr(dst[:, j, 0:2], bn[:, j, :])
                                m.then_inc(S["chunk_used"].sem, 1)
                    dv.wait_ge(S["chunk_used"].sem, S["chunk_used"].base + 2 * n)
                    for st, ready in ((stat, S["stat_var"]), (stat2, S["stat2_var"])):
                        v = st[:, :, :] if norm == "rms" else st[:, :, 1:2]
                        nc.vector.tensor_scalar(v, v, 1.0 / HD if norm == "rms" else 1.0, RMS_EPS if norm == "rms" else LN_EPS, ALU.mult, ALU.add).then_inc(ready.sem, 1)
                    for st, ready, n_ in ((stat, S["stat_root"], 1), (stat2, S["stat2_root"], 1)):
                        v = st[:, :, :] if norm == "rms" else st[:, :, 1:2]
                        dv.wait_ge(ready.sem, ready.base + 1)
                        nc.vector.reciprocal(v, v)

                @block.scalar
                def _(act):
                    for st, ready, done in ((stat, S["stat_var"], S["stat_root"]), (stat2, S["stat2_var"], S["stat2_root"])):
                        v = st[:, :, :] if norm == "rms" else st[:, :, 1:2]
                        act.wait_ge(ready.sem, ready.base + 1)
                        nc.scalar.activation(v, v, ACT.Sqrt).then_inc(done.sem, 1)
            S.advance(dict(chunk_used=2 * n, chunk_in=16 * n, squared=2 * n, stat_var=1, stat2_var=1, stat_root=1, stat2_root=1))
            mem.close()

        def fold_norms():
            mats = [("L3xq", "L3gq", "L3aq", "L3bq"), ("L3xqs", "L3gq", "L3aq", "L3bqs"), ("L3xk", "L3gk", "L3ak", "L3bk"),
                    ("L3xks", "L3gk", "L3ak", "L3bks"), ("L3xv", "L3gv", "L3av", None), ("L3xo", "L3go", "L3ao", None)]
            mem = Memory(nc, "fold")
            psF, bvb = mem.pb("psF", [P, 512]), mem.sb("bvb", [P, D])
            with nc.Block() as block:
                @block.vector
                def _(dv):
                    for n, (w, g_, _, _) in enumerate(mats):
                        nc.vector.tensor_scalar(wp[:, n, :], Wm(w), C(g_), None, ALU.mult)
                    for n, b in enumerate(("L3av", "L3ao", "L3bv")):
                        dst = colb[:, n, :] if n < 2 else bvb[:, :]
                        m = nc.vector.tensor_scalar(dst, ident, 0.0, C(b), ALU.mult, ALU.add)
                    m.then_inc(S["prep"].sem, 1)
                    dv.wait_ge(S["prep_pe"].sem, S["prep_pe"].base + 1)
                    for n, (_, _, _, b) in enumerate(mats[:4]):
                        nc.vector.tensor_scalar(colx[:, n:n + 1], psF[:, n:n + 1], C(b), None, ALU.add)
                    nc.vector.tensor_copy(rowx[:, 1, :], psF[:, 128:256])
                    nc.vector.tensor_tensor(rowx[:, 0, :], psF[:, 256:384], R("L3b"), ALU.add)

                @block.tensor
                def _(pe):
                    pe.wait_ge(S["prep"].sem, S["prep"].base + 1)
                    for n, (w, _, b, _) in enumerate(mats[:4]):
                        nc.tensor.matmul(psF[:, n:n + 1], Wm(w), C(b), start=True, stop=True)
                    nc.tensor.matmul(psF[:, 128:256], colb[:, 0, :], Wm("L3xv"), start=True, stop=False)
                    nc.tensor.matmul(psF[:, 128:256], bvb[:, :], ident, start=False, stop=True)
                    nc.tensor.matmul(psF[:, 256:384], colb[:, 1, :], Wm("L3xo"), start=True, stop=True).then_inc(S["prep_pe"].sem, 1)
            S.advance(dict(prep=1, prep_pe=1))
            mem.close()

        TB = BATCH // P

        class Bat:

            def __init__(self, i, c):
                self.i, self.c, self.u = i, c, c % 2
                self.ok = i is not None or 0 <= c < NBATCH
                self.b = c if i is None else i * 2 + c

            def __sub__(self, k):
                return Bat(self.i, self.c - k)

            def tiles(self):
                return bass.ds(self.b * TB, TB)

        def batches(eng, slot, depth):
            first = 2
            turns = (NBATCH - first) // 2
            for c in range(first):
                slot(Bat(None, c))
            with eng.Fori(0, turns) as i:
                for c in range(2):
                    slot(Bat(i, first + c))
            for c in range(first + 2 * turns, NBATCH + depth):
                slot(Bat(None, c))

        def moe(L, ne, fc, fw, gated, w1, w2, extra, XO=None):
            mem = Memory(nc, L)
            W1 = mem.sb("W1", [P, ne, fc * fw * (2 if gated else 1)])
            W2 = mem.sb("W2", [fw, ne, fc, D])
            RW = mem.sb("RW", [P, 16])
            RBI = mem.sb("RBI", [P, 16])
            B1 = mem.sb("B1", [P, ne, fc])
            B2 = mem.sb("B2", [ne, D])
            LG = mem.sb("LG", [P, TILES, 16])
            gate = mem.sb("gate", [P, TILES, ne])
            XS = mem.sb("XS", [P, 2, TB, D])
            XT = mem.sb("XT", [P, 2, BATCH])
            SG = mem.sb("SG", [fw, 2, BATCH])
            G = mem.sb("G", [fw, 2, fc, BATCH])
            ACC = mem.sb("ACC", [P, 2, TB, D])
            GS = mem.sb("GS", [P, 2, TB, ne])
            GT = mem.sb("GT", [ne, 2, BATCH])
            st, ag, rt = mem.sb("st", [P, 2, TB, 6]), mem.sb("ag", [P, 2, TB, 2]), mem.sb("rt", [P, 2, 2, TB])
            t1, t2, t3, t4 = (mem.sb(f"t{n}", [P, TILES, 8]) for n in range(4))
            psX = mem.pb("psX", [P, BATCH])
            psL = mem.pb("psL", [P, TB, 128])
            psY = mem.pb("psY", [P, 2, 2, BATCH])
            psO = mem.pb("psO", [P, 2, TB, D])
            nl = 8 if gated else 12
            nx = 2 if gated else 3
            steps = ne * fc

            with nc.Block() as block:
                @block.sync
                def _(sp):
                    ld = [(W1[:, :, :], io[w1]), (W2[:, :, :, :], io[w2]), (RW[:, 0:nl], io[extra["rw"]])]
                    if not gated:
                        ld += [(B1[:, :, :], io[extra["b1"]]), (B2[:, :], io[extra["b2"]]), (RBI[:, 0:nl], io[extra["rb"]].partition_broadcast(P))]
                    for d, s_ in ld:
                        sp.dma_start(d, s_).then_inc(S["weights_in"].sem, 16)
                    sp.wait_ge(S["weights_in"].sem, S["weights_in"].base + 16 * len(ld))
                S.advance(dict(weights_in=16 * (6 if not gated else 3)))

            with nc.Block() as block:
                @block.gpsimd
                def _(g):
                    def slot(B):
                        if after(B.b - 1):
                            g.wait_ge(S["turned"].sem, S["turned"].base + B.b - 1)
                        nc.gpsimd.tensor_copy(XS[:, B.u], X[:, B.tiles(), :]).then_inc(S["xs"].sem, 1)
                    batches(g, slot, 0)

                @block.tensor
                def _(pe):
                    def slot(B):
                        pe.wait_ge(S["xs"].sem, S["xs"].base + B.b + 1)
                        if after(B.b):
                            pe.wait_ge(S["xt_out"].sem, S["xt_out"].base + B.b)
                        for j in range(TB):
                            m = nc.tensor.transpose(psX[:, j * P:(j + 1) * P], XS[:, B.u, j, :], ident)
                        m.then_inc(S["turned"].sem, 1)
                        pe.wait_ge(S["xt_out"].sem, S["xt_out"].base + B.b + 1)
                        if after(B.b):
                            pe.wait_ge(S["logits_out"].sem, S["logits_out"].base + B.b)
                        for j in range(TB):
                            m = nc.tensor.matmul(psL[:, j, 0:nl], XT[:, B.u, j * P:(j + 1) * P], RW[:, 0:nl], start=True, stop=True)
                        m.then_inc(S["logits"].sem, 1)
                    batches(pe, slot, 0)

                @block.scalar
                def _(act):
                    def slot(B):
                        act.wait_ge(S["turned"].sem, S["turned"].base + B.b + 1)
                        if after(B.b - 1):
                            act.wait_ge(S["logits"].sem, S["logits"].base + B.b - 1)
                        nc.scalar.activation(XT[:, B.u, :], psX[:, :], ACT.Copy).then_inc(S["xt_out"].sem, 1)
                    batches(act, slot, 0)

                @block.vector
                def _(dv):
                    def slot(B):
                        dv.wait_ge(S["logits"].sem, S["logits"].base + B.b + 1)
                        dst = LG[:, B.tiles(), 0:nl]
                        if gated:
                            nc.vector.tensor_copy(dst, psL[:, :, 0:nl]).then_inc(S["logits_out"].sem, 1)
                        else:
                            nc.vector.tensor_tensor(dst, psL[:, :, 0:nl], RBI[:, 0:nl].unsqueeze(1).to_broadcast([P, TB, nl]), ALU.add).then_inc(S["logits_out"].sem, 1)
                    batches(dv, slot, 0)
            S.advance(dict.fromkeys(("xs", "turned", "xt_out", "logits", "logits_out"), NBATCH))

            T_ = [P, TILES]
            with nc.Block() as block:
                cnt = [0]

                @block.vector
                def _(dv):
                    def link(ins):
                        ins.then_inc(S["route"].sem, 1)
                        cnt[0] += 1
                        dv.wait_ge(S["route"].sem, S["route"].base + cnt[0])
                    b3 = lambda ap, n: ap.unsqueeze(2).to_broadcast([P, TILES, n])
                    if gated:
                        lg = LG[:, :, 0:8]
                        mx_, sec = t2[:, :, 0], t2[:, :, 1]
                        link(nc.vector.tensor_reduce(mx_, lg, AX, ALU.max))
                        link(nc.vector.tensor_tensor(t1[:, :, :], lg, b3(mx_, 8), ALU.subtract))
                        link(nc.vector.tensor_scalar(t3[:, :, :], t1[:, :, :], 0.0, NEG, ALU.is_ge, ALU.mult))
                        link(nc.vector.tensor_tensor(t3[:, :, :], t3[:, :, :], t1[:, :, :], ALU.add))
                        link(nc.vector.tensor_reduce(sec, t3[:, :, :], AX, ALU.max))
                        link(nc.vector.tensor_tensor(t3[:, :, :], t1[:, :, :], b3(sec, 8), ALU.is_ge))
                        dv.wait_ge(S["route_exp"].sem, S["route_exp"].base + 1)
                        link(nc.vector.tensor_reduce(mx_, t4[:, :, :], AX, ALU.add))
                        link(nc.vector.reciprocal(mx_, mx_))
                        link(nc.vector.tensor_tensor(t3[:, :, :], t3[:, :, :], t4[:, :, :], ALU.mult))
                        link(nc.vector.tensor_tensor(gate[:, :, :], t3[:, :, :], b3(mx_, 8), ALU.mult))
                    else:
                        gl, el = LG[:, :, 0:4], LG[:, :, 4:12]
                        mg, sg_ = t2[:, :, 0], t2[:, :, 1]
                        m2, s2 = t2[:, :, 4:8], t3[:, :, 0:4]
                        pair = lambda ap: ap.rearrange("p t (g e) -> p (t g) e", e=2)
                        flat = lambda ap: ap.rearrange("p t g -> p (t g)")
                        link(nc.vector.tensor_reduce(mg, gl, AX, ALU.max))
                        el4 = el.rearrange("p t (g e) -> p t g e", e=2)
                        link(nc.vector.tensor_tensor(m2, el4[:, :, :, 0], el4[:, :, :, 1], ALU.max))
                        link(nc.vector.tensor_tensor(t1[:, :, 0:4], gl, b3(mg, 4), ALU.subtract))
                        for j in range(2):
                            dst = t4[:, :, :].rearrange("p t (g e) -> p t g e", e=2)[:, :, :, j]
                            link(nc.vector.tensor_tensor(dst, el4[:, :, :, j], m2, ALU.subtract))
                        link(nc.vector.tensor_scalar(gate[:, :, :], t4[:, :, :], 0.0, None, ALU.is_ge))
                        link(nc.vector.tensor_scalar(t3[:, :, 4:8], t1[:, :, 0:4], 0.0, None, ALU.is_ge))
                        dv.wait_ge(S["route_exp"].sem, S["route_exp"].base + 1)
                        link(nc.vector.tensor_reduce(sg_, t1[:, :, 0:4], AX, ALU.add))
                        t44 = t4[:, :, :].rearrange("p t (g e) -> p t g e", e=2)
                        link(nc.vector.tensor_tensor(s2, t44[:, :, :, 0], t44[:, :, :, 1], ALU.add))
                        link(nc.vector.tensor_tensor(s2, s2, b3(sg_, 4), ALU.mult))
                        link(nc.vector.reciprocal(s2, s2))
                        link(nc.vector.tensor_tensor(s2, s2, t3[:, :, 4:8], ALU.mult))
                        for j in range(2):
                            dst = gate[:, :, :].rearrange("p t (g e) -> p t g e", e=2)[:, :, :, j]
                            link(nc.vector.tensor_tensor(dst, dst, s2, ALU.mult))

                @block.scalar
                def _(act):
                    if gated:
                        act.wait_ge(S["route"].sem, S["route"].base + 2)
                        nc.scalar.activation(t4[:, :, :], t1[:, :, :], ACT.Exp).then_inc(S["route_exp"].sem, 1)
                    else:
                        act.wait_ge(S["route"].sem, S["route"].base + 7)
                        nc.scalar.activation(t4[:, :, :], t4[:, :, :], ACT.Exp)
                        nc.scalar.activation(t1[:, :, 0:4], t1[:, :, 0:4], ACT.Exp).then_inc(S["route_exp"].sem, 1)
                S.advance(dict(route_exp=1))
            S.advance(dict(route=cnt[0]))

            with nc.Block() as block:
                @block.gpsimd
                def _(g):
                    def slot(B):
                        if B.ok:
                            if after(B.b - 1):
                                g.wait_ge(S["turned"].sem, S["turned"].base + B.b - 1)
                            if not gated:
                                if after(B.b - 1):
                                    g.wait_ge(S["gt_turned"].sem, S["gt_turned"].base + B.b - 1)
                                nc.gpsimd.tensor_copy(GS[:, B.u], gate[:, B.tiles(), :])
                            nc.gpsimd.tensor_copy(XS[:, B.u], X[:, B.tiles(), :]).then_inc(S["xs"].sem, 1)
                        A = B - 1
                        if A.ok:
                            if not gated:
                                g.wait_ge(S["stats"].sem, S["stats"].base + 2 * A.b + 1)
                                nc.gpsimd.tensor_tensor(rt[:, A.u, 0, :], ag[:, A.u, :, 1], eps[:, 0:TB], ALU.add).then_inc(S["var_eps"].sem, 1)
                                g.wait_ge(S["var_eps"].sem, S["var_eps"].base + 2 * A.b + 1)
                                nc.gpsimd.tensor_tensor(rt[:, A.u, 1, :], rt[:, A.u, 0, :], half[:, 0:TB], ALU.pow).then_inc(S["rstd"].sem, 1)
                            k = 1 if gated else 2
                            g.wait_ge(S["stats"].sem, S["stats"].base + k * A.b + k)
                            if after(A.b - 1):
                                g.wait_ge(S["out_rows"].sem, S["out_rows"].base + A.b - 1)
                            nc.gpsimd.tensor_tensor(rt[:, A.u, 0, :], ag[:, A.u, :, 1], eps[:, 0:TB], ALU.add).then_inc(S["var_eps"].sem, 1)
                            g.wait_ge(S["var_eps"].sem, S["var_eps"].base + k * A.b + k)
                            nc.gpsimd.tensor_tensor(rt[:, A.u, 1, :], rt[:, A.u, 0, :], half[:, 0:TB], ALU.pow).then_inc(S["rstd"].sem, 1)
                    batches(g, slot, 1)

                @block.tensor
                def _(pe):
                    def products(B, m):
                        n = B.b * (ne + (0 if gated else 1)) + m
                        pe.wait_ge(S["g_ready"].sem, S["g_ready"].base + B.b * steps + (m + 1) * fc)
                        if after(n - 1):
                            pe.wait_ge(S["o_added"].sem, S["o_added"].base + n - 1)
                        ob = (m + (0 if gated else B.u)) % 2
                        for j in range(TB):
                            for c in range(fc):
                                i_ = nc.tensor.matmul(psO[:, ob, j, :], G[:, m % 2, c, j * P:(j + 1) * P], W2[:, m, c, :], start=c == 0, stop=c == fc - 1)
                        i_.then_inc(S["o_done"].sem, 1)

                    def slot(B):
                        pe.wait_ge(S["xs"].sem, S["xs"].base + B.b + 1)
                        if after(B.b):
                            pe.wait_ge(S["xt_out"].sem, S["xt_out"].base + B.b)
                        for j in range(TB):
                            i_ = nc.tensor.transpose(psX[:, j * P:(j + 1) * P], XS[:, B.u, j, :], ident)
                        i_.then_inc(S["turned"].sem, 1)
                        pe.wait_ge(S["xt_out"].sem, S["xt_out"].base + B.b + 1)
                        for m in range(ne):
                            for c in range(fc):
                                n = B.b * steps + m * fc + c
                                yb = (m * fc + c) % 2
                                if after(n - 1):
                                    pe.wait_ge(S["g_ready"].sem, S["g_ready"].base + n - 1)
                                i_ = nc.tensor.matmul(psY[0:fw, yb, 0, :], W1[:, m, c * fw:(c + 1) * fw], XT[:, B.u, :], start=True, stop=True)
                                if gated:
                                    o_ = fc * fw + c * fw
                                    i_ = nc.tensor.matmul(psY[0:fw, yb, 1, :], W1[:, m, o_:o_ + fw], XT[:, B.u, :], start=True, stop=True)
                                i_.then_inc(S["hidden"].sem, 1)
                            if m:
                                products(B, m - 1)
                        products(B, ne - 1)
                        if not gated:
                            if after(B.b):
                                pe.wait_ge(S["gt_out"].sem, S["gt_out"].base + B.b)
                            for j in range(TB):
                                i_ = nc.tensor.transpose(psL[0:ne, j, :], GS[:, B.u, j, :], ident)
                            i_.then_inc(S["gt_turned"].sem, 1)
                            pe.wait_ge(S["gt_out"].sem, S["gt_out"].base + B.b + 1)
                            pe.wait_ge(S["o_added"].sem, S["o_added"].base + B.b * (ne + 1) + ne - 1)
                            for j in range(TB):
                                i_ = nc.tensor.matmul(psO[:, B.u, j, :], GT[:, B.u, j * P:(j + 1) * P], B2[:, :], start=True, stop=True)
                            i_.then_inc(S["o_done"].sem, 1)
                    batches(pe, slot, 0)

                @block.scalar
                def _(act):
                    def slot(B):
                        act.wait_ge(S["turned"].sem, S["turned"].base + B.b + 1)
                        if after((B.b - 1) * steps):
                            act.wait_ge(S["hidden"].sem, S["hidden"].base + (B.b - 1) * steps)
                        nc.scalar.activation(XT[:, B.u, :], psX[:, :], ACT.Copy).then_inc(S["xt_out"].sem, 1)
                        for m in range(ne):
                            for c in range(fc):
                                n = B.b * steps + m * fc + c
                                yb = (m * fc + c) % 2
                                act.wait_ge(S["hidden"].sem, S["hidden"].base + n + 1)
                                if gated:
                                    if after(n - 1):
                                        act.wait_ge(S["g_ready"].sem, S["g_ready"].base + n - 1)
                                    nc.scalar.activation(SG[:, yb, :], psY[0:fw, yb, 0, :], ACT.Silu).then_inc(S["silu"].sem, 1)
                                else:
                                    if after(B.b * (ne + 1) + m - 1):
                                        act.wait_ge(S["o_done"].sem, S["o_done"].base + B.b * (ne + 1) + m - 1)
                                    i_ = nc.scalar.activation(G[:, m % 2, c, :], psY[0:fw, yb, 0, :], ACT.Relu, bias=B1[:, m, c:c + 1])
                                    i_.then_inc(S["g_ready"].sem, 1)
                        if not gated:
                            act.wait_ge(S["gt_turned"].sem, S["gt_turned"].base + B.b + 1)
                            if after((B.b - 1) * (ne + 1)):
                                act.wait_ge(S["o_done"].sem, S["o_done"].base + (B.b - 1) * (ne + 1))
                            nc.scalar.activation(GT[:, B.u, :], psL[0:ne, :, :].rearrange("p t k -> p (t k)"), ACT.Copy).then_inc(S["gt_out"].sem, 1)
                    batches(act, slot, 0)

                @block.vector
                def _(dv):
                    def slot(B):
                        if B.ok:
                            ob = 0
                            for m in range(ne + 1):
                                if m < ne and gated:
                                    for c in range(fc):
                                        n = B.b * steps + m * fc + c
                                        yb = (m * fc + c) % 2
                                        dv.wait_ge(S["silu"].sem, S["silu"].base + n + 1)
                                        if after(B.b * ne + m - 1):
                                            dv.wait_ge(S["o_done"].sem, S["o_done"].base + B.b * ne + m - 1)
                                        i_ = nc.vector.tensor_tensor(G[:, m % 2, c, :], SG[:, yb, :], psY[0:fw, yb, 1, :], ALU.mult)
                                        i_.then_inc(S["g_ready"].sem, 1)
                                if m == 2:
                                    tail(B - 1)
                                if m:
                                    add(B, m - 1)
                            if not gated:
                                e = B.b * (ne + 1) + ne
                                dv.wait_ge(S["o_done"].sem, S["o_done"].base + e + 1)
                                dv.wait_ge(S["o_added"].sem, S["o_added"].base + e)
                                nc.vector.tensor_tensor(ACC[:, B.u], ACC[:, B.u], psO[:, B.u], ALU.add).then_inc(S["o_added"].sem, 1)
                                dv.wait_ge(S["o_added"].sem, S["o_added"].base + e + 1)
                            stats(B, 0)
                        else:
                            tail(B - 1)

                    def add(B, m):
                        e = B.b * (ne if gated else ne + 1) + m
                        ob = (m + (0 if gated else B.u)) % 2
                        dv.wait_ge(S["o_done"].sem, S["o_done"].base + e + 1)
                        if after(e):
                            dv.wait_ge(S["o_added"].sem, S["o_added"].base + e)
                        if m == 0:
                            if after(B.b - 1):
                                dv.wait_ge(S["out_rows"].sem, S["out_rows"].base + B.b - 1)
                        for j in range(TB):
                            t_ = bass.ds(B.b * TB + j, 1)
                            base_ = X[:, t_, :].rearrange("p a d -> p (a d)") if m == 0 else ACC[:, B.u, j, :]
                            i_ = nc.vector.scalar_tensor_tensor(ACC[:, B.u, j, :], psO[:, ob, j, :], gate[:, t_, m:m + 1].rearrange("p a e -> p (a e)"), base_, ALU.mult, ALU.add)
                        i_.then_inc(S["o_added"].sem, 1)

                    def stats(B, second):
                        k = 1 if gated else 2
                        n = k * B.b + second
                        if second == 0:
                            dv.wait_ge(S["o_added"].sem, S["o_added"].base + (B.b + 1) * (ne if gated else ne + 1))
                        for j in range(TB):
                            i_ = nc.vector.bn_stats(st[:, B.u, j, :], ACC[:, B.u, j, :])
                        i_.then_inc(S["bn"].sem, 1)
                        dv.wait_ge(S["bn"].sem, S["bn"].base + n + 1)
                        pace(nc.vector, S)
                        for j in range(TB):
                            i_ = nc.vector.bn_aggr(ag[:, B.u, j, :], st[:, B.u, j, :])
                        i_.then_inc(S["stats"].sem, 1)

                    def tail(A):
                        if not A.ok:
                            return
                        if not gated:
                            dv.wait_ge(S["rstd"].sem, S["rstd"].base + 2 * A.b + 1)
                            for j in range(TB):
                                i_ = nc.vector.tensor_scalar(ACC[:, A.u, j, :], ACC[:, A.u, j, :], ag[:, A.u, j, 0:1], rt[:, A.u, 1, j:j + 1], ALU.subtract, ALU.mult)
                            i_.then_inc(S["own"].sem, 1)
                            k = 3 * A.b
                            dv.wait_ge(S["own"].sem, S["own"].base + k + 1)
                            nc.vector.tensor_tensor(ACC[:, A.u], ACC[:, A.u], R("g2").unsqueeze(1).to_broadcast([P, TB, D]), ALU.mult).then_inc(S["own"].sem, 1)
                            dv.wait_ge(S["own"].sem, S["own"].base + k + 2)
                            nc.vector.tensor_tensor(ACC[:, A.u], ACC[:, A.u], XO[:, A.tiles(), :], ALU.add).then_inc(S["own"].sem, 1)
                            dv.wait_ge(S["own"].sem, S["own"].base + k + 3)
                            stats(A, 1)
                            dv.wait_ge(S["rstd"].sem, S["rstd"].base + 2 * A.b + 2)
                        else:
                            dv.wait_ge(S["rstd"].sem, S["rstd"].base + A.b + 1)
                        for j in range(TB):
                            i_ = nc.vector.tensor_scalar(X[:, bass.ds(A.b * TB + j, 1), :].rearrange("p a d -> p (a d)"), ACC[:, A.u, j, :],
                                                         ag[:, A.u, j, 0:1], rt[:, A.u, 1, j:j + 1], ALU.subtract, ALU.mult)
                        i_.then_inc(S["out_rows"].sem, 1)
                    batches(dv, slot, 1)
            k = 1 if gated else 2
            S.advance(dict.fromkeys(("xs", "turned", "xt_out", "out_rows"), NBATCH))
            S.advance(dict.fromkeys(("hidden", "g_ready"), NBATCH * steps))
            S.advance(dict(silu=NBATCH * steps), gated)
            S.advance(dict.fromkeys(("bn", "stats", "var_eps", "rstd"), k * NBATCH))
            S.advance(dict.fromkeys(("o_done", "o_added"), NBATCH * (ne + (0 if gated else 1))))
            S.advance(dict(own=3 * NBATCH, gt_turned=NBATCH, gt_out=NBATCH), not gated)
            mem.close()

        def row_stats(B, src, st, ag):
            for j in range(TB):
                m = nc.vector.bn_stats(st[:, B.u, j, :], src[:, B.u, j, :])
            m.then_inc(S["bn"].sem, 1)
            nc.vector.wait_ge(S["bn"].sem, S["bn"].base + B.b + 1)
            pace(nc.vector, S)
            for j in range(TB):
                m = nc.vector.bn_aggr(ag[:, B.u, j, :], st[:, B.u, j, :])
            m.then_inc(S["stats"].sem, 1)

        def row_root(B, ag, rt):
            nc.gpsimd.wait_ge(S["stats"].sem, S["stats"].base + B.b + 1)
            nc.gpsimd.tensor_tensor(rt[:, B.u, 0, :], ag[:, B.u, :, 1], eps[:, 0:TB], ALU.add).then_inc(S["var_eps"].sem, 1)
            nc.gpsimd.wait_ge(S["var_eps"].sem, S["var_eps"].base + B.b + 1)
            nc.gpsimd.tensor_tensor(rt[:, B.u, 1, :], rt[:, B.u, 0, :], half[:, 0:TB], ALU.pow).then_inc(S["rstd"].sem, 1)

        def row_out(B, src, ag, rt):
            nc.vector.wait_ge(S["rstd"].sem, S["rstd"].base + B.b + 1)
            for j in range(TB):
                m = nc.vector.tensor_scalar(X[:, bass.ds(B.t0 + j, 1), :].rearrange("p a d -> p (a d)"), src[:, B.u, j, :],
                                            ag[:, B.u, j, 0:1], rt[:, B.u, 1, j:j + 1], ALU.subtract, ALU.mult)
            m.then_inc(S["out_rows"].sem, 1)

        class Micro(Bat):

            def __init__(self, i, c):
                super().__init__(i, c)
                self.e = c // 2 if i is None else i + c // 2
                self.t0 = (self.u * (NBATCH // 2) + self.e) * TB
                self.rows = bass.ds(self.t0, TB)

            def __sub__(self, k):
                return Micro(self.i, self.c - k)

        def micros(eng, slot):
            for c in range(2):
                slot(Micro(None, c))
            with eng.Fori(0, NBATCH // 2 - 1) as i:
                for c in range(2):
                    slot(Micro(i, 2 + c))
            slot(Micro(None, NBATCH))

        FLAT = "p t k -> p (t k)"

        def expert_blocks():
            FC = 4
            mem = Memory(nc, "L2f")
            W1, W2 = mem.sb("W1", [P, 2, FC * D]), mem.sb("W2", [P, 2, FC, D])
            B1, B2 = mem.sb("B1", [P, 2, FC]), mem.sb("B2", [P, 8])
            XS, XN = mem.sb("XS", [P, 2, TB, D]), mem.sb("XN", [P, 2, TB, D])
            XT, XNT, XA = mem.sb("XT", [P, 2, BATCH]), mem.sb("XNT", [P, 2, BATCH]), mem.sb("XA", [P, 2, BATCH])
            H = mem.sb("H", [P, 2, FC, BATCH])
            EO, F = mem.sb("EO", [P, 2, BATCH]), mem.sb("F", [P, 2, BATCH])
            RB = mem.sb("RB", [P, 2, TB, D])
            sti, agi, rti = mem.sb("sti", [P, 2, TB, 6]), mem.sb("agi", [P, 2, TB, 2]), mem.sb("rti", [P, 2, 2, TB])
            st, ag, rt = mem.sb("st", [P, 2, TB, 6]), mem.sb("ag", [P, 2, TB, 2]), mem.sb("rt", [P, 2, 2, TB])
            ps = mem.pb("ps", [P, 2, 4, BATCH])

            with nc.Block() as block:
                @block.sync
                def _(sp):
                    sp.dma_start(B2[:, :], io["b2c"]).then_inc(S["weights_in"].sem, 16)
                    sp.wait_ge(S["weights_in"].sem, S["weights_in"].base + 16)
            S.advance(dict(weights_in=16))

            with nc.Block() as block:
                @block.sync
                def _(sp):
                    def slot(B):
                        if B.ok:
                            if after(B.b - 1):
                                sp.wait_ge(S["expert"].sem, S["expert"].base + B.b - 1)
                            got = (S["w_in0"] if B.u == 0 else S["w_in1"]).sem
                            sp.dma_start(B1[:, B.u, :], io["b1c"][bass.ds(B.e * P, P), :]).then_inc(got, 16)
                            sp.dma_start(W1[:, B.u, :], io["w1c"][bass.ds(B.e * D, D), :]).then_inc(got, 16)
                            sp.dma_start(W2[:, B.u, :, :], io["w2c"][bass.ds(B.e * FC * D, FC * D), :].rearrange("(c p) d -> p c d", p=P)).then_inc(got, 16)
                    micros(sp, slot)

                @block.gpsimd
                def _(g):
                    def slot(B):
                        A = B - 1
                        if B.ok:
                            if after(B.b - 1):
                                g.wait_ge(S["out_rows"].sem, S["out_rows"].base + B.b - 1)
                            nc.gpsimd.tensor_copy(XS[:, B.u], X[:, B.rows, :]).then_inc(S["xs"].sem, 1)
                            g.wait_ge(S["in_stats"].sem, S["in_stats"].base + B.b + 1)
                            nc.gpsimd.tensor_tensor(rti[:, B.u, 0, :], agi[:, B.u, :, 1], eps[:, 0:TB], ALU.add).then_inc(S["in_eps"].sem, 1)
                            g.wait_ge(S["in_eps"].sem, S["in_eps"].base + B.b + 1)
                            nc.gpsimd.tensor_tensor(rti[:, B.u, 1, :], rti[:, B.u, 0, :], half[:, 0:TB], ALU.pow).then_inc(S["in_rstd"].sem, 1)
                        if A.ok:
                            row_root(A, ag, rt)
                    micros(g, slot)

                @block.tensor
                def _(pe):
                    def slot(B):
                        A = B - 1
                        if B.ok:
                            pe.wait_ge(S["xs"].sem, S["xs"].base + B.b + 1)
                            for j in range(TB):
                                nc.tensor.transpose(ps[:, B.u, 0, j * P:(j + 1) * P], XS[:, B.u, j, :], ident)
                            pe.wait_ge(S["xn"].sem, S["xn"].base + B.b + 1)
                            for j in range(TB):
                                m = nc.tensor.transpose(ps[:, B.u, 1, j * P:(j + 1) * P], XN[:, B.u, j, :], ident)
                            m.then_inc(S["turned"].sem, 1)
                        if A.ok:
                            pe.wait_ge(S["gelu"].sem, S["gelu"].base + FC * A.b + FC)
                            for c in range(FC):
                                m = nc.tensor.matmul(ps[:, A.u, 2, :], W2[:, A.u, c, :], H[:, A.u, c, :], start=c == 0, stop=c == FC - 1)
                            m.then_inc(S["expert"].sem, 1)
                        if B.ok:
                            pe.wait_ge(S["xnt_out"].sem, S["xnt_out"].base + B.b + 1)
                            nc.tensor.matmul(ps[:, B.u, 2, :], Wm("L2fa"), XNT[:, B.u, :], start=True, stop=True).then_inc(S["attn"].sem, 1)
                        if A.ok:
                            pe.wait_ge(S["expert_out"].sem, S["expert_out"].base + A.b + 1)
                            nc.tensor.matmul(ps[:, A.u, 3, :], Wm("L2fn"), EO[:, A.u, :], start=True, stop=True).then_inc(S["next"].sem, 1)
                        if B.ok:
                            pe.wait_ge(S["xa"].sem, S["xa"].base + B.b + 1)
                            pe.wait_ge((S["w_in0"] if B.u == 0 else S["w_in1"]).sem, (S["w_in0"] if B.u == 0 else S["w_in1"]).base + 48 * (B.e + 1))
                            for c in range(FC):
                                if after(FC * B.b + c - 1 if c > 1 else 0):
                                    pe.wait_ge(S["gelu"].sem, S["gelu"].base + (FC * B.b + c - 1 if c > 1 else 0))
                                nc.tensor.matmul(ps[:, B.u, c % 2, :], W1[:, B.u, c * D:(c + 1) * D], XA[:, B.u, :], start=True, stop=True).then_inc(S["hidden"].sem, 1)
                                if c == 1 and A.ok:
                                    pe.wait_ge(S["next_out"].sem, S["next_out"].base + A.b + 1)
                                    for j in range(TB):
                                        m = nc.tensor.transpose(ps[:, A.u, 2, j * P:(j + 1) * P], F[:, A.u, j * P:(j + 1) * P], ident)
                                    m.then_inc(S["back"].sem, 1)
                        elif A.ok:
                            pe.wait_ge(S["next_out"].sem, S["next_out"].base + A.b + 1)
                            for j in range(TB):
                                m = nc.tensor.transpose(ps[:, A.u, 2, j * P:(j + 1) * P], F[:, A.u, j * P:(j + 1) * P], ident)
                            m.then_inc(S["back"].sem, 1)
                    micros(pe, slot)

                @block.scalar
                def _(act):
                    def slot(B):
                        A = B - 1
                        if B.ok:
                            act.wait_ge(S["turned"].sem, S["turned"].base + B.b + 1)
                            nc.scalar.activation(XNT[:, B.u, :], ps[:, B.u, 1, :], ACT.Identity, scale=C("L2g"), bias=C("L2b")).then_inc(S["xnt_out"].sem, 1)
                        if A.ok:
                            act.wait_ge(S["next"].sem, S["next"].base + A.b + 1)
                            nc.scalar.activation(F[:, A.u, :], ps[:, A.u, 3, :], ACT.Gelu, bias=C("L2fnb")).then_inc(S["next_out"].sem, 1)
                        if B.ok:
                            for c in range(FC):
                                act.wait_ge(S["hidden"].sem, S["hidden"].base + FC * B.b + c + 1)
                                nc.scalar.activation(H[:, B.u, c, :], ps[:, B.u, c % 2, :], ACT.Gelu,
                                                     bias=B1[:, B.u, c:c + 1]).then_inc(S["gelu"].sem, 1)
                    micros(act, slot)

                @block.vector
                def _(dv):
                    def slot(B):
                        A = B - 1
                        if B.ok:
                            if after(B.b - 1):
                                dv.wait_ge(S["out_rows"].sem, S["out_rows"].base + B.b - 1)
                            for j in range(TB):
                                m = nc.vector.bn_stats(sti[:, B.u, j, :], X[:, bass.ds(B.t0 + j, 1), :].rearrange("p a d -> p (a d)"))
                            m.then_inc(S["in_bn"].sem, 1)
                            dv.wait_ge(S["in_bn"].sem, S["in_bn"].base + B.b + 1)
                            pace(nc.vector, S)
                            for j in range(TB):
                                m = nc.vector.bn_aggr(agi[:, B.u, j, :], sti[:, B.u, j, :])
                            m.then_inc(S["in_stats"].sem, 1)
                            dv.wait_ge(S["in_rstd"].sem, S["in_rstd"].base + B.b + 1)
                            dv.wait_ge(S["xs"].sem, S["xs"].base + B.b + 1)
                            for j in range(TB):
                                m = nc.vector.tensor_scalar(XN[:, B.u, j, :], XS[:, B.u, j, :], agi[:, B.u, j, 0:1], rti[:, B.u, 1, j:j + 1], ALU.subtract, ALU.mult)
                            m.then_inc(S["xn"].sem, 1)
                        if A.ok:
                            dv.wait_ge(S["expert"].sem, S["expert"].base + A.b + 1)
                            nc.vector.tensor_scalar(EO[:, A.u, :], ps[:, A.u, 2, :], B2[:, bass.ds(A.e, 1)], None, ALU.add).then_inc(S["expert_out"].sem, 1)
                        if B.ok:
                            dv.wait_ge(S["turned"].sem, S["turned"].base + B.b + 1)
                            nc.vector.tensor_scalar(XT[:, B.u, :], ps[:, B.u, 0, :], C("L2fab"), None, ALU.add).then_inc(S["xt_out"].sem, 1)
                            dv.wait_ge(S["attn"].sem, S["attn"].base + B.b + 1)
                            dv.wait_ge(S["xt_out"].sem, S["xt_out"].base + B.b + 1)
                            nc.vector.tensor_tensor(XA[:, B.u, :], ps[:, B.u, 2, :], XT[:, B.u, :], ALU.add).then_inc(S["xa"].sem, 1)
                        if A.ok:
                            dv.wait_ge(S["back"].sem, S["back"].base + A.b + 1)
                            nc.vector.tensor_tensor(RB[:, A.u], ps[:, A.u, 2, :].rearrange("p (t d) -> p t d", d=D), XS[:, A.u], ALU.add).then_inc(S["res"].sem, 1)
                            dv.wait_ge(S["res"].sem, S["res"].base + A.b + 1)
                            row_stats(A, RB, st, ag)
                            row_out(A, RB, ag, rt)
                    micros(dv, slot)
            S.advance(dict.fromkeys(("expert", "xs", "in_bn", "in_stats", "in_eps", "in_rstd", "xn", "turned", "xnt_out", "attn", "expert_out", "next", "xa",
                                     "next_out", "back", "xt_out", "res", "bn", "stats", "var_eps", "rstd", "out_rows"), NBATCH))
            S.advance(dict(hidden=FC * NBATCH, gelu=FC * NBATCH, w_in0=24 * NBATCH, w_in1=24 * NBATCH))
            mem.close()

        def channel_mix():
            mem = Memory(nc, "L3f")
            NSEQ = BATCH // SEQ
            XS = mem.sb("XS", [P, 2, TB, D])
            XP = mem.sb("XP", [P, 2, NSEQ, SEQ + 1])
            mu1 = mem.sb("mu1", [P, 2])
            T1, T2 = mem.sb("T1", [P, 2, BATCH]), mem.sb("T2", [P, 2, BATCH])
            XR, XK = mem.sb("XR", [P, 2, BATCH]), mem.sb("XK", [P, 2, BATCH])
            KA = mem.sb("KA", [P, 2, BATCH])
            RG, RB = mem.sb("RG", [P, 2, TB, D]), mem.sb("RB", [P, 2, TB, D])
            st, ag, rt = mem.sb("st", [P, 2, TB, 6]), mem.sb("ag", [P, 2, TB, 2]), mem.sb("rt", [P, 2, 2, TB])
            ps = mem.pb("ps", [P, 2, 4, BATCH])
            with nc.Block() as block:
                @block.vector
                def _(dv):
                    nc.vector.memset(XP[:, :, :, :], 0.0)
                    nc.vector.tensor_scalar(mu1[:, 0:1], C("mur"), -1.0, 1.0, ALU.mult, ALU.add)
                    nc.vector.tensor_scalar(mu1[:, 1:2], C("muk"), -1.0, 1.0, ALU.mult, ALU.add)
            seqs = lambda ap: ap.rearrange("p (s k) -> p s k", k=SEQ)
            with nc.Block() as block:
                @block.gpsimd
                def _(g):
                    def slot(B):
                        A = B - 1
                        if B.ok:
                            if after(B.b - 1):
                                g.wait_ge(S["out_rows"].sem, S["out_rows"].base + B.b - 1)
                            nc.gpsimd.tensor_copy(XS[:, B.u], X[:, B.rows, :]).then_inc(S["xs"].sem, 1)
                        if A.ok:
                            row_root(A, ag, rt)
                    micros(g, slot)

                @block.tensor
                def _(pe):
                    def slot(B):
                        A = B - 1
                        if B.ok:
                            pe.wait_ge(S["xs"].sem, S["xs"].base + B.b + 1)
                            for j in range(TB):
                                m = nc.tensor.transpose(ps[:, B.u, 0, j * P:(j + 1) * P], XS[:, B.u, j, :], ident)
                            m.then_inc(S["turned"].sem, 1)
                        if A.ok:
                            pe.wait_ge(S["ka"].sem, S["ka"].base + A.b + 1)
                            for j in range(TB):
                                m = nc.tensor.matmul(ps[:, A.u, 3, j * P:(j + 1) * P], KA[:, A.u, j * P:(j + 1) * P], Wm("L3fv"), start=True, stop=True)
                            m.then_inc(S["back"].sem, 1)
                        if B.ok:
                            pe.wait_ge(S["xk"].sem, S["xk"].base + B.b + 1)
                            nc.tensor.matmul(ps[:, B.u, 1, :], Wm("L3fk"), XK[:, B.u, :], start=True, stop=True).then_inc(S["hidden"].sem, 1)
                            pe.wait_ge(S["xr"].sem, S["xr"].base + B.b + 1)
                            for j in range(TB):
                                m = nc.tensor.matmul(ps[:, B.u, 2, j * P:(j + 1) * P], XR[:, B.u, j * P:(j + 1) * P], Wm("L3fr"), start=True, stop=True)
                            m.then_inc(S["attn"].sem, 1)
                    micros(pe, slot)

                @block.scalar
                def _(act):
                    def slot(B):
                        A = B - 1
                        if B.ok:
                            act.wait_ge(S["turned"].sem, S["turned"].base + B.b + 1)
                            nc.scalar.activation(XP[:, B.u, :, 1:SEQ + 1], seqs(ps[:, B.u, 0, :]), ACT.Copy).then_inc(S["xt_out"].sem, 1)
                            act.wait_ge(S["xt_out"].sem, S["xt_out"].base + B.b + 1)
                            nc.scalar.activation(seqs(T1[:, B.u, :]), XP[:, B.u, :, 0:SEQ], ACT.Copy, scale=mu1[:, 1:2])
                            nc.scalar.activation(seqs(T2[:, B.u, :]), XP[:, B.u, :, 0:SEQ], ACT.Copy, scale=mu1[:, 0:1]).then_inc(S["prev"].sem, 1)
                            act.wait_ge(S["attn"].sem, S["attn"].base + B.b + 1)
                            nc.scalar.activation(RG[:, B.u].rearrange(FLAT), ps[:, B.u, 2, :], ACT.Sigmoid).then_inc(S["gelu"].sem, 1)
                    micros(act, slot)

                @block.vector
                def _(dv):
                    def slot(B):
                        A = B - 1
                        if B.ok:
                            dv.wait_ge(S["prev"].sem, S["prev"].base + B.b + 1)
                            nc.vector.scalar_tensor_tensor(seqs(XK[:, B.u, :]), XP[:, B.u, :, 1:SEQ + 1], C("muk"), seqs(T1[:, B.u, :]), ALU.mult, ALU.add).then_inc(S["xk"].sem, 1)
                            nc.vector.scalar_tensor_tensor(seqs(XR[:, B.u, :]), XP[:, B.u, :, 1:SEQ + 1], C("mur"), seqs(T2[:, B.u, :]), ALU.mult, ALU.add).then_inc(S["xr"].sem, 1)
                        if A.ok:
                            dv.wait_ge(S["back"].sem, S["back"].base + A.b + 1)
                            dv.wait_ge(S["gelu"].sem, S["gelu"].base + A.b + 1)
                            nc.vector.tensor_tensor(RB[:, A.u].rearrange(FLAT), ps[:, A.u, 3, :], RG[:, A.u].rearrange(FLAT), ALU.mult).then_inc(S["next"].sem, 1)
                        if B.ok:
                            dv.wait_ge(S["hidden"].sem, S["hidden"].base + B.b + 1)
                            nc.vector.tensor_scalar(T1[:, B.u, :], ps[:, B.u, 1, :], 0.0, None, ALU.max).then_inc(S["next_out"].sem, 1)
                            dv.wait_ge(S["next_out"].sem, S["next_out"].base + B.b + 1)
                            nc.vector.tensor_tensor(KA[:, B.u, :], T1[:, B.u, :], T1[:, B.u, :], ALU.mult).then_inc(S["ka"].sem, 1)
                        if A.ok:
                            dv.wait_ge(S["next"].sem, S["next"].base + A.b + 1)
                            nc.vector.tensor_tensor(RB[:, A.u], RB[:, A.u], XS[:, A.u], ALU.add).then_inc(S["res"].sem, 1)
                            dv.wait_ge(S["res"].sem, S["res"].base + A.b + 1)
                            row_stats(A, RB, st, ag)
                            row_out(A, RB, ag, rt)
                    micros(dv, slot)
            S.advance(dict.fromkeys(("xs", "turned", "attn", "hidden", "gelu", "next", "next_out", "ka", "xr", "xk", "prev", "back", "xt_out", "res",
                                     "bn", "stats", "var_eps", "rstd", "out_rows"), NBATCH))
            mem.close()

        def recurrent_block():
            FC, CK = 4, 4
            NSEQ = BATCH // SEQ
            RMS3_EPS = 1e-6
            mem = Memory(nc, "L3a")
            WG, WU, WD = mem.sb("WG", [P, FC * D]), mem.sb("WU", [P, FC * D]), mem.sb("WD", [P, FC, D])
            decay, dtmp = mem.sb("decay", [P, 1]), mem.sb("dtmp", [P, 4])
            eps3, nw = mem.sb("eps3", [P, TB]), mem.sb("nw", [P, 2])
            SQR = mem.sb("SQR", [P, 2, TB, D])
            ms, ms2 = mem.sb("ms", [P, 2, 2, TB]), mem.sb("ms2", [P, 2, 2, TB])
            XN, XT = mem.sb("XN", [P, 2, TB, D]), mem.sb("XT", [P, 2, BATCH])
            XP = mem.sb("XP", [P, 2, NSEQ, SEQ + CK - 1])
            YB, XC, RG, IG = (mem.sb(n, [P, 2, BATCH]) for n in ("YB", "XC", "RG", "IG"))
            A1, A2, HS = mem.sb("A1", [P, 2, BATCH]), mem.sb("A2", [P, 2, BATCH]), mem.sb("HS", [P, 2, BATCH])
            H1 = mem.sb("H1", [P, 2, TB, D])
            GG, G2 = mem.sb("GG", [P, 2, BATCH]), mem.sb("G2", [P, FC, BATCH])
            RB = mem.sb("RB", [P, 2, TB, D])
            st, ag, rt = mem.sb("st", [P, 2, TB, 6]), mem.sb("ag", [P, 2, TB, 2]), mem.sb("rt", [P, 2, 2, TB])
            ps = mem.pb("ps", [P, 2, 4, BATCH])
            seqs = lambda ap: ap.rearrange("p (s k) -> p s k", k=SEQ)
            flat = lambda ap: ap.rearrange("p t k -> p (t k)")

            with nc.Block() as block:
                @block.sync
                def _(sp):
                    for d, s_ in ((WG[:, :], io["wg"]), (WU[:, :], io["wu"]), (WD[:, :, :], io["wd"])):
                        sp.dma_start(d, s_).then_inc(S["weights_in"].sem, 16)
                    sp.wait_ge(S["weights_in"].sem, S["weights_in"].base + 48)

                @block.vector
                def _(dv):
                    nc.vector.memset(XP[:, :, :, :], 0.0)
                    nc.vector.memset(eps3[:, :], D * RMS3_EPS)
                    nc.vector.tensor_scalar(nw[:, 0:1], C("n1"), float(np.sqrt(D)), None, ALU.mult)
                    nc.vector.tensor_scalar(nw[:, 1:2], C("n2"), float(np.sqrt(D)), None, ALU.mult)
                    nc.vector.tensor_scalar(dtmp[:, 0:1], C("lam"), -1.0, None, ALU.mult).then_inc(S["prep"].sem, 1)
                    nc.vector.tensor_scalar(dtmp[:, 3:4], C("lam"), 0.0, None, ALU.max)
                    dv.wait_ge(S["prep"].sem, S["prep"].base + 1)
                    nc.vector.tensor_tensor(dtmp[:, 1:2], dtmp[:, 0:1], C("lam"), ALU.min).then_inc(S["prep"].sem, 1)
                    dv.wait_ge(S["prep_act"].sem, S["prep_act"].base + 1)
                    nc.vector.tensor_tensor(dtmp[:, 3:4], dtmp[:, 3:4], dtmp[:, 2:3], ALU.add).then_inc(S["prep"].sem, 1)
                    dv.wait_ge(S["prep"].sem, S["prep"].base + 3)
                    nc.vector.tensor_scalar(decay[:, :], dtmp[:, 3:4], -8.0, None, ALU.mult)

                @block.scalar
                def _(act):
                    act.wait_ge(S["prep"].sem, S["prep"].base + 2)
                    nc.scalar.activation(dtmp[:, 2:3], dtmp[:, 1:2], ACT.Exp).then_inc(S["prep_exp"].sem, 1)
                    act.wait_ge(S["prep_exp"].sem, S["prep_exp"].base + 1)
                    nc.scalar.activation(dtmp[:, 2:3], dtmp[:, 2:3], ACT.Ln, bias=1.0).then_inc(S["prep_act"].sem, 1)
            S.advance(dict(weights_in=48, prep=3, prep_exp=1, prep_act=1))

            with nc.Block() as block:
                @block.gpsimd
                def _(g):
                    def root(B, ms_, means, eps, done):
                        g.wait_ge(means.sem, means.base + B.b + 1)
                        nc.gpsimd.tensor_tensor(ms_[:, B.u, 1, :], ms_[:, B.u, 0, :], eps3[:, :], ALU.add).then_inc(eps.sem, 1)
                        g.wait_ge(eps.sem, eps.base + B.b + 1)
                        nc.gpsimd.tensor_tensor(ms_[:, B.u, 0, :], ms_[:, B.u, 1, :], half[:, 0:TB], ALU.pow).then_inc(done.sem, 1)

                    def slot(B):
                        A = B - 1
                        if B.ok:
                            if after(B.b - 1):
                                g.wait_ge(S["out_rows"].sem, S["out_rows"].base + B.b - 1)
                            pace(g, S)
                            nc.gpsimd.tensor_tensor(SQR[:, B.u], X[:, B.rows, :], X[:, B.rows, :], ALU.mult).then_inc(S["squares"].sem, 1)
                            root(B, ms, S["means"], S["in_eps"], S["in_rstd"])
                        if A.ok:
                            g.wait_ge(S["h1"].sem, S["h1"].base + A.b + 1)
                            nc.gpsimd.tensor_tensor(SQR[:, A.u], H1[:, A.u], H1[:, A.u], ALU.mult).then_inc(S["squares2"].sem, 1)
                            root(A, ms2, S["means2"], S["h_eps"], S["h_rstd"])
                            g.wait_ge(S["un"].sem, S["un"].base + A.b + 1)
                            pace(g, S)
                            nc.gpsimd.tensor_tensor(H1[:, A.u], H1[:, A.u], X[:, A.rows, :], ALU.add).then_inc(S["h1_x"].sem, 1)
                        if B.ok:
                            g.wait_ge(S["gates_out"].sem, S["gates_out"].base + B.b + 1)
                            nc.gpsimd.tensor_tensor(IG[:, B.u, :], IG[:, B.u, :], XC[:, B.u, :], ALU.mult).then_inc(S["ix"].sem, 1)
                        if A.ok:
                            row_root(A, ag, rt)
                    micros(g, slot)

                @block.tensor
                def _(pe):
                    def turn(B, bank, src, ready, done):
                        pe.wait_ge(ready.sem, ready.base + B.b + 1)
                        for j in range(TB):
                            m = nc.tensor.transpose(ps[:, B.u, bank, j * P:(j + 1) * P], src[:, B.u, j, :], ident)
                        m.then_inc(done.sem, 1)

                    def hidden(A, c):
                        b1, b2 = ((3, 0), (1, 2))[c % 2]
                        if after(FC * A.b + c - 1 if c > 1 else 0):
                            pe.wait_ge(S["gg"].sem, S["gg"].base + (FC * A.b + c - 1 if c > 1 else 0))
                        if c == 0:
                            pe.wait_ge(S["u_out"].sem, S["u_out"].base + A.b + 1)
                        nc.tensor.matmul(ps[:, A.u, b1, :], WG[:, c * D:(c + 1) * D], XT[:, A.u, :], start=True, stop=True)
                        nc.tensor.matmul(ps[:, A.u, b2, :], WU[:, c * D:(c + 1) * D], XT[:, A.u, :], start=True, stop=True).then_inc(S["hidden"].sem, 1)

                    def slot(B):
                        A = B - 1
                        if B.ok:
                            turn(B, 0, XN, S["xn"], S["turned"])
                        if A.ok:
                            pe.wait_ge(S["hy"].sem, S["hy"].base + A.b + 1)
                            for j in range(TB):
                                m = nc.tensor.matmul(ps[:, A.u, 1, j * P:(j + 1) * P], HS[:, A.u, j * P:(j + 1) * P], Wm("L3Wo"), start=True, stop=True)
                            m.then_inc(S["mix"].sem, 1)
                        if B.ok:
                            pe.wait_ge(S["xt_out"].sem, S["xt_out"].base + B.b + 1)
                            nc.tensor.matmul(ps[:, B.u, 1, :], Wm("L3Wx"), XT[:, B.u, :], start=True, stop=True).then_inc(S["xb"].sem, 1)
                            nc.tensor.matmul(ps[:, B.u, 2, :], Wm("L3Wy"), XT[:, B.u, :], start=True, stop=True).then_inc(S["yb"].sem, 1)
                        if A.ok:
                            turn(A, 2, RB, S["un"], S["turned2"])
                            hidden(A, 0)
                            hidden(A, 1)
                        if B.ok:
                            pe.wait_ge(S["conv"].sem, S["conv"].base + 5 * (B.b + 1))
                            nc.tensor.matmul(ps[:, B.u, 3, :], Wm("L3Wa"), XC[:, B.u, :], start=True, stop=True)
                            nc.tensor.matmul(ps[:, B.u, 0, :], Wm("L3Wi"), XC[:, B.u, :], start=True, stop=True).then_inc(S["gates"].sem, 1)
                        if A.ok:
                            hidden(A, 2)
                            hidden(A, 3)
                            pe.wait_ge(S["gg"].sem, S["gg"].base + FC * (A.b + 1))
                            for j in range(TB):
                                for c in range(FC):
                                    m = nc.tensor.matmul(ps[:, A.u, 3, j * P:(j + 1) * P], G2[:, c, j * P:(j + 1) * P], WD[:, c, :], start=c == 0, stop=c == FC - 1)
                            m.then_inc(S["back"].sem, 1)
                    micros(pe, slot)

                @block.scalar
                def _(act):
                    def gelu(A, c):
                        act.wait_ge(S["hidden"].sem, S["hidden"].base + FC * A.b + c + 1)
                        if after(FC * A.b + c - 1):
                            act.wait_ge(S["gg"].sem, S["gg"].base + FC * A.b + c - 1)
                        nc.scalar.activation(GG[:, c % 2, :], ps[:, A.u, (3, 1)[c % 2], :], ACT.Gelu_apprx_tanh).then_inc(S["gelu"].sem, 1)

                    def slot(B):
                        A = B - 1
                        if B.ok:
                            act.wait_ge(S["turned"].sem, S["turned"].base + B.b + 1)
                            nc.scalar.activation(XT[:, B.u, :], ps[:, B.u, 0, :], ACT.Copy, scale=nw[:, 0:1]).then_inc(S["xt_out"].sem, 1)
                            act.wait_ge(S["yb"].sem, S["yb"].base + B.b + 1)
                            nc.scalar.activation(YB[:, B.u, :], ps[:, B.u, 2, :], ACT.Gelu_apprx_tanh).then_inc(S["yb_out"].sem, 1)
                        if A.ok:
                            act.wait_ge(S["turned2"].sem, S["turned2"].base + A.b + 1)
                            nc.scalar.activation(XT[:, A.u, :], ps[:, A.u, 2, :], ACT.Copy, scale=nw[:, 1:2]).then_inc(S["u_out"].sem, 1)
                            for c in range(FC):
                                gelu(A, c)
                        if B.ok:
                            act.wait_ge(S["gates"].sem, S["gates"].base + B.b + 1)
                            nc.scalar.activation(RG[:, B.u, :], ps[:, B.u, 3, :], ACT.Sigmoid)
                            nc.scalar.activation(IG[:, B.u, :], ps[:, B.u, 0, :], ACT.Sigmoid).then_inc(S["gates_out"].sem, 1)
                            act.wait_ge(S["gates_out"].sem, S["gates_out"].base + B.b + 1)
                            nc.scalar.activation(A1[:, B.u, :], RG[:, B.u, :], ACT.Exp, scale=decay[:, 0:1]).then_inc(S["a_out"].sem, 1)
                            act.wait_ge(S["floored"].sem, S["floored"].base + B.b + 1)
                            nc.scalar.activation(A2[:, B.u, :], A2[:, B.u, :], ACT.Sqrt).then_inc(S["m_root"].sem, 1)
                    micros(act, slot)

                @block.vector
                def _(dv):
                    def mean_square(B, squares, ms_, done):
                        dv.wait_ge(squares.sem, squares.base + B.b + 1)
                        nc.vector.tensor_reduce(ms_[:, B.u, 0, :], SQR[:, B.u], AX, ALU.add).then_inc(done.sem, 1)

                    def scaled(B, dst, src, ms_, ready, done):
                        dv.wait_ge(ready.sem, ready.base + B.b + 1)
                        nc.vector.tensor_tensor(dst[:, B.u], src, ms_[:, B.u, 0, :].unsqueeze(2).to_broadcast([P, TB, D]), ALU.mult).then_inc(done.sem, 1)

                    def gated(A, c):
                        dv.wait_ge(S["gelu"].sem, S["gelu"].base + FC * A.b + c + 1)
                        if c == 0:
                            if after(A.b):
                                dv.wait_ge(S["back"].sem, S["back"].base + A.b)
                        nc.vector.tensor_tensor(G2[:, c, :], GG[:, c % 2, :], ps[:, A.u, (0, 2)[c % 2], :], ALU.mult).then_inc(S["gg"].sem, 1)

                    def slot(B):
                        A = B - 1
                        if B.ok:
                            if after(B.b - 1):
                                dv.wait_ge(S["out_rows"].sem, S["out_rows"].base + B.b - 1)
                            mean_square(B, S["squares"], ms, S["means"])
                            scaled(B, XN, X[:, B.rows, :], ms, S["in_rstd"], S["xn"])
                        if A.ok:
                            dv.wait_ge(S["mix"].sem, S["mix"].base + A.b + 1)
                            nc.vector.tensor_tensor(H1[:, A.u], ps[:, A.u, 1, :].rearrange("p (t d) -> p t d", d=D), X[:, A.rows, :], ALU.add).then_inc(S["h1"].sem, 1)
                        if B.ok:
                            dv.wait_ge(S["xb"].sem, S["xb"].base + B.b + 1)
                            nc.vector.tensor_copy(XP[:, B.u, :, CK - 1:], seqs(ps[:, B.u, 1, :])).then_inc(S["conv"].sem, 1)
                        if A.ok:
                            mean_square(A, S["squares2"], ms2, S["means2"])
                        if B.ok:
                            xc = seqs(XC[:, B.u, :])
                            dv.wait_ge(S["conv"].sem, S["conv"].base + 5 * B.b + 1)
                            nc.vector.tensor_scalar(xc, XP[:, B.u, :, 0:SEQ], C("c0"), C("cb"), ALU.mult, ALU.add).then_inc(S["conv"].sem, 1)
                        if A.ok:
                            dv.wait_ge(S["h1"].sem, S["h1"].base + A.b + 1)
                            scaled(A, RB, H1[:, A.u], ms2, S["h_rstd"], S["un"])
                        if B.ok:
                            for k in range(1, CK):
                                dv.wait_ge(S["conv"].sem, S["conv"].base + 5 * B.b + 1 + k)
                                nc.vector.scalar_tensor_tensor(xc, XP[:, B.u, :, k:k + SEQ], C(f"c{k}"), xc, ALU.mult, ALU.add).then_inc(S["conv"].sem, 1)
                        if A.ok:
                            for c in range(FC):
                                gated(A, c)
                        if B.ok:
                            dv.wait_ge(S["a_out"].sem, S["a_out"].base + B.b + 1)
                            nc.vector.tensor_tensor(A2[:, B.u, :], A1[:, B.u, :], A1[:, B.u, :], ALU.mult).then_inc(S["a_squared"].sem, 1)
                            dv.wait_ge(S["a_squared"].sem, S["a_squared"].base + B.b + 1)
                            nc.vector.tensor_scalar(A2[:, B.u, :], A2[:, B.u, :], -1.0, 1.0, ALU.mult, ALU.add).then_inc(S["one_less"].sem, 1)
                            nc.vector.memset(seqs(A1[:, B.u, :])[:, :, 0:1], 0.0).then_inc(S["cut"].sem, 1)
                            dv.wait_ge(S["one_less"].sem, S["one_less"].base + B.b + 1)
                            nc.vector.tensor_scalar(A2[:, B.u, :], A2[:, B.u, :], 1e-12, None, ALU.max).then_inc(S["floored"].sem, 1)
                        if A.ok:
                            dv.wait_ge(S["back"].sem, S["back"].base + A.b + 1)
                            dv.wait_ge(S["h1_x"].sem, S["h1_x"].base + A.b + 1)
                            nc.vector.tensor_tensor(RB[:, A.u], ps[:, A.u, 3, :].rearrange("p (t d) -> p t d", d=D), H1[:, A.u], ALU.add).then_inc(S["res"].sem, 1)
                            dv.wait_ge(S["res"].sem, S["res"].base + A.b + 1)
                            row_stats(A, RB, st, ag)
                        if B.ok:
                            dv.wait_ge(S["m_root"].sem, S["m_root"].base + B.b + 1)
                            dv.wait_ge(S["ix"].sem, S["ix"].base + B.b + 1)
                            nc.vector.tensor_tensor(A2[:, B.u, :], A2[:, B.u, :], IG[:, B.u, :], ALU.mult).then_inc(S["b_out"].sem, 1)
                            dv.wait_ge(S["b_out"].sem, S["b_out"].base + B.b + 1)
                            dv.wait_ge(S["cut"].sem, S["cut"].base + B.b + 1)
                            nc.vector.tensor_tensor_scan(HS[:, B.u, :], A1[:, B.u, :], A2[:, B.u, :], 0.0, ALU.mult, ALU.add).then_inc(S["scanned"].sem, 1)
                            dv.wait_ge(S["scanned"].sem, S["scanned"].base + B.b + 1)
                            dv.wait_ge(S["yb_out"].sem, S["yb_out"].base + B.b + 1)
                            nc.vector.tensor_tensor(HS[:, B.u, :], HS[:, B.u, :], YB[:, B.u, :], ALU.mult).then_inc(S["hy"].sem, 1)
                        if A.ok:
                            row_out(A, RB, ag, rt)
                    micros(dv, slot)
            S.advance(dict.fromkeys(("squares", "squares2", "means", "means2", "in_eps", "in_rstd", "h_eps", "h_rstd", "un", "h1_x", "gates_out", "ix", "xn", "turned",
                                     "hy", "mix", "xt_out", "xb", "yb", "turned2", "u_out", "gates", "back", "yb_out", "a_out", "floored", "m_root", "h1",
                                     "a_squared", "one_less", "cut", "res", "b_out", "scanned", "bn", "stats", "var_eps", "rstd", "out_rows"), NBATCH))
            S.advance(dict(conv=5 * NBATCH, hidden=FC * NBATCH, gelu=FC * NBATCH, gg=FC * NBATCH))
            mem.close()

        def grouped_attention():
            QC = HEADS // 2
            mem = Memory(nc, "L1a")
            WQ, WK, WV = mem.sb("WQ", [P, QC, P]), mem.sb("WK", [P, KVH, 2, GD]), mem.sb("WV", [P, KVH * GD])
            WO = mem.sb("WO", [P, QC, D])
            XS, XT = mem.sb("XS", [P, 2, 2, D]), mem.sb("XT", [P, 2, 2 * P])
            QT = mem.sb("QT", [P, 2, QC, 2 * P])
            KB = mem.sb("KB", [P, 2, 4, KVH, 2, SEQ])
            VB = mem.sb("VB", [P, 2, 4, KVH, 2, GD])
            PR, PT = mem.sb("PR", [P, 2, HEADS, SEQ]), mem.sb("PT", [P, QC, P])
            mx, rden = mem.sb("mx", [P, 2, HEADS]), mem.sb("rden", [P, 2, 2, HEADS])
            ON, OT = mem.sb("ON", [P, QC, P]), mem.sb("OT", [P, QC, P])
            RB, st, ag, rs = mem.sb("RB", [P, 2, D]), mem.sb("st", [P, 2, 6]), mem.sb("ag", [P, 2, 2]), mem.sb("rs", [P, 2, 2])
            psF, psS = mem.pb("psF", [P, 2, 512]), mem.pb("psS", [P, 2, 8, SEQ])
            psP, psO = mem.pb("psP", [P, 2, 4, P]), mem.pb("psO", [P, 2, 4, P])
            psJ = psO[:, 0, 0, :]
            scale = GD ** -0.5

            FILLS = [("x", 0), ("k", 0), ("k", 1), ("q", 0), ("q", 1), ("q", 2), ("q", 3), ("v", 0), ("v", 1)]
            NFILL = len(FILLS)
            by_act = [1, 1, 1, 0, 1, 0, 1, 1, 1]
            by_dve = [0, 1, 1, 1, 0, 1, 0, 1, 1]
            NA, ND = sum(by_act), sum(by_dve)
            PLACES = (((0,), (1, 2), (3, 4)), ((5,), (6, 7), (8,)))

            def copied(eng, p, n, also=None):
                q, k = (p, n) if n >= 0 else (p - 1, n + NFILL)
                if also is not None and n < also:
                    eng.wait_ge(S["out_a"].sem, S["out_a"].base + p * NA + sum(by_act[:also + 1]))
                else:
                    if after(q * NA + sum(by_act[:k + 1])):
                        eng.wait_ge(S["out_a"].sem, S["out_a"].base + q * NA + sum(by_act[:k + 1]))
                if after(q * ND + sum(by_dve[:k + 1])):
                    eng.wait_ge(S["out_d"].sem, S["out_d"].base + q * ND + sum(by_dve[:k + 1]))

            with nc.Block() as block:
                @block.sync
                def _(sp):
                    for d, s_ in ((WQ[:, :, :], io["wq"]), (WK[:, :, :, :], io["wk"]), (WV[:, :], io["wv"]), (WO[:, :, :], io["wo"])):
                        sp.dma_start(d, s_).then_inc(S["weights_in"].sem, 16)
                    sp.wait_ge(S["weights_in"].sem, S["weights_in"].base + 64)

                @block.vector
                def _(dv):
                    nc.vector.memset(KB[:, :, :, :, :, :], 0.0)

                @block.gpsimd
                def _(g):
                    nc.gpsimd.memset(VB[:, :, :, :, :, :], 0.0)
            S.advance(dict(weights_in=64))

            def copy_out(eng, N, n):
                kind, k = FILLS[n]
                act = eng is nc.scalar
                bank = psF[:, (N.u + n) % 2, :]
                eng.wait_ge(S["front"].sem, S["front"].base + N.p * NFILL + n + 1)
                half_ = slice(0, 64) if act else slice(64, 128)
                h = 0 if act else 1
                if kind == "x":
                    dst, src = XT[:, N.u, :], bank[:, 0:256]
                elif kind == "q":
                    if after(2 * N.p - 2):
                        eng.wait_ge(S["scores"].sem, S["scores"].base + 2 * N.p - 2)
                    dst, src = QT[:, N.u, 2 * k:2 * k + 2, :].rearrange("p c t -> p (c t)"), bank
                elif kind == "k":
                    if after(2 * N.p - 2):
                        eng.wait_ge(S["scores"].sem, S["scores"].base + 2 * N.p - 2)
                    dst = KB[half_, N.u, :, 2 * k:2 * k + 2, h, :]
                    src = bank[half_, :].rearrange("p (j s k) -> p s j k", j=2, k=SEQ)
                else:
                    if after(2 * N.p - 2):
                        eng.wait_ge(S["pv"].sem, S["pv"].base + 2 * N.p - 2)
                    dst = VB[half_, N.u, 2 * k:2 * k + 2, :, h, :]
                    src = bank[half_, :].rearrange("p (s j k) -> p s j k", s=2, k=GD)
                if act:
                    nc.scalar.activation(dst, src, ACT.Copy).then_inc(S["out_a"].sem, 1)
                else:
                    nc.vector.tensor_copy(dst, src).then_inc(S["out_d"].sem, 1)

            def copies(eng, T, place):
                N = T + 2 if T.par == 0 else T + 1
                if N.ok:
                    for n in PLACES[T.par][place]:
                        if (by_act if eng is nc.scalar else by_dve)[n]:
                            copy_out(eng, N, n)

            with nc.Block() as block:
                @block.gpsimd
                def _(g):
                    def slot(T):
                        N, A = T + 2, T - 1
                        if T.par == 0 and N.ok:
                            if after((N.p - 2) * NFILL + 1):
                                g.wait_ge(S["front"].sem, S["front"].base + (N.p - 2) * NFILL + 1)
                            nc.gpsimd.tensor_copy(XS[:, N.u], X[:, bass.ds(N.t, 2), :]).then_inc(S["xs"].sem, 1)
                        if A.ok:
                            g.wait_ge(S["stats"].sem, S["stats"].base + A.t + 1)
                            if after(A.t - 1):
                                g.wait_ge(S["out_rows"].sem, S["out_rows"].base + A.t - 1)
                            nc.gpsimd.tensor_tensor(rs[:, A.par, 0:1], ag[:, A.par, 1:2], eps[:, 0:1], ALU.add).then_inc(S["var_eps"].sem, 1)
                            g.wait_ge(S["var_eps"].sem, S["var_eps"].base + A.t + 1)
                            nc.gpsimd.tensor_tensor(rs[:, A.par, 1:2], rs[:, A.par, 0:1], half[:, 0:1], ALU.pow).then_inc(S["rstd"].sem, 1)
                    pipeline(g, slot, 2)

                @block.tensor
                def _(pe):
                    def fill(N, n):
                        kind, k = FILLS[n]
                        bank = psF[:, (N.u + n) % 2, :]
                        copied(pe, N.p, n - 2, 0 if n else None)
                        if kind == "x":
                            pe.wait_ge(S["xs"].sem, S["xs"].base + N.p + 1)
                            for a in range(2):
                                m = nc.tensor.transpose(bank[:, a * P:a * P + P], XS[:, N.u, a, :], ident)
                        if kind == "k":
                            for j in range(2):
                                m = nc.tensor.matmul(bank[:, 256 * j:256 * j + 256], WK[:, 2 * k + j, :, :].rearrange("p h d -> p (h d)"), XT[:, N.u, :], start=True, stop=True)
                        if kind == "q":
                            for j in range(2):
                                m = nc.tensor.matmul(bank[:, 256 * j:256 * j + 256], WQ[:, 2 * k + j, :], XT[:, N.u, :], start=True, stop=True)
                        if kind == "v":
                            for s in range(2):
                                for a in range(2):
                                    q4 = 2 * k + s
                                    m = nc.tensor.matmul(bank[64 * a:64 * a + 64, 256 * s:256 * s + 256], XT[:, N.u, q4 * SEQ:(q4 + 1) * SEQ], WV[:, :], start=True, stop=True)
                        m.then_inc(S["front"].sem, 1)

                    def fills(T, place):
                        N = T + 2 if T.par == 0 else T + 1
                        if N.ok:
                            for n in PLACES[T.par][place]:
                                fill(N, n)

                    def slot(T):
                        A = T - 1
                        if A.ok:
                            pe.wait_ge(S["probs"].sem, S["probs"].base + A.t + 1)
                            for hb, free, done in ((0, S["ot_a"], S["turned_a"]), (1, S["ot_b"], S["turned_b"])):
                                if after(A.t):
                                    pe.wait_ge(free.sem, free.base + A.t)
                                for j in range(4):
                                    b = hb * 4 + j
                                    m = nc.tensor.transpose(psP[:, hb, j, :], PR[:, A.par, 2 * b:2 * b + 2, :].rearrange("p h k -> p (h k)"), ident)
                                m.then_inc(done.sem, 1)
                        if T.ok:
                            copied(pe, T.p, NFILL - 1)
                            if after(T.t):
                                pe.wait_ge(S["shifted"].sem, S["shifted"].base + T.t)
                            for hh in range(2):
                                nc.tensor.matmul(psS[:, hh], idb[:, :], causal[:, :].unsqueeze(1).to_broadcast([P, 8, SEQ]), start=True, stop=False, skip_group_check=True)
                            for c in range(QC):
                                for s in range(2):
                                    q4 = 2 * T.par + s
                                    m = nc.tensor.matmul(psS[64 * s:64 * s + 64, c // 4, 2 * (c % 4):2 * (c % 4) + 2, :], QT[:, T.u, c, q4 * SEQ:(q4 + 1) * SEQ],
                                                         KB[:, T.u, q4, c // 2, :, :], start=False, stop=True, skip_group_check=True)
                            m.then_inc(S["scores"].sem, 1)
                        fills(T, 0)
                        if A.ok:
                            pe.wait_ge(S["pt_a"].sem, S["pt_a"].base + A.t + 1)
                            pe.wait_ge(S["pt_b"].sem, S["pt_b"].base + A.t + 1)
                            if after(A.t):
                                pe.wait_ge(S["res"].sem, S["res"].base + A.t)
                            for c in range(QC):
                                for s in range(2):
                                    m = nc.tensor.matmul(psO[64 * s:64 * s + 64, c // 4, c % 4, :], PT[:, c, 64 * s:64 * s + 64],
                                                         VB[:, A.u, 2 * A.par + s, c // 2, :, :], start=True, stop=True)
                            m.then_inc(S["pv"].sem, 1)
                        fills(T, 1)
                        if A.ok:
                            pe.wait_ge(S["normed"].sem, S["normed"].base + A.t + 1)
                            for hb, done in ((0, S["o_turned_a"]), (1, S["o_turned_b"])):
                                for j in range(4):
                                    m = nc.tensor.transpose(psP[:, hb, j, :], ON[:, 4 * hb + j, :], ident)
                                m.then_inc(done.sem, 1)
                        fills(T, 2)
                        if A.ok:
                            pe.wait_ge(S["ot_a"].sem, S["ot_a"].base + A.t + 1)
                            pe.wait_ge(S["ot_b"].sem, S["ot_b"].base + A.t + 1)
                            for c in range(QC):
                                m = nc.tensor.matmul(psJ, OT[:, c, :], WO[:, c, :], start=c == 0, stop=c == QC - 1)
                            m.then_inc(S["proj"].sem, 1)
                    pipeline(pe, slot, 2)

                @block.scalar
                def _(act):
                    def slot(T):
                        A = T - 1
                        if A.ok:
                            act.wait_ge(S["turned_a"].sem, S["turned_a"].base + A.t + 1)
                            if after(A.t):
                                act.wait_ge(S["pv"].sem, S["pv"].base + A.t)
                            nc.scalar.activation(PT[:, 0:4, :], psP[:, 0], ACT.Copy).then_inc(S["pt_a"].sem, 1)
                        copies(act, T, 0)
                        if T.ok:
                            act.wait_ge(S["shifted"].sem, S["shifted"].base + T.t + 1)
                            nc.scalar.activation(PR[:, T.par], PR[:, T.par], ACT.Exp, scale=scale).then_inc(S["probs"].sem, 1)
                        copies(act, T, 1)
                        if A.ok:
                            act.wait_ge(S["o_turned_a"].sem, S["o_turned_a"].base + A.t + 1)
                            if after(A.t):
                                act.wait_ge(S["proj"].sem, S["proj"].base + A.t)
                            nc.scalar.activation(OT[:, 0:4, :], psP[:, 0], ACT.Copy).then_inc(S["ot_a"].sem, 1)
                        copies(act, T, 2)
                    pipeline(act, slot, 2)

                @block.vector
                def _(dv):
                    def slot(T):
                        A, E = T - 1, T - 2
                        if A.ok:
                            dv.wait_ge(S["turned_b"].sem, S["turned_b"].base + A.t + 1)
                            if after(A.t):
                                dv.wait_ge(S["pv"].sem, S["pv"].base + A.t)
                            nc.vector.tensor_copy(PT[:, 4:8, :], psP[:, 1]).then_inc(S["pt_b"].sem, 1)
                        if T.ok:
                            sc = psS[:, :, :, :].rearrange("p b h k -> p (b h) k")
                            dv.wait_ge(S["scores"].sem, S["scores"].base + T.t + 1)
                            nc.vector.tensor_reduce(mx[:, T.par, :], sc, AX, ALU.max).then_inc(S["maxed"].sem, 1)
                            dv.wait_ge(S["maxed"].sem, S["maxed"].base + T.t + 1)
                            if after(T.t - 1):
                                dv.wait_ge(S["turned_b"].sem, S["turned_b"].base + T.t - 1)
                            nc.vector.tensor_tensor(PR[:, T.par], sc, mx[:, T.par, :].unsqueeze(2).to_broadcast([P, HEADS, SEQ]), ALU.subtract).then_inc(S["shifted"].sem, 1)
                        copies(dv, T, 0)
                        if A.ok:
                            dv.wait_ge(S["pv"].sem, S["pv"].base + A.t + 1)
                            dv.wait_ge(S["recip"].sem, S["recip"].base + A.t + 1)
                            if after(A.t):
                                dv.wait_ge(S["o_turned_b"].sem, S["o_turned_b"].base + A.t)
                            nc.vector.tensor_tensor(ON[:, :, :].rearrange("p c (h d) -> p (c h) d", d=GD), psO[:, :, :, :].rearrange("p b c (h d) -> p (b c h) d", d=GD),
                                                    rden[:, A.par, 1, :].unsqueeze(2).to_broadcast([P, HEADS, GD]), ALU.mult).then_inc(S["normed"].sem, 1)
                        copies(dv, T, 1)
                        if A.ok:
                            dv.wait_ge(S["o_turned_b"].sem, S["o_turned_b"].base + A.t + 1)
                            if after(A.t):
                                dv.wait_ge(S["proj"].sem, S["proj"].base + A.t)
                            nc.vector.tensor_copy(OT[:, 4:8, :], psP[:, 1]).then_inc(S["ot_b"].sem, 1)
                        copies(dv, T, 2)
                        if T.ok:
                            dv.wait_ge(S["probs"].sem, S["probs"].base + T.t + 1)
                            if after(T.t - 1):
                                dv.wait_ge(S["normed"].sem, S["normed"].base + T.t - 1)
                            nc.vector.tensor_reduce(rden[:, T.par, 0, :], PR[:, T.par], AX, ALU.add).then_inc(S["summed"].sem, 1)
                            dv.wait_ge(S["summed"].sem, S["summed"].base + T.t + 1)
                            nc.vector.reciprocal(rden[:, T.par, 1, :], rden[:, T.par, 0, :]).then_inc(S["recip"].sem, 1)
                        if E.ok:
                            dv.wait_ge(S["rstd"].sem, S["rstd"].base + E.t + 1)
                            nc.vector.tensor_scalar(X[:, bass.ds(E.t, 1), :].rearrange("p a d -> p (a d)"), RB[:, E.par, :],
                                                    ag[:, E.par, 0:1], rs[:, E.par, 1:2], ALU.subtract, ALU.mult).then_inc(S["out_rows"].sem, 1)
                        if A.ok:
                            dv.wait_ge(S["proj"].sem, S["proj"].base + A.t + 1)
                            if after(A.t - 1):
                                dv.wait_ge(S["out_rows"].sem, S["out_rows"].base + A.t - 1)
                            nc.vector.tensor_tensor(RB[:, A.par, :], psJ, X[:, bass.ds(A.t, 1), :].rearrange("p a d -> p (a d)"), ALU.add).then_inc(S["res"].sem, 1)
                            dv.wait_ge(S["res"].sem, S["res"].base + A.t + 1)
                            nc.vector.bn_stats(st[:, A.par, :], RB[:, A.par, :]).then_inc(S["bn"].sem, 1)
                            dv.wait_ge(S["bn"].sem, S["bn"].base + A.t + 1)
                            pace(nc.vector, S)
                            nc.vector.bn_aggr(ag[:, A.par, :], st[:, A.par, :]).then_inc(S["stats"].sem, 1)
                    pipeline(dv, slot, 2)
            S.advance(dict.fromkeys(("scores", "maxed", "shifted", "probs", "turned_a", "turned_b", "pt_a", "pt_b", "pv", "normed", "o_turned_a", "o_turned_b",
                                     "ot_a", "ot_b", "proj", "res", "bn", "stats", "var_eps", "rstd", "out_rows", "summed", "recip"), TILES))
            S.advance(dict(front=NFILL * PAIRS, out_a=NA * PAIRS, out_d=ND * PAIRS, xs=PAIRS))
            mem.close()

        static = lambda T: causal[:, :]
        per_tile = lambda T: maskk[:, bass.ds(T.t, 1), :].rearrange("p a k -> p (a k)")
        attention("L0a", Wm("L0q"), Wm("L0k"), Wm("L0v"), Wm("L0o"), qs=Wm("L0qs"), ks=Wm("L0ks"), mask=static)
        source_stats("rms")
        attention("L0x", ident, ident, ident, Wm("L0xo"), qs=Wm("SWAP"), ks=Wm("SWAP"), gq=C("qn"), gqs=C("qns"), gk=C("kn"), gks=C("kns"),
                  bo=R("L0xb"), cross=True, norm="rms")
        moe("L0f", 8, 2, 88, True, "w1a", "w2a", dict(rw="rwa"))
        grouped_attention()
        key_masks("mask")
        attention("L1x", Wm("L1xq"), Wm("L1xk"), Wm("L1xv"), Wm("L1xo"), bq=C("L1bq"), bk=C("L1bk"), bv=C("L1bv"), bo=R("L1xb"),
                  cross=True, mask=per_tile, keymask=True)
        keep = Memory(nc, "keep")
        XO = keep.sb("XO", [P, TILES, D])
        with nc.Block() as block:
            @block.vector
            def _(dv):
                nc.vector.tensor_tensor(XO[:, :, :], X[:, :, :], R("b2").unsqueeze(1).to_broadcast([P, TILES, D]), ALU.add)
        attention("L1f", Wm("L1fq"), Wm("L1fk"), Wm("L1fv"), Wm("L1fo"), bq=C("L1fbq"), bk=C("L1fbk"), bv=C("L1fbv"), bo=R("L1fb"),
                  affine=(R("g1"), R("b1")))
        moe("L1m", 8, 2, 128, False, "w1b", "w2b", dict(rw="rwb", rb="rbb", b1="b1b", b2="b2b"), XO)
        keep.close()
        attention("L2a", Wm("L2q"), Wm("L2k"), Wm("L2v"), Wm("L2o"), qs=Wm("L2qs"), ks=Wm("L2ks"), bq=C("L2bq"), bqs=C("L2bqs"),
                  bk=C("L2bk"), bks=C("L2bks"), bv=C("L2bv"), bo=R("L2b"), cq=2, ck=2, mask=static)
        attention("L2x", Wm("L2xq"), Wm("L2xk"), Wm("L2xv"), Wm("L2xo"), bq=C("L2xbq"), bk=C("L2xbk"), bv=C("L2xbv"), bo=R("L2xb"), cross=True)
        expert_blocks()
        recurrent_block()
        key_masks("cell")
        source_stats("ln")
        fold_norms()
        attention("L3x", wp[:, 0, :], wp[:, 2, :], wp[:, 4, :], wp[:, 5, :], qs=wp[:, 1, :], ks=wp[:, 3, :], bq=colx[:, 0:1], bqs=colx[:, 1:2],
                  bk=colx[:, 2:3], bks=colx[:, 3:4], cq=4, ck=0, cross=True, norm="ln", mask=per_tile, ln_o=True)
        channel_mix()
        store()


def _swap(w, kind):
    n = w.shape[-1]
    order = np.arange(n) ^ 1 if kind == "pairs" else (np.arange(n) + n // 2) % n
    return w[..., order]


def _rope_tables():
    def table(power, pos, sign):
        inv = (np.float32(1.0) / np.float32(10000.0) ** power.astype(np.float32)).astype(np.float32)
        ang = (inv[:, None] * pos[None, :].astype(np.float32)).astype(np.float32)
        return np.cos(ang).astype(np.float32), (sign[:, None] * np.sin(ang)).astype(np.float32)

    f = np.arange(D)
    pairs = ((f % HD) // 2 * 2 / np.float32(HD))
    psign = np.where(f % 2 == 0, -1.0, 1.0).astype(np.float32)
    halves = (f % (D // 2)) / np.float32(D // 2)
    hsign = np.where(f < D // 2, -1.0, 1.0).astype(np.float32)
    pos = np.arange(SEQ)
    t = [*table(pairs, pos, psign), *table(halves, pos, hsign), *table(pairs, pos - SEQ // 2, psign)]
    return np.ascontiguousarray(np.stack(t, 1))


def kernel(**inputs):
    import concourse.bacc as bacc
    from concourse.bass_utils import run_bass_kernel_spmd

    a = {k: np.asarray(v) for k, v in inputs.items()}
    T = lambda n: a[n].T
    ipw, ipb = a["L1_ffn_in_proj_w"], a["L1_ffn_in_proj_b"]
    eye = np.eye(D, dtype=np.float32)
    w = {"I": eye, "SWAP": _swap(eye, "pairs"),
         "L0q": T("L0_attn_wq"), "L0qs": _swap(T("L0_attn_wq"), "pairs"), "L0k": T("L0_attn_wk"), "L0ks": _swap(T("L0_attn_wk"), "pairs"),
         "L0v": T("L0_attn_wv"), "L0o": T("L0_attn_wo"), "L0xo": T("L0_xattn_proj_w"),
         "L1xq": T("L1_xattn_Wq"), "L1xk": T("L1_xattn_Wk"), "L1xv": T("L1_xattn_Wv"), "L1xo": T("L1_xattn_Wo"),
         "L1fq": ipw[0:D].T, "L1fk": ipw[D:2 * D].T, "L1fv": ipw[2 * D:].T, "L1fo": T("L1_ffn_out_proj_w"),
         "L2q": T("L2_attn_Wq"), "L2qs": _swap(T("L2_attn_Wq"), "halves"), "L2k": T("L2_attn_Wk"), "L2ks": _swap(T("L2_attn_Wk"), "halves"),
         "L2v": T("L2_attn_Wv"), "L2o": T("L2_attn_Wo"),
         "L2xq": T("L2_xattn_Wq"), "L2xk": T("L2_xattn_Wk"), "L2xv": T("L2_xattn_Wv"), "L2xo": T("L2_xattn_Wo"),
         "L3xq": T("L3_xattn_w_q"), "L3xqs": _swap(T("L3_xattn_w_q"), "pairs"), "L3xk": T("L3_xattn_w_k"), "L3xks": _swap(T("L3_xattn_w_k"), "pairs"),
         "L3xv": T("L3_xattn_w_v"), "L3xo": T("L3_xattn_w_o"),
         "L2fa": T("L2_ffn_attn_w"), "L2fn": T("L2_ffn_next_w"), "L3Wx": a["L3_attn_Wx"], "L3Wy": a["L3_attn_Wy"], "L3Wi": a["L3_attn_Wi"],
         "L3Wa": a["L3_attn_Wa"], "L3Wo": a["L3_attn_Wo"], "L3fr": T("L3_ffn_W_r"), "L3fk": T("L3_ffn_W_k"), "L3fv": T("L3_ffn_W_v")}
    qn, kn = np.tile(a["L0_xattn_q_norm_w"], HEADS), np.tile(a["L0_xattn_k_norm_w"], HEADS)
    c = {"qn": qn, "qns": _swap(qn, "pairs"), "kn": kn, "kns": _swap(kn, "pairs"),
         "L1bq": a["L1_xattn_bq"], "L1bk": a["L1_xattn_bk"], "L1bv": a["L1_xattn_bv"], "L1fbq": ipb[0:D], "L1fbk": ipb[D:2 * D], "L1fbv": ipb[2 * D:],
         "L2bq": a["L2_attn_bq"], "L2bqs": _swap(a["L2_attn_bq"], "halves"), "L2bk": a["L2_attn_bk"], "L2bks": _swap(a["L2_attn_bk"], "halves"),
         "L2bv": a["L2_attn_bv"], "L2xbq": a["L2_xattn_bq"], "L2xbk": a["L2_xattn_bk"], "L2xbv": a["L2_xattn_bv"],
         "L3bq": a["L3_xattn_b_q"], "L3bqs": _swap(a["L3_xattn_b_q"], "pairs"), "L3bk": a["L3_xattn_b_k"], "L3bks": _swap(a["L3_xattn_b_k"], "pairs"),
         "L3gq": a["L3_xattn_ln_q_w"], "L3aq": a["L3_xattn_ln_q_b"], "L3gk": a["L3_xattn_ln_k_w"], "L3ak": a["L3_xattn_ln_k_b"],
         "L3gv": a["L3_xattn_ln_v_w"], "L3av": a["L3_xattn_ln_v_b"], "L3go": a["L3_xattn_ln_o_w"], "L3ao": a["L3_xattn_ln_o_b"], "L3bv": a["L3_xattn_b_v"],
         "L2fab": a["L2_ffn_attn_b"], "L2fnb": a["L2_ffn_next_b"], "n1": a["L3_attn_norm1_w"], "n2": a["L3_attn_norm2_w"], "cb": a["L3_attn_conv_b"],
         "lam": a["L3_attn_lam"], **{f"c{k}": a["L3_attn_conv_w"][k] for k in range(4)}, "mur": a["L3_ffn_mu_r"], "muk": a["L3_ffn_mu_k"],
         "L2g": a["L2_ffn_ln_scale"], "L2b": a["L2_ffn_ln_bias"]}
    r = {"L0xb": a["L0_xattn_proj_b"], "L1xb": a["L1_xattn_bo"], "L1fb": a["L1_ffn_out_proj_b"], "L2b": a["L2_attn_bo"], "L2xb": a["L2_xattn_bo"],
         "L3b": a["L3_xattn_b_o"], "g1": a["L1_ffn_ln1_g"], "b1": a["L1_ffn_ln1_b"], "g2": a["L1_ffn_ln2_g"], "b2": a["L1_ffn_ln2_b"]}
    q, k = np.arange(P)[:, None] % SEQ, np.arange(SEQ)[None, :]
    arrays = {
        "x": a["x"].reshape(TOK, D), "ctx": a["ctx_1024"].reshape(TOK, D), "ctxT": a["ctx_1024"].reshape(TOK, D).T,
        "mask": a["mask_BxS2_ik0"].reshape(TOK), "cell": a["itok_Bx1xSx1_0_63"].reshape(TOK), "cellT": a["itok_Bx1xSx1_0_63"].reshape(TILES, P).T,
        "W": np.stack([w[n] for n in SQ], 1), "col": np.stack([c[n] for n in COL], 1), "row": np.stack([r[n] for n in ROW], 0),
        "rope": _rope_tables(),
        "causal": np.where(k <= q, np.float32(0.0), np.float32(NEG)),
    }
    arrays |= {
        "w1a": a["L0_ffn_w1"].transpose(1, 0, 2), "w2a": a["L0_ffn_w2"].reshape(8, 2, 88, D).transpose(2, 0, 1, 3), "rwa": a["L0_ffn_router_weight"],
        "w1b": a["L1_ffn_w1"].transpose(1, 0, 2), "w2b": a["L1_ffn_w2"].reshape(8, 2, 128, D).transpose(2, 0, 1, 3),
        "b1b": a["L1_ffn_b1"].reshape(8, 2, 128).transpose(2, 0, 1), "b2b": a["L1_ffn_b2"],
        "rwb": np.concatenate([a["L1_ffn_w_group"], a["L1_ffn_w_expert"].transpose(1, 0, 2).reshape(D, 8)], 1),
        "rbb": np.concatenate([a["L1_ffn_b_group"], a["L1_ffn_b_expert"].reshape(8)])}
    arrays |= {"w1c": a["L2_ffn_w1"].reshape(8 * D, 512), "w2c": a["L2_ffn_w2"].reshape(8 * 512, D),
               "b1c": a["L2_ffn_b1"].reshape(8, 4, 128).transpose(0, 2, 1).reshape(8 * 128, 4), "b2c": a["L2_ffn_b2"].T}
    arrays |= {"wg": a["L3_attn_Wg"], "wu": a["L3_attn_Wu"], "wd": a["L3_attn_Wd"].reshape(4, 128, D).transpose(1, 0, 2)}
    wk = a["L1_attn_Wk"].T.reshape(D, 4, 1, 64)
    arrays |= {"wq": a["L1_attn_Wq"].T.reshape(D, 8, 128), "wk": np.concatenate([wk, wk], 2), "wv": a["L1_attn_Wv"].T,
               "wo": a["L1_attn_Wo"].T.reshape(8, 128, D).transpose(1, 0, 2)}
    nc = bacc.Bacc("TRN2", target_bir_lowering=False, num_devices=1)
    arrays = {n: np.ascontiguousarray(v) for n, v in arrays.items()}
    io = {n: nc.dram_tensor("in_" + n, v.shape, mybir.dt.from_np(v.dtype), kind="ExternalInput").ap() for n, v in arrays.items()}
    out = nc.dram_tensor("out", (TOK, D), F32, kind="ExternalOutput").ap()
    build(nc, io, out)
    res = run_bass_kernel_spmd(nc, [{"in_" + n: v for n, v in arrays.items()}], core_ids=[0])
    return res.results[0]["out"].reshape(NB, SEQ, D)
```

```python
from contextlib import ExitStack

import numpy as np

import concourse.bass as bass
from concourse import mybir

NB, SEQ, D = 128, 64, 128
HEADS, HD = 16, 8
P = 128
TOK = NB * SEQ
TILES = TOK // P
PAIRS = TILES // 2
BATCH = 512
NBATCH = TOK // BATCH
KVH, GD = 4, 64
HP = HEADS // 2
VW = 2 * HD + 2
LN_EPS = 1e-5
RMS_EPS = 1.1920928955078125e-07
LATE_KEYS = 4
NEG = -1e30

F32, BF16, I32 = mybir.dt.float32, mybir.dt.bfloat16, mybir.dt.int32
ALU, ACT, AX = mybir.AluOpType, mybir.ActivationFunctionType, mybir.AxisListType.X

SQ = ["I", "SWAP", "L0q", "L0qs", "L0k", "L0ks", "L0v", "L0o", "L0xo",
      "L1xq", "L1xk", "L1xv", "L1xo", "L1fq", "L1fk", "L1fv", "L1fo",
      "L2q", "L2qs", "L2k", "L2ks", "L2v", "L2o", "L2xq", "L2xk", "L2xv", "L2xo",
      "L3xq", "L3xqs", "L3xk", "L3xks", "L3xv", "L3xo",
      "L2fa", "L2fn", "L3Wx", "L3Wy", "L3Wi", "L3Wa", "L3Wo", "L3fr", "L3fk", "L3fv"]
COL = ["qn", "qns", "kn", "kns", "L1bq", "L1bk", "L1bv", "L1fbq", "L1fbk", "L1fbv",
       "L2bq", "L2bqs", "L2bk", "L2bks", "L2bv", "L2xbq", "L2xbk", "L2xbv",
       "L3bq", "L3bqs", "L3bk", "L3bks", "L3gq", "L3aq", "L3gk", "L3ak", "L3gv", "L3av", "L3go", "L3ao", "L3bv",
       "L2fab", "L2fnb", "n1", "n2", "cb", "lam", "c0", "c1", "c2", "c3", "mur", "muk", "L2g", "L2b"]
ROW = ["L0xb", "L1xb", "L1fb", "L2b", "L2xb", "L3b", "g1", "b1", "g2", "b2"]


class Signal:

    def __init__(self, ctx, nc, name):
        self.sem, self.base = ctx.enter_context(nc.semaphore(name)), 0


class Signals(dict):

    def __init__(self, ctx, nc):
        super().__init__()
        self.ctx, self.nc = ctx, nc

    def __missing__(self, name):
        self[name] = Signal(self.ctx, self.nc, name)
        return self[name]

    def advance(self, given, when=True):
        for name, n in given.items():
            if when:
                self[name].base += n


def after(count):
    return not isinstance(count, int) or count > 0


def pace(eng, S):
    eng.sem_inc(S["paced"].sem, 1)


class Memory(ExitStack):

    def __init__(self, nc, layer):
        super().__init__()
        self.nc, self.layer = nc, layer

    def sb(self, name, shape, dt=F32):
        return self.enter_context(self.nc.sbuf_tensor(f"{self.layer}_{name}", shape, dt))

    def pb(self, name, shape, dt=F32):
        return self.enter_context(self.nc.psum_tensor(f"{self.layer}_{name}", shape, dt))


class At:

    def __init__(self, i, c, n=TILES):
        self.i, self.c, self.n = i, c, n
        self.ok = i is not None or 0 <= c < n
        self.t = c if i is None else i * 4 + c
        self.par = c % 2
        self.u = (c // 2) % 2

    def __add__(self, k):
        return At(self.i, self.c + k, self.n)

    def __sub__(self, k):
        return self + (-k)

    @property
    def p(self):
        return self.c // 2 if self.i is None else self.i * 2 + self.c // 2


def pipeline(eng, slot, ahead=3):
    first, turns = 8, 13
    for c in range(-ahead, first):
        slot(At(None, c))
    with eng.Fori(0, turns) as i:
        for c in range(4):
            slot(At(i, first + c))
    for c in range(first + 4 * turns, TILES + 6):
        slot(At(None, c))


def build(nc, io, out):
    ctx = ExitStack()
    with ctx:
        S = Signals(ctx, nc)

        def sb(name, shape, dt=F32):
            return ctx.enter_context(nc.sbuf_tensor(name, shape, dt))

        def pb(name, shape, dt=F32):
            return ctx.enter_context(nc.psum_tensor(name, shape, dt))

        X = sb("X", [P, TILES, D])
        W = sb("W", [P, len(SQ), D])
        col = sb("col", [P, len(COL)])
        row = sb("row", [P, len(ROW), D])
        rope = sb("rope", [P, 6, SEQ])
        idb = sb("idb", [P, P], BF16)
        causal = sb("causal", [P, SEQ], BF16)
        maskk = sb("maskk", [P, TILES, SEQ], BF16)
        stat = sb("stat", [P, TILES, HEADS])
        stat2 = sb("stat2", [P, TILES, HEADS])
        wp = sb("wp", [P, 6, D])
        colx = sb("colx", [P, 8])
        rowx = sb("rowx", [P, 2, D])
        colb = sb("colb", [P, 2, D])
        half = sb("half", [P, 4])
        zeros = sb("zeros", [P, 1])
        eps = sb("eps", [P, 4])
        cellq = sb("cellq", [P, TILES], I32)
        ident = W[:, SQ.index("I"), :]
        Wm = lambda n: W[:, SQ.index(n), :]
        C = lambda n: col[:, COL.index(n):COL.index(n) + 1]
        R = lambda n: row[:, ROW.index(n), :]

        mem0 = Memory(nc, "setup")
        causal32 = mem0.sb("causal32", [P, SEQ])
        with nc.Block() as block:
            @block.sync
            def _(sp):
                for dst, src in ((W[:, :, :], io["W"]), (X[:, :, :], io["x"].rearrange("(t p) d -> p t d", p=P)),
                                 (col[:, :], io["col"]), (rope[:, :, :], io["rope"])):
                    sp.dma_start(dst, src).then_inc(S["loaded"].sem, 16)
                sp.dma_start(row[:, :, :], io["row"].partition_broadcast(P)).then_inc(S["loaded"].sem, 16)
                sp.dma_start(causal32[:, :], io["causal"]).then_inc(S["loaded"].sem, 16)
                sp.wait_ge(S["loaded"].sem, 6 * 16)

            @block.vector
            def _(v):
                nc.vector.memset(half[:, :], -0.5)
                nc.vector.memset(zeros[:, :], 0.0)
                nc.vector.memset(eps[:, :], LN_EPS)
                v.wait_ge(S["loaded"].sem, S["loaded"].base + 6 * 16)
                nc.vector.tensor_copy(idb[:, :], ident)
                nc.vector.tensor_copy(causal[:, :], causal32[:, :])
        mem0.close()

        def attention(L, q, k, v, o, qs=None, ks=None, gq=None, gqs=None, gk=None, gks=None, bq=None, bqs=None, bk=None, bks=None, bv=None, bo=None,
                      cq=0, ck=0, cross=False, norm=None, mask=None, keymask=False, ln_o=False, affine=None):
            mem = Memory(nc, L)
            XS = mem.sb("XS", [P, 2, 2, D])
            CS = mem.sb("CS", [P, 2, 2, D])
            XR = mem.sb("XR", [P, 2, 2, D])
            XT = mem.sb("XT", [P, 2, 2 * P])
            CT = mem.sb("CT", [P, 2, 2 * P])
            CR = mem.sb("CR", [P, 2, 2 * P])
            CN = mem.sb("CN", [P, 2, 2, D])
            RA = mem.sb("RA", [P, 2, 2, 2 * P])
            MI = mem.sb("MI", [P, 2, 2 * P], I32)
            MF = mem.sb("MF", [P, 2, 2 * P])
            QT = mem.sb("QT", [P, 2, 2 * P])
            KT = mem.sb("KT", [P, 2, 2 * P])
            KB = mem.sb("KB", [P, 2, HEADS, 4, SEQ])
            VB = mem.sb("VB", [P, 2, 4, HP, VW])
            PR = mem.sb("PR", [P, 2, HEADS, SEQ])
            PT = mem.sb("PT", [P, 2, HP, P])
            mx = mem.sb("mx", [P, 2, HEADS])
            rden = mem.sb("rden", [P, 2, HP, 2])
            ON = mem.sb("ON", [P, 2, D])
            OT = mem.sb("OT", [P, 2, P])
            RB = mem.sb("RB", [P, 2, 2, D])
            st6 = mem.sb("st6", [P, 2, 6])
            mv = mem.sb("mv", [P, 2, 2, 2])
            rs = mem.sb("rs", [P, 2, 2, 2])
            st6o = mem.sb("st6o", [P, 2, 6])
            mvo = mem.sb("mvo", [P, 2, 2])
            rso = mem.sb("rso", [P, 2, 2])
            OL = mem.sb("OL", [P, 2, D])

            psS = mem.pb("psS", [P, 2, HEADS, SEQ])
            psP = mem.pb("psP", [P, 2, 4, P])
            psF = mem.pb("psF", [P, 512])
            psB = mem.pb("psB", [P, 512])
            psO, psOT, psJ = psB[:, 0:HP * VW], psB[:, 256:384], psB[:, 384:512]
            scale = HD ** -0.5
            steps = ["tx"] + (["tc"] if cross and norm else []) + ["k", "q", "v"]
            NS = len(steps)
            NF = NS + 1
            e = 1 if ln_o else 0
            sidx = {s: n for n, s in enumerate(steps)}
            zero = zeros[:, 0:1]
            late = 0 if ln_o else LATE_KEYS
            raw = cross and norm != "ln"

            def front_done(eng, p, step):
                eng.wait_ge(S["front_out"].sem, S["front_out"].base + p * NF + (NF if step == "v" else sidx[step] + 1))

            def wait_front(eng, p, step):
                eng.wait_ge(S["front"].sem, S["front"].base + p * NS + sidx[step] + 1)


            with nc.Block() as block:
                @block.vector
                def _(dv):
                    nc.vector.memset(VB[:, :, :, :, :], 0.0).then_inc(S["zeroed"].sem, 1)
                    nc.vector.memset(KB[:, 0, :, :, :], 0.0)
                    dv.wait_ge(S["zeroed"].sem, S["zeroed"].base + 1)
                    nc.vector.memset(VB[0:64, :, :, :, 2 * HD:2 * HD + 1], 1.0)
                    nc.vector.memset(VB[64:128, :, :, :, 2 * HD + 1:VW], 1.0)

                @block.gpsimd
                def _(g):
                    nc.gpsimd.memset(KB[:, 1, :, :, :], 0.0)
            S.advance(dict(zeroed=1))
            src = (CR if norm is None else CT) if cross else XT
            srcv = (CR if raw else CT) if cross else XT
            bias_row = rowx[:, 0, :] if bv is not None or ln_o else bo
            if bv is not None and not ln_o:
                with nc.Block() as block:
                    @block.vector
                    def _(dv):
                        nc.vector.tensor_scalar(colb[:, 0, :], ident, 0.0, bv, ALU.mult, ALU.add).then_inc(S["prep"].sem, 1)
                        dv.wait_ge(S["prep_pe"].sem, S["prep_pe"].base + 1)
                        nc.vector.tensor_tensor(rowx[:, 0, :], psJ, bo, ALU.add)

                    @block.tensor
                    def _(pe):
                        pe.wait_ge(S["prep"].sem, S["prep"].base + 1)
                        nc.tensor.matmul(psJ, colb[:, 0, :], o, start=True, stop=True).then_inc(S["prep_pe"].sem, 1)
                S["prep"].base += 1
                S["prep_pe"].base += 1

            def parity_wait(eng, name, K, each):
                if K.i is None and K.c < 0:
                    return
                n = K.c // 4 if K.i is None else K.i + K.c // 4
                eng.wait_ge(S[f"{name}{K.u}"].sem, S[f"{name}{K.u}"].base + (n + 1) * each)

            def parity_sem(name, K):
                return S[f"{name}{K.u}"].sem

            def xrow(t):
                return X[:, t, :] if isinstance(t, int) else X[:, bass.ds(t, 1), :].rearrange("p a d -> p (a d)")

            heads = lambda ap: ap.rearrange("p t (h d) -> p (t h) d", d=HD)

            with nc.Block() as block:
                @block.sync
                def _(sp):
                    def slot(T):
                        N = T + 4
                        if T.par == 0 and N.ok:
                            if raw:
                                if after((N.p - 2) * NS + NS):
                                    sp.wait_ge(S["front"].sem, S["front"].base + (N.p - 2) * NS + NS)
                                sp.dma_start(CR[:, N.u, :], io["ctxT"][:, bass.ds(N.p * 256, 256)]).then_inc(parity_sem("ctx_in", N), 16)
                            if cross and norm:
                                if after(N.p - 1):
                                    sp.wait_ge(S["ctx_normed"].sem, S["ctx_normed"].base + N.p - 1)
                                sp.dma_start(CS[:, N.u, :, :], io["ctx"][bass.ds(N.p * 256, 256), :].rearrange("(t p) d -> p t d", p=P)).then_inc(parity_sem("rows_in", N), 16)
                            if keymask:
                                if after(N.p - 1):
                                    sp.wait_ge(S["mask_used"].sem, S["mask_used"].base + N.p - 1)
                                sp.dma_start(MI[:, N.u, :], io["mask"][bass.ds(N.p * 256, 256)].partition_broadcast(P)).then_inc(parity_sem("mask_in", N), 16)
                        K = T + 2
                        if T.par == 0 and K.ok:
                            if ks is not None:
                                sp.wait_ge(S["k_roped"].sem, S["k_roped"].base + K.p + 1)
                            else:
                                front_done(sp, K.p, "k")
                            if after(2 * K.p - 2):
                                sp.wait_ge(S["scores"].sem, S["scores"].base + 2 * K.p - 2)
                            for h in range(HEADS - late):
                                sp.dma_start(KB[HD * h:HD * h + HD, K.u, h, :, :].rearrange("p s k -> p (s k)"), KT[HD * h:HD * h + HD, K.u, :]).then_inc(parity_sem("keys_in", K), 16)
                    pipeline(sp, slot, 4)

                @block.gpsimd
                def _(g):
                    def normalise(N, dst, src_, st, between, done):
                        if norm == "rms":
                            r = st[:, bass.ds(N.t, 2), :].rearrange("p t h -> p (t h)").unsqueeze(2).to_broadcast([P, 2 * HEADS, HD])
                            nc.gpsimd.tensor_tensor(heads(dst), heads(src_), r, ALU.mult).then_inc(done.sem, 1)
                        else:
                            nc.gpsimd.tensor_tensor(dst, src_, st[:, bass.ds(N.t, 2), 0:1].to_broadcast([P, 2, D]), ALU.subtract).then_inc(between.sem, 1)
                            g.wait_ge(between.sem, between.base + N.p + 1)
                            nc.gpsimd.tensor_tensor(dst, dst, st[:, bass.ds(N.t, 2), 1:2].to_broadcast([P, 2, D]), ALU.mult).then_inc(done.sem, 1)

                    def slot(T):
                        N = T + 2
                        if T.par == 0 and N.ok:
                            if ks is not None:
                                front_done(g, N.p, "k")
                                parity_wait(g, "keys_in", N - 4, 16 * (HEADS - late))
                                if late:
                                    parity_wait(g, "late_keys_in", N - 4, 16 * late)
                                nc.gpsimd.tensor_tensor(KT[:, N.u], RA[:, 0, 0], RA[:, 0, 1], ALU.add).then_inc(S["k_roped"].sem, 1)
                            if late and ks is not None:
                                g.wait_ge(S["k_roped"].sem, S["k_roped"].base + N.p + 1)
                            elif late:
                                front_done(g, N.p, "k")
                            if late:
                                if after(2 * N.p - 2):
                                    g.wait_ge(S["scores"].sem, S["scores"].base + 2 * N.p - 2)
                                pace(g, S)
                            for h in range(HEADS - late, HEADS):
                                nc.gpsimd.dma_start(KB[HD * h:HD * h + HD, N.u, h, :, :].rearrange("p s k -> p (s k)"), KT[HD * h:HD * h + HD, N.u, :]).then_inc(parity_sem("late_keys_in", N), 16)
                        K = T + 1
                        if T.par == 1 and K.ok and qs is not None:
                            front_done(g, K.p, "q")
                            if after(2 * K.p - 2):
                                g.wait_ge(S["scores"].sem, S["scores"].base + 2 * K.p - 2)
                            nc.gpsimd.tensor_tensor(QT[:, K.u], RA[:, 1, 0], RA[:, 1, 1], ALU.add).then_inc(S["q_roped"].sem, 1)
                        N = T + 3
                        if T.par == 1 and N.ok:
                            if after((N.p - 2) * NS + 1):
                                g.wait_ge(S["front"].sem, S["front"].base + (N.p - 2) * NS + 1)
                            xin = X[:, bass.ds(N.t, 2), :]
                            if norm:
                                normalise(N, XS[:, N.u], xin, stat, S["x_centred"], S["xs"])
                            else:
                                nc.gpsimd.tensor_copy(XS[:, N.u], xin).then_inc(S["xs"].sem, 1)
                            if cross and norm:
                                parity_wait(g, "rows_in", N, 16)
                                if after((N.p - 2) * NS + 2):
                                    g.wait_ge(S["front"].sem, S["front"].base + (N.p - 2) * NS + 2)
                                normalise(N, CN[:, N.u], CS[:, N.u], stat2, S["ctx_centred"], S["ctx_normed"])
                        A = T - 2
                        if A.par == 0 and A.ok and bias_row is not None:
                            if after(2 * (A.p - 1)):
                                g.wait_ge(S["res"].sem, S["res"].base + 2 * (A.p - 1))
                            nc.gpsimd.tensor_tensor(XR[:, A.u], X[:, bass.ds(A.t, 2), :], bias_row.unsqueeze(1).to_broadcast([P, 2, D]), ALU.add).then_inc(S["xres"].sem, 1)
                        A = T - 3
                        if ln_o and A.ok:
                            g.wait_ge(S["o_stats"].sem, S["o_stats"].base + A.t + 1)
                            if after(A.t - 1):
                                g.wait_ge(S["o_ready"].sem, S["o_ready"].base + A.t - 1)
                            nc.gpsimd.tensor_tensor(rso[:, A.par, 0:1], mvo[:, A.par, 1:2], eps[:, 0:1], ALU.add).then_inc(S["o_eps"].sem, 1)
                            g.wait_ge(S["o_eps"].sem, S["o_eps"].base + A.t + 1)
                            nc.gpsimd.tensor_tensor(rso[:, A.par, 1:2], rso[:, A.par, 0:1], half[:, 0:1], ALU.pow).then_inc(S["o_rstd"].sem, 1)
                        F = T - 4 - e
                        if F.par == 1 and F.ok:
                            g.wait_ge(S["stats"].sem, S["stats"].base + F.t + 1)
                            if after(F.p - 1):
                                g.wait_ge(S["out_rows"].sem, S["out_rows"].base + F.p - 1)
                            nc.gpsimd.tensor_tensor(rs[:, F.u, 0, :], mv[:, F.u, :, 1], eps[:, 0:2], ALU.add).then_inc(S["var_eps"].sem, 1)
                            g.wait_ge(S["var_eps"].sem, S["var_eps"].base + F.p + 1)
                            nc.gpsimd.tensor_tensor(rs[:, F.u, 1, :], rs[:, F.u, 0, :], half[:, 0:2], ALU.pow).then_inc(S["rstd"].sem, 1)
                    pipeline(g, slot)

                @block.tensor
                def _(pe):
                    def front(N, step):
                        if after(N.p * NF + sidx[step]):
                            pe.wait_ge(S["front_out"].sem, S["front_out"].base + N.p * NF + sidx[step])
                        if step == "tx":
                            pe.wait_ge(S["xs"].sem, S["xs"].base + N.p + 1)
                            for a in range(2):
                                m = nc.tensor.transpose(psF[:, a * P:a * P + P], XS[:, N.u, a, :], ident)
                        if step == "tc":
                            pe.wait_ge(S["ctx_normed"].sem, S["ctx_normed"].base + N.p + 1)
                            for a in range(2):
                                m = nc.tensor.transpose(psF[:, a * P:a * P + P], CN[:, N.u, a, :], ident)
                        if step in ("k", "q"):
                            s_, w, ws = (src, k, ks) if step == "k" else (XT, q, qs)
                            if raw:
                                parity_wait(pe, "ctx_in", N, 16)
                            m = nc.tensor.matmul(psF[:, 0:256], w, s_[:, N.u, :], start=True, stop=True)
                            if ws is not None:
                                m = nc.tensor.matmul(psF[:, 256:512], ws, s_[:, N.u, :], start=True, stop=True)
                        if step == "v":
                            for s in range(4):
                                for a in range(2):
                                    m = nc.tensor.matmul(psF[64 * a:64 * a + 64, s * D:s * D + D], srcv[:, N.u, s * SEQ:(s + 1) * SEQ], v, start=True, stop=True)
                        m.then_inc(S["front"].sem, 1)

                    def projections(T):
                        if T.par == 0 and (T + 2).ok:
                            front(T + 2, "k")
                        if T.par == 1 and (T + 1).ok:
                            front(T + 1, "q")

                    def slot(T):
                        N, K, M = T + 2, T + 1, T + 3
                        if late == 0:
                            projections(T)
                        def scores(hh):
                            if qs is not None:
                                pe.wait_ge(S["q_roped"].sem, S["q_roped"].base + T.p + 1)
                            else:
                                front_done(pe, T.p, "q")
                            parity_wait(pe, "keys_in", T, 16 * (HEADS - late))
                            if late:
                                parity_wait(pe, "late_keys_in", T, 16 * late)
                            if after(T.t - 1):
                                pe.wait_ge(S["shifted"].sem, S["shifted"].base + T.t - 1)
                            if mask is not None:
                                mk = mask(T).unsqueeze(1).to_broadcast([P, 8, SEQ])
                                nc.tensor.matmul(psS[:, T.par, 8 * hh:8 * hh + 8, :], idb[:, :], mk, start=True, stop=False, skip_group_check=True)
                            for s in range(2):
                                q4 = 2 * T.par + s
                                m = nc.tensor.matmul(psS[64 * s:64 * s + 64, T.par, 8 * hh:8 * hh + 8, :],
                                                     QT[:, T.u, q4 * SEQ:(q4 + 1) * SEQ], KB[:, T.u, 8 * hh:8 * hh + 8, q4, :],
                                                     start=mask is None, stop=True, skip_group_check=True)
                            if hh == 1:
                                m.then_inc(S["scores"].sem, 1)

                        if T.ok:
                            scores(0)
                        if late:
                            projections(T)
                        A = T - 3 - e
                        if A.ok:
                            pe.wait_ge(S["normed"].sem, S["normed"].base + (T.t - 2 if T.i is not None else min(T.c - 2, TILES)))
                            if ln_o:
                                pe.wait_ge(S["o_ready"].sem, S["o_ready"].base + A.t + 1)
                            nc.tensor.transpose(psOT, (OL if ln_o else ON)[:, A.par, :], ident).then_inc(S["o_turned"].sem, 1)
                        if T.ok:
                            scores(1)
                        A = T - 3 - e
                        if A.ok:
                            pe.wait_ge(S["ot"].sem, S["ot"].base + A.t + 1)
                            nc.tensor.matmul(psJ, OT[:, A.par, :], o, start=True, stop=True).then_inc(S["proj"].sem, 1)
                        A = T - 1
                        if A.ok:
                            pe.wait_ge(S["probs"].sem, S["probs"].base + A.t + 1)
                            for hb, freed, turned in ((0, S["pt_a"], S["turned_a"]), (1, S["pt_b"], S["turned_b"])):
                                if after(A.t):
                                    pe.wait_ge(freed.sem, freed.base + A.t)
                                for j in range(4):
                                    b = hb * 4 + j
                                    m = nc.tensor.transpose(psP[:, hb, j, :], PR[:, A.par, 2 * b:2 * b + 2, :].rearrange("p h k -> p (h k)"), ident)
                                m.then_inc(turned.sem, 1)
                        if T.par == 1 and K.ok:
                            front(K, "v")
                        A = T - 2
                        if A.ok:
                            pe.wait_ge(S["pt_a"].sem, S["pt_a"].base + A.t + 1)
                            pe.wait_ge(S["pt_b"].sem, S["pt_b"].base + A.t + 1)
                            front_done(pe, A.p, "v")
                            if after(A.t - e):
                                pe.wait_ge(S["res"].sem, S["res"].base + A.t - e)
                            for b in range(HP):
                                for s in range(2):
                                    m = nc.tensor.matmul(psO[64 * s:64 * s + 64, b * VW:(b + 1) * VW], PT[:, A.par, b, 64 * s:64 * s + 64],
                                                         VB[:, A.u, 2 * A.par + s, b, :], start=True, stop=True)
                            m.then_inc(S["pv"].sem, 1)
                        if T.par == 1 and M.ok:
                            front(M, "tx")
                            if "tc" in steps:
                                front(M, "tc")
                    pipeline(pe, slot)

                @block.scalar
                def _(act):
                    def slot(T):
                        N, K, M = T + 2, T + 1, T + 3
                        if T.par == 0 and N.ok and ks is None and not keymask:
                            wait_front(act, N.p, "k")
                            parity_wait(act, "keys_in", N - 4, 16 * (HEADS - late))
                            if late:
                                parity_wait(act, "late_keys_in", N - 4, 16 * late)
                            nc.scalar.activation(KT[:, N.u, :], psF[:, 0:256], ACT.Identity, bias=bk if bk is not None else zero).then_inc(S["front_out"].sem, 1)
                        if T.par == 1 and K.ok and qs is None:
                            wait_front(act, K.p, "q")
                            if after(2 * K.p - 2):
                                act.wait_ge(S["scores"].sem, S["scores"].base + 2 * K.p - 2)
                            nc.scalar.activation(QT[:, K.u, :], psF[:, 0:256], ACT.Identity, bias=bq if bq is not None else zero).then_inc(S["front_out"].sem, 1)
                        A = T - 3 - e
                        if A.ok:
                            act.wait_ge(S["o_turned"].sem, S["o_turned"].base + A.t + 1)
                            if after(A.t - 1):
                                act.wait_ge(S["proj"].sem, S["proj"].base + A.t - 1)
                            nc.scalar.activation(OT[:, A.par, :], psOT, ACT.Copy).then_inc(S["ot"].sem, 1)
                        A = T - 1
                        if A.ok:
                            act.wait_ge(S["turned_a"].sem, S["turned_a"].base + A.t + 1)
                            if after(A.t - 1):
                                act.wait_ge(S["pv"].sem, S["pv"].base + A.t - 1)
                            nc.scalar.activation(PT[:, A.par, 0:4, :], psP[:, 0], ACT.Copy).then_inc(S["pt_a"].sem, 1)
                        if T.ok:
                            act.wait_ge(S["shifted"].sem, S["shifted"].base + T.t + 1)
                            nc.scalar.activation(PR[:, T.par], PR[:, T.par], ACT.Exp, scale=scale).then_inc(S["probs"].sem, 1)
                        if T.par == 1 and K.ok:
                            wait_front(act, K.p, "v")
                            if after(2 * (K.p - 1)):
                                act.wait_ge(S["pv"].sem, S["pv"].base + 2 * (K.p - 1))
                            nc.scalar.activation(VB[0:64, K.u, :, :, 0:HD].rearrange("p s b d -> p (s b) d"),
                                                 psF[0:64, :].rearrange("p (b h d) -> p b h d", h=2, d=HD)[:, :, 0, :], ACT.Copy).then_inc(S["front_out"].sem, 1)
                        if T.par == 1 and M.ok:
                            wait_front(act, M.p, "tx")
                            if after((M.p - 2) * NS + (sidx["q"] + 1 if cross else NS)):
                                act.wait_ge(S["front"].sem, S["front"].base + (M.p - 2) * NS + (sidx["q"] + 1 if cross else NS))
                            nc.scalar.activation(XT[:, M.u, :], psF[:, 0:256], ACT.Copy).then_inc(S["front_out"].sem, 1)
                            if "tc" in steps:
                                wait_front(act, M.p, "tc")
                                if after((M.p - 2) * NS + NS):
                                    act.wait_ge(S["front"].sem, S["front"].base + (M.p - 2) * NS + NS)
                                nc.scalar.activation(CT[:, M.u, :], psF[:, 0:256], ACT.Copy).then_inc(S["front_out"].sem, 1)
                    pipeline(act, slot)

                @block.vector
                def _(dv):
                    def rope_parts(N, step, parts, tab, n, roped):
                        wait_front(dv, N.p, step)
                        if after(N.p):
                            dv.wait_ge(roped.sem, roped.base + N.p)
                        by_seq = lambda ap: ap.rearrange("p (s k) -> p s k", s=4)
                        for j, (vec, op) in enumerate(parts):
                            table = rope[:, tab + j, :].unsqueeze(1).to_broadcast([P, 4, SEQ])
                            m = nc.vector.scalar_tensor_tensor(by_seq(RA[:, n, j]), by_seq(psF[:, 256 * j:256 * j + 256]), vec, table, op, ALU.mult)
                        m.then_inc(S["front_out"].sem, 1)

                    def part(g_, b_):
                        return (g_, ALU.mult) if g_ is not None else (b_ if b_ is not None else zero, ALU.add)

                    def slot(T):
                        N, K = T + 2, T + 1
                        A = T - 4
                        if ln_o and A.ok:
                            dv.wait_ge(S["o_rstd"].sem, S["o_rstd"].base + A.t + 1)
                            if after(A.t - 1):
                                dv.wait_ge(S["o_turned"].sem, S["o_turned"].base + A.t - 1)
                            nc.vector.tensor_scalar(OL[:, A.par, :], ON[:, A.par, :], mvo[:, A.par, 0:1], rso[:, A.par, 1:2], ALU.subtract, ALU.mult).then_inc(S["o_ready"].sem, 1)
                        A = T - 3
                        if A.ok:
                            dv.wait_ge(S["pv"].sem, S["pv"].base + A.t + 1)
                            o3 = psO.rearrange("p (b c) -> p b c", c=VW)
                            nc.vector.reciprocal(rden[:, A.par], o3[:, :, 2 * HD:VW]).then_inc(S["recip"].sem, 1)
                            dv.wait_ge(S["recip"].sem, S["recip"].base + A.t + 1)
                            if after(A.t - 1):
                                dv.wait_ge((S["o_ready"] if ln_o else S["o_turned"]).sem, (S["o_ready"] if ln_o else S["o_turned"]).base + A.t - 1)
                            nc.vector.tensor_tensor(ON[:, A.par, :].rearrange("p (b h d) -> p b h d", h=2, d=HD),
                                                    o3[:, :, 0:2 * HD].rearrange("p b (h d) -> p b h d", h=2),
                                                    rden[:, A.par].unsqueeze(3).to_broadcast([P, HP, 2, HD]), ALU.mult).then_inc(S["normed"].sem, 1)
                            if ln_o:
                                dv.wait_ge(S["normed"].sem, S["normed"].base + A.t + 1)
                                nc.vector.tensor_tensor(ON[:, A.par, :], ON[:, A.par, :], rowx[:, 1, :], ALU.add).then_inc(S["o_sum"].sem, 1)
                                dv.wait_ge(S["o_sum"].sem, S["o_sum"].base + A.t + 1)
                                nc.vector.bn_stats(st6o[:, A.par, :], ON[:, A.par, :]).then_inc(S["o_bn"].sem, 1)
                                dv.wait_ge(S["o_bn"].sem, S["o_bn"].base + A.t + 1)
                                pace(nc.vector, S)
                                nc.vector.bn_aggr(mvo[:, A.par, :], st6o[:, A.par, :]).then_inc(S["o_stats"].sem, 1)
                        if T.par == 0 and N.ok:
                            if ks is not None:
                                rope_parts(N, "k", (part(gk, bk), part(gks, bks)), ck, 0, S["k_roped"])
                            elif keymask:
                                wait_front(dv, N.p, "k")
                                dv.wait_ge(S["mask_used"].sem, S["mask_used"].base + N.p + 1)
                                parity_wait(dv, "keys_in", N - 4, 16 * (HEADS - late))
                                if late:
                                    parity_wait(dv, "late_keys_in", N - 4, 16 * late)
                                nc.vector.scalar_tensor_tensor(KT[:, N.u, :], psF[:, 0:256], bk, MF[:, N.u, :], ALU.add, ALU.mult).then_inc(S["front_out"].sem, 1)
                        if T.par == 1 and K.ok and qs is not None:
                            rope_parts(K, "q", (part(gq, bq), part(gqs, bqs)), cq, 1, S["q_roped"])
                        if T.ok:
                            dv.wait_ge(S["scores"].sem, S["scores"].base + T.t + 1)
                            nc.vector.tensor_reduce(mx[:, T.par, :], psS[:, T.par], AX, ALU.max).then_inc(S["maxed"].sem, 1)
                        J = T - 3 - e
                        if J.ok:
                            dv.wait_ge(S["proj"].sem, S["proj"].base + J.t + 1)
                            if bias_row is not None:
                                dv.wait_ge(S["xres"].sem, S["xres"].base + J.p + 1)
                            res = XR[:, J.u, J.par, :] if bias_row is not None else xrow(J.t)
                            if after(J.p - 1):
                                dv.wait_ge(S["out_rows"].sem, S["out_rows"].base + J.p - 1)
                            nc.vector.tensor_tensor(RB[:, J.u, J.par, :], psJ, res, ALU.add).then_inc(S["res"].sem, 1)
                        if T.ok:
                            dv.wait_ge(S["maxed"].sem, S["maxed"].base + T.t + 1)
                            if after(T.t - 1):
                                dv.wait_ge(S["turned_b"].sem, S["turned_b"].base + T.t - 1)
                            nc.vector.tensor_tensor(PR[:, T.par], psS[:, T.par], mx[:, T.par, :].unsqueeze(2).to_broadcast([P, HEADS, SEQ]), ALU.subtract).then_inc(S["shifted"].sem, 1)
                        if J.ok:
                            dv.wait_ge(S["res"].sem, S["res"].base + J.t + 1)
                            nc.vector.bn_stats(st6[:, J.par, :], RB[:, J.u, J.par, :]).then_inc(S["bn"].sem, 1)
                        A = T - 1
                        if A.ok:
                            dv.wait_ge(S["turned_b"].sem, S["turned_b"].base + A.t + 1)
                            if after(A.t - 1):
                                dv.wait_ge(S["pv"].sem, S["pv"].base + A.t - 1)
                            nc.vector.tensor_copy(PT[:, A.par, 4:8, :], psP[:, 1]).then_inc(S["pt_b"].sem, 1)
                        if J.ok:
                            dv.wait_ge(S["bn"].sem, S["bn"].base + J.t + 1)
                            pace(nc.vector, S)
                            nc.vector.bn_aggr(mv[:, J.u, J.par, :], st6[:, J.par, :]).then_inc(S["stats"].sem, 1)
                        A = T - 5 - e
                        if A.par == 1 and A.ok:
                            dv.wait_ge(S["rstd"].sem, S["rstd"].base + A.p + 1)
                            for a in range(2):
                                xo = xrow((A - 1 + a).t)
                                m = nc.vector.tensor_scalar(xo, RB[:, A.u, a, :], mv[:, A.u, a, 0:1], rs[:, A.u, 1, a:a + 1], ALU.subtract, ALU.mult)
                                if affine is not None:
                                    m.then_inc(S["unscaled"].sem, 1)
                                    dv.wait_ge(S["unscaled"].sem, S["unscaled"].base + 2 * A.t - 1 + 2 * a)
                                    nc.vector.tensor_tensor(xo, xo, affine[0], ALU.mult).then_inc(S["unscaled"].sem, 1)
                                    dv.wait_ge(S["unscaled"].sem, S["unscaled"].base + 2 * A.t + 2 * a)
                                    m = nc.vector.tensor_tensor(xo, xo, affine[1], ALU.add)
                            m.then_inc(S["out_rows"].sem, 1)
                        if T.par == 1 and K.ok:
                            wait_front(dv, K.p, "v")
                            if after(2 * (K.p - 1)):
                                dv.wait_ge(S["pv"].sem, S["pv"].base + 2 * (K.p - 1))
                            nc.vector.tensor_copy(VB[64:128, K.u, :, :, HD:2 * HD].rearrange("p s b d -> p (s b) d"),
                                                  psF[64:128, :].rearrange("p (b h d) -> p b h d", h=2, d=HD)[:, :, 1, :]).then_inc(S["front_out"].sem, 1)
                        M = T + 3
                        if T.par == 1 and M.ok and keymask:
                            parity_wait(dv, "mask_in", M, 16)
                            nc.vector.tensor_scalar(MF[:, M.u, :], MI[:, M.u, :], 0.0, None, ALU.not_equal).then_inc(S["mask_used"].sem, 1)
                    pipeline(dv, slot)

            S.advance(dict(front=NS * PAIRS, front_out=NF * PAIRS, keys_in0=8 * (HEADS - late) * PAIRS, keys_in1=8 * (HEADS - late) * PAIRS,
                           late_keys_in0=8 * late * PAIRS, late_keys_in1=8 * late * PAIRS))
            S.advance(dict.fromkeys(("xs", "rstd", "var_eps", "out_rows"), PAIRS))
            S.advance(dict.fromkeys(("scores", "shifted", "maxed", "probs", "pt_a", "pt_b", "turned_a", "turned_b", "pv", "normed",
                                     "recip", "ot", "o_turned", "proj", "res", "bn", "stats"), TILES))
            S.advance(dict.fromkeys(("q_roped",), PAIRS), qs is not None)
            S.advance(dict.fromkeys(("k_roped",), PAIRS), ks is not None)
            S.advance(dict.fromkeys(("xres",), PAIRS), bias_row is not None)
            S.advance(dict(mask_used=PAIRS, mask_in0=8 * PAIRS, mask_in1=8 * PAIRS), keymask)
            S.advance(dict(ctx_in0=8 * PAIRS, ctx_in1=8 * PAIRS), raw)
            S.advance(dict(rows_in0=8 * PAIRS, rows_in1=8 * PAIRS, ctx_normed=PAIRS), cross and norm is not None)
            S.advance(dict(x_centred=PAIRS), norm == "ln")
            S.advance(dict(unscaled=2 * TILES), affine is not None)
            S.advance(dict(ctx_centred=PAIRS), norm == "ln" and cross)
            S.advance(dict.fromkeys(("o_sum", "o_bn", "o_stats", "o_eps", "o_rstd", "o_ready"), TILES), ln_o)
            mem.close()

        def store():
            with nc.Block() as block:
                @block.sync
                def _(sp):
                    sp.dma_start(out.rearrange("(t p) d -> p t d", p=P), X[:, :, :]).then_inc(S["stored"].sem, 16)
                    sp.wait_ge(S["stored"].sem, 16)

        def key_masks(which):
            mem = Memory(nc, "masks_" + which)
            MK = mem.sb("MK", [P, TILES * SEQ // 4], I32)
            KEEP = mem.sb("KEEP", [P, TILES * SEQ // 4])
            n = 4
            w = TILES // n
            src = io["mask"] if which == "mask" else io["cell"]
            with nc.Block() as block:
                @block.sync
                def _(sp):
                    if which == "cell":
                        sp.dma_start(cellq[:, :], io["cellT"]).then_inc(S["mask_rows"].sem, 16)
                    for r in range(n):
                        if r:
                            sp.wait_ge(S["mask_made"].sem, S["mask_made"].base + r)
                        for s in range(2):
                            rows = src.rearrange("(t s k) -> s t k", s=2, k=SEQ)[s, r * w:(r + 1) * w, :]
                            sp.dma_start(MK[64 * s:64 * s + 64, 0:w * SEQ].rearrange("p (t k) -> p t k", k=SEQ),
                                         rows.partition_broadcast(64)).then_inc(S["mask_rows"].sem, 16)

                @block.vector
                def _(dv):
                    own = 16 if which == "cell" else 0
                    for r in range(n):
                        dv.wait_ge(S["mask_rows"].sem, S["mask_rows"].base + own + 32 * (r + 1))
                        mk = MK[:, 0:w * SEQ].rearrange("p (t k) -> p t k", k=SEQ)
                        keep = KEEP[:, :].rearrange("p (t k) -> p t k", k=SEQ)
                        if which == "mask":
                            nc.vector.tensor_scalar(keep, mk, 0.0, None, ALU.not_equal).then_inc(S["mask_keep"].sem, 1)
                        else:
                            nc.vector.tensor_tensor(keep, mk, cellq[:, r * w:(r + 1) * w].unsqueeze(2).to_broadcast([P, w, SEQ]), ALU.is_equal).then_inc(S["mask_keep"].sem, 1)
                        dv.wait_ge(S["mask_keep"].sem, S["mask_keep"].base + r + 1)
                        out_ = maskk[:, r * w:(r + 1) * w, :]
                        nc.vector.tensor_scalar(out_, keep, 1.0, -NEG, ALU.subtract, ALU.mult).then_inc(S["mask_neg"].sem, 1)
                        dv.wait_ge(S["mask_neg"].sem, S["mask_neg"].base + r + 1)
                        if which == "cell":
                            nc.vector.tensor_tensor(out_, out_, causal[:, :].unsqueeze(1).to_broadcast([P, w, SEQ]), ALU.add).then_inc(S["mask_made"].sem, 1)
                        else:
                            nc.vector.tensor_copy(keep, keep).then_inc(S["mask_made"].sem, 1)
            S.advance(dict(mask_rows=32 * n + (16 if which == "cell" else 0), mask_made=n, mask_neg=n, mask_keep=n))
            mem.close()

        def source_stats(norm):
            n = 8
            w = TILES // n
            mem = Memory(nc, "stats_" + norm)
            chunk = mem.sb("chunk", [P, 2, w, D])
            sq = mem.sb("sq", [P, 2, w, D])
            bn = mem.sb("bn", [P, w, 6])
            with nc.Block() as block:
                @block.sync
                def _(sp):
                    for r in range(n):
                        if after(2 * (r - 1)):
                            sp.wait_ge((S["squared"] if norm == "rms" else S["chunk_used"]).sem, (S["squared"] if norm == "rms" else S["chunk_used"]).base + 2 * (r - 1))
                        sp.dma_start(chunk[:, r % 2, :, :], io["ctx"][r * w * P:(r + 1) * w * P, :].rearrange("(t p) d -> p t d", p=P)).then_inc((S["chunk_in1"] if r % 2 else S["chunk_in"]).sem, 16)

                @block.vector
                def _(dv):
                    k = 0
                    for r in range(n):
                        for src_, st in ((X[:, r * w:(r + 1) * w, :], stat), (chunk[:, r % 2, :, :], stat2)):
                            if st is stat2 and norm == "ln":
                                dv.wait_ge((S["chunk_in1"] if r % 2 else S["chunk_in"]).sem, (S["chunk_in1"] if r % 2 else S["chunk_in"]).base + 16 * (r // 2 + 1))
                            dst = st[:, r * w:(r + 1) * w, :]
                            if norm == "ln":
                                if after(k):
                                    dv.wait_ge(S["chunk_used"].sem, S["chunk_used"].base + k)
                            k += 1
                            if norm == "rms":
                                dv.wait_ge(S["squared"].sem, S["squared"].base + k)
                                nc.vector.tensor_reduce(dst.rearrange("p t h -> p (t h)"), sq[:, (k - 1) % 2, :, :].rearrange("p t (h d) -> p (t h) d", d=HD), AX, ALU.add).then_inc(S["chunk_used"].sem, 1)
                            else:
                                for j in range(w):
                                    m = nc.vector.bn_stats(bn[:, j, :], src_[:, j, :])
                                m.then_inc(S["squared"].sem, 1)
                                dv.wait_ge(S["squared"].sem, S["squared"].base + k)
                                for j in range(w):
                                    m = nc.vector.bn_aggr(dst[:, j, 0:2], bn[:, j, :])
                                m.then_inc(S["chunk_used"].sem, 1)
                    dv.wait_ge(S["chunk_used"].sem, S["chunk_used"].base + 2 * n)
                    for st, ready in ((stat, S["stat_var"]), (stat2, S["stat2_var"])):
                        v = st[:, :, :] if norm == "rms" else st[:, :, 1:2]
                        nc.vector.tensor_scalar(v, v, 1.0 / HD if norm == "rms" else 1.0, RMS_EPS if norm == "rms" else LN_EPS, ALU.mult, ALU.add).then_inc(ready.sem, 1)
                    for st, ready, n_ in ((stat, S["stat_root"], 1), (stat2, S["stat2_root"], 1)):
                        v = st[:, :, :] if norm == "rms" else st[:, :, 1:2]
                        dv.wait_ge(ready.sem, ready.base + 1)
                        nc.vector.reciprocal(v, v)

                @block.scalar
                def _(act):
                    if norm == "rms":
                        for k in range(2 * n):
                            r = k // 2
                            if k % 2:
                                act.wait_ge((S["chunk_in1"] if r % 2 else S["chunk_in"]).sem, (S["chunk_in1"] if r % 2 else S["chunk_in"]).base + 16 * (r // 2 + 1))
                            if after(k - 1):
                                act.wait_ge(S["chunk_used"].sem, S["chunk_used"].base + k - 1)
                            src_ = chunk[:, r % 2, :, :] if k % 2 else X[:, r * w:(r + 1) * w, :]
                            nc.scalar.activation(sq[:, k % 2, :, :], src_, ACT.Square).then_inc(S["squared"].sem, 1)
                    for st, ready, done in ((stat, S["stat_var"], S["stat_root"]), (stat2, S["stat2_var"], S["stat2_root"])):
                        v = st[:, :, :] if norm == "rms" else st[:, :, 1:2]
                        act.wait_ge(ready.sem, ready.base + 1)
                        nc.scalar.activation(v, v, ACT.Sqrt).then_inc(done.sem, 1)
            S.advance(dict(chunk_used=2 * n, chunk_in=8 * n, chunk_in1=8 * n, squared=2 * n, stat_var=1, stat2_var=1, stat_root=1, stat2_root=1))
            mem.close()

        def fold_norms():
            mats = [("L3xq", "L3gq", "L3aq", "L3bq"), ("L3xqs", "L3gq", "L3aq", "L3bqs"), ("L3xk", "L3gk", "L3ak", "L3bk"),
                    ("L3xks", "L3gk", "L3ak", "L3bks"), ("L3xv", "L3gv", "L3av", None), ("L3xo", "L3go", "L3ao", None)]
            mem = Memory(nc, "fold")
            psF, bvb = mem.pb("psF", [P, 512]), mem.sb("bvb", [P, D])
            with nc.Block() as block:
                @block.vector
                def _(dv):
                    for n, (w, g_, _, _) in enumerate(mats):
                        nc.vector.tensor_scalar(wp[:, n, :], Wm(w), C(g_), None, ALU.mult)
                    for n, b in enumerate(("L3av", "L3ao", "L3bv")):
                        dst = colb[:, n, :] if n < 2 else bvb[:, :]
                        m = nc.vector.tensor_scalar(dst, ident, 0.0, C(b), ALU.mult, ALU.add)
                    m.then_inc(S["prep"].sem, 1)
                    dv.wait_ge(S["prep_pe"].sem, S["prep_pe"].base + 1)
                    for n, (_, _, _, b) in enumerate(mats[:4]):
                        nc.vector.tensor_scalar(colx[:, n:n + 1], psF[:, n:n + 1], C(b), None, ALU.add)
                    nc.vector.tensor_copy(rowx[:, 1, :], psF[:, 128:256])
                    nc.vector.tensor_tensor(rowx[:, 0, :], psF[:, 256:384], R("L3b"), ALU.add)

                @block.tensor
                def _(pe):
                    pe.wait_ge(S["prep"].sem, S["prep"].base + 1)
                    for n, (w, _, b, _) in enumerate(mats[:4]):
                        nc.tensor.matmul(psF[:, n:n + 1], Wm(w), C(b), start=True, stop=True)
                    nc.tensor.matmul(psF[:, 128:256], colb[:, 0, :], Wm("L3xv"), start=True, stop=False)
                    nc.tensor.matmul(psF[:, 128:256], bvb[:, :], ident, start=False, stop=True)
                    nc.tensor.matmul(psF[:, 256:384], colb[:, 1, :], Wm("L3xo"), start=True, stop=True).then_inc(S["prep_pe"].sem, 1)
            S.advance(dict(prep=1, prep_pe=1))
            mem.close()

        TB = BATCH // P

        class Bat:

            def __init__(self, i, c):
                self.i, self.c, self.u = i, c, c % 2
                self.ok = i is not None or 0 <= c < NBATCH
                self.b = c if i is None else i * 2 + c
                self.t0 = self.b * TB

            def __sub__(self, k):
                return Bat(self.i, self.c - k)

            def tiles(self):
                return bass.ds(self.b * TB, TB)

        def batches(eng, slot, depth, ahead=0):
            first = 2
            turns = (NBATCH - first) // 2 - ahead
            for c in range(first):
                slot(Bat(None, c))
            with eng.Fori(0, turns) as i:
                for c in range(2):
                    slot(Bat(i, first + c))
            for c in range(first + 2 * turns, NBATCH + depth):
                slot(Bat(None, c))

        def packed_experts(L, NCH, W1, W2, XS, XT, SG, G, ACC, st, ag, rt, psX, psY, psG, psO, gate3, G3S, G3T, SEL):
            with nc.Block() as block:
                @block.gpsimd
                def _(g):
                    def slot(B):
                        if B.ok:
                            if after(B.b - 1):
                                g.wait_ge(S["gt_turned"].sem, S["gt_turned"].base + B.b - 1)
                            nc.gpsimd.tensor_copy(XS[:, B.u], X[:, B.tiles(), :])
                            nc.gpsimd.tensor_copy(G3S[:, B.u], gate3[:, B.tiles(), :, :].rearrange("p t k e -> p t (k e)")).then_inc(S["xs"].sem, 1)
                        if (B - 1).ok:
                            row_root(B - 1, ag, rt)
                    batches(g, slot, 1)

                @block.tensor
                def _(pe):
                    def turn_rows(B):
                        pe.wait_ge(S["xs"].sem, S["xs"].base + B.b + 1)
                        if after(B.b):
                            pe.wait_ge(S["gt_out"].sem, S["gt_out"].base + B.b)
                        for j in range(TB):
                            m = nc.tensor.transpose(psX[:, j * P:(j + 1) * P], XS[:, B.u, j, :], ident)
                        m.then_inc(S["turned"].sem, 1)

                    def turn_gates(B):
                        pe.wait_ge(S["xt_out"].sem, S["xt_out"].base + B.b + 1)
                        for j in range(TB):
                            m = nc.tensor.transpose(psX[0:24, j * P:(j + 1) * P], G3S[:, B.u, j, :], ident)
                        m.then_inc(S["gt_turned"].sem, 1)

                    def slot(B):
                        if B.c == 0 and B.i is None:
                            turn_rows(B)
                            turn_gates(B)
                        for c in range(NCH + 1):
                            n = B.b * NCH + c
                            if c < NCH:
                                if c == 0:
                                    pe.wait_ge(S["gt_out"].sem, S["gt_out"].base + B.b + 1)
                                yb = 0 if (NCH * B.u + c) % 2 == 0 else 1
                                if after(n - 1):
                                    pe.wait_ge(S["g_ready"].sem, S["g_ready"].base + n - 1)
                                nc.tensor.matmul(psY[:, yb, 0, :], W1[:, 0, c, :], XT[:, B.u, :], start=True, stop=True).then_inc(S["hidden"].sem, 1)
                                nc.tensor.matmul(psG[:, yb, :], SEL[:, c, :], G3T[:, B.u, :], start=True, stop=True)
                                nc.tensor.matmul(psY[:, yb, 1, :], W1[:, 1, c, :], XT[:, B.u, :], start=True, stop=True).then_inc(S["hidden2"].sem, 1)
                            if c:
                                k = c - 1
                                gb = 0 if (NCH * B.u + k) % 2 == 0 else 1
                                pe.wait_ge(S["g_ready"].sem, S["g_ready"].base + n)
                                if k == 0:
                                    if after(B.b):
                                        pe.wait_ge(S["o_added"].sem, S["o_added"].base + B.b)
                                for j in range(TB):
                                    m = nc.tensor.matmul(psO[:, j, :], G[:, gb, 0, j * P:(j + 1) * P], W2[:, k, :], start=k == 0 and j == 0, stop=k == NCH - 1, skip_group_check=True)
                                m.then_inc(S["o_done"].sem, 1)
                            if c in (4, 6):
                                nxt = Bat(B.i, B.c + 1)
                                if nxt.ok:
                                    (turn_rows if c == 4 else turn_gates)(nxt)
                    batches(pe, slot, 0, 1)

                @block.scalar
                def _(act):
                    def rows(B):
                        act.wait_ge(S["turned"].sem, S["turned"].base + B.b + 1)
                        nc.scalar.activation(XT[:, B.u, :], psX[:, :], ACT.Copy).then_inc(S["xt_out"].sem, 1)

                    def gates(B):
                        act.wait_ge(S["gt_turned"].sem, S["gt_turned"].base + B.b + 1)
                        nc.scalar.activation(G3T[:, B.u, :], psX[0:24, :], ACT.Copy).then_inc(S["gt_out"].sem, 1)

                    def slot(B):
                        if B.c == 0 and B.i is None:
                            rows(B)
                            gates(B)
                        for c in range(NCH):
                            n = B.b * NCH + c
                            yb = 0 if (NCH * B.u + c) % 2 == 0 else 1
                            act.wait_ge(S["hidden"].sem, S["hidden"].base + n + 1)
                            if after(n - 1):
                                act.wait_ge(S["g_ready"].sem, S["g_ready"].base + n - 1)
                            nc.scalar.activation(SG[:, yb, :], psY[:, yb, 0, :], ACT.Silu).then_inc(S["silu"].sem, 1)
                            if c in (4, 6):
                                nxt = Bat(B.i, B.c + 1)
                                if nxt.ok:
                                    (rows if c == 4 else gates)(nxt)
                    batches(act, slot, 0, 1)

                @block.vector
                def _(dv):
                    def slot(B):
                        A = B - 1
                        if B.ok:
                            for c in range(NCH):
                                n = B.b * NCH + c
                                yb = 0 if (NCH * B.u + c) % 2 == 0 else 1
                                dv.wait_ge(S["silu"].sem, S["silu"].base + n + 1)
                                dv.wait_ge(S["hidden2"].sem, S["hidden2"].base + n + 1)
                                nc.vector.tensor_tensor(SG[:, yb, :], SG[:, yb, :], psY[:, yb, 1, :], ALU.mult).then_inc(S["product"].sem, 1)
                                dv.wait_ge(S["product"].sem, S["product"].base + n + 1)
                                if after(n - 1):
                                    dv.wait_ge(S["o_done"].sem, S["o_done"].base + n - 1)
                                nc.vector.tensor_tensor(G[:, yb, 0, :], SG[:, yb, :], psG[:, yb, :], ALU.mult).then_inc(S["g_ready"].sem, 1)
                                if c == 0 and A.ok:
                                    dv.wait_ge(S["o_done"].sem, S["o_done"].base + A.b * NCH + NCH)
                                    if after(A.b - 1):
                                        dv.wait_ge(S["out_rows"].sem, S["out_rows"].base + A.b - 1)
                                    nc.vector.tensor_tensor(ACC[:, A.u], psO[:, :, :], X[:, A.tiles(), :], ALU.add).then_inc(S["o_added"].sem, 1)
                                    dv.wait_ge(S["o_added"].sem, S["o_added"].base + A.b + 1)
                                    row_stats(A, ACC, st, ag)
                                if c == 3 and A.ok:
                                    row_out(A, ACC, ag, rt)
                        elif A.ok:
                            dv.wait_ge(S["o_done"].sem, S["o_done"].base + A.b * NCH + NCH)
                            dv.wait_ge(S["out_rows"].sem, S["out_rows"].base + A.b - 1)
                            nc.vector.tensor_tensor(ACC[:, A.u], psO[:, :, :], X[:, A.tiles(), :], ALU.add).then_inc(S["o_added"].sem, 1)
                            dv.wait_ge(S["o_added"].sem, S["o_added"].base + A.b + 1)
                            row_stats(A, ACC, st, ag)
                            row_out(A, ACC, ag, rt)
                    batches(dv, slot, 1)
            S.advance(dict.fromkeys(("xs", "turned", "xt_out", "gt_turned", "gt_out", "o_added", "bn", "stats", "var_eps", "rstd", "out_rows"), NBATCH))
            S.advance(dict.fromkeys(("hidden", "hidden2", "silu", "product", "g_ready", "o_done"), NBATCH * NCH))

        def moe(L, ne, fc, fw, gated, w1, w2, extra, XO=None):
            mem = Memory(nc, L)
            NCH = ne * fc * fw // P
            W1 = mem.sb("W1", [P, 2, NCH, P] if gated else [P, ne, fc * fw])
            W2 = mem.sb("W2", [P, NCH, D] if gated else [fw, ne, fc, D])
            RW = mem.sb("RW", [P, 16])
            RBI = mem.sb("RBI", [P, 16])
            B1 = mem.sb("B1", [P, ne, fc])
            B2 = mem.sb("B2", [ne, D])
            LG = mem.sb("LG", [P, TILES, 16])
            gate = mem.sb("gate", [P, TILES, ne])
            XS = mem.sb("XS", [P, 2, TB, D])
            XT = mem.sb("XT", [P, 2, BATCH])
            SG = mem.sb("SG", [P, 2, BATCH])
            G = mem.sb("G", [P, 2, 2, BATCH])
            ACC = mem.sb("ACC", [P, 2, TB, D])
            GS = mem.sb("GS", [P, 2, TB, ne])
            GT = mem.sb("GT", [ne, 2, BATCH])
            st, ag, rt = mem.sb("st", [P, 2, TB, 6]), mem.sb("ag", [P, 2, TB, 2]), mem.sb("rt", [P, 2, 2, TB])
            t1, t2, t3, t4 = (mem.sb(f"t{n}", [P, TILES, 8]) for n in range(4))
            psX = mem.pb("psX", [P, BATCH])
            psY = mem.pb("psY", [P, 2, 2, BATCH])
            if gated:
                psG = mem.pb("psG", [P, 2, BATCH])
                psO = mem.pb("psO", [P, TB, D])
                psL = psO
                gate3 = mem.sb("gate3", [P, TILES, 3, ne])
                G3S, G3T = mem.sb("G3S", [P, 2, TB, 3 * ne]), mem.sb("G3T", [3 * ne, 2, BATCH], BF16)
                SEL32, SEL = mem.sb("SEL32", [3 * ne, NCH, P]), mem.sb("SEL", [3 * ne, NCH, P], BF16)
                part = mem.sb("part", [P, TILES, ne], BF16)
            else:
                psL = mem.pb("psL", [P, TB, 128])
                psO = mem.pb("psO", [P, 2, TB, D])
            nl = 8 if gated else 12
            steps = ne * fc

            with nc.Block() as block:
                @block.sync
                def _(sp):
                    ld = [(W1[:, :, :, :] if gated else W1[:, :, :], io[w1]), (W2[:, :, :] if gated else W2[:, :, :, :], io[w2]), (RW[:, 0:nl], io[extra["rw"]])]
                    if not gated:
                        ld += [(B1[:, :, :], io[extra["b1"]]), (B2[:, :], io[extra["b2"]]), (RBI[:, 0:nl], io[extra["rb"]].partition_broadcast(P))]
                    else:
                        ld += [(SEL32[:, :, :], io["sel"])]
                    for d, s_ in ld:
                        sp.dma_start(d, s_).then_inc(S["weights_in"].sem, 16)
                    sp.wait_ge(S["weights_in"].sem, S["weights_in"].base + 16 * len(ld))
                S.advance(dict(weights_in=16 * (6 if not gated else 4)))

            with nc.Block() as block:
                @block.gpsimd
                def _(g):
                    def slot(B):
                        if after(B.b - 1):
                            g.wait_ge(S["turned"].sem, S["turned"].base + B.b - 1)
                        nc.gpsimd.tensor_copy(XS[:, B.u], X[:, B.tiles(), :]).then_inc(S["xs"].sem, 1)
                    batches(g, slot, 0)

                @block.tensor
                def _(pe):
                    def slot(B):
                        pe.wait_ge(S["xs"].sem, S["xs"].base + B.b + 1)
                        if after(B.b):
                            pe.wait_ge(S["xt_out"].sem, S["xt_out"].base + B.b)
                        for j in range(TB):
                            m = nc.tensor.transpose(psX[:, j * P:(j + 1) * P], XS[:, B.u, j, :], ident)
                        m.then_inc(S["turned"].sem, 1)
                        pe.wait_ge(S["xt_out"].sem, S["xt_out"].base + B.b + 1)
                        if after(B.b):
                            pe.wait_ge(S["logits_out"].sem, S["logits_out"].base + B.b)
                        for j in range(TB):
                            m = nc.tensor.matmul(psL[:, j, 0:nl], XT[:, B.u, j * P:(j + 1) * P], RW[:, 0:nl], start=True, stop=True)
                        m.then_inc(S["logits"].sem, 1)
                    batches(pe, slot, 0)

                @block.scalar
                def _(act):
                    def slot(B):
                        act.wait_ge(S["turned"].sem, S["turned"].base + B.b + 1)
                        if after(B.b - 1):
                            act.wait_ge(S["logits"].sem, S["logits"].base + B.b - 1)
                        nc.scalar.activation(XT[:, B.u, :], psX[:, :], ACT.Copy).then_inc(S["xt_out"].sem, 1)
                    batches(act, slot, 0)

                @block.vector
                def _(dv):
                    def slot(B):
                        dv.wait_ge(S["logits"].sem, S["logits"].base + B.b + 1)
                        dst = LG[:, B.tiles(), 0:nl]
                        if gated:
                            nc.vector.tensor_copy(dst, psL[:, :, 0:nl]).then_inc(S["logits_out"].sem, 1)
                        else:
                            nc.vector.tensor_tensor(dst, psL[:, :, 0:nl], RBI[:, 0:nl].unsqueeze(1).to_broadcast([P, TB, nl]), ALU.add).then_inc(S["logits_out"].sem, 1)
                    batches(dv, slot, 0)
            S.advance(dict.fromkeys(("xs", "turned", "xt_out", "logits", "logits_out"), NBATCH))

            T_ = [P, TILES]
            with nc.Block() as block:
                cnt = [0]

                @block.vector
                def _(dv):
                    def link(ins):
                        ins.then_inc(S["route"].sem, 1)
                        cnt[0] += 1
                        dv.wait_ge(S["route"].sem, S["route"].base + cnt[0])
                    b3 = lambda ap, n: ap.unsqueeze(2).to_broadcast([P, TILES, n])
                    if gated:
                        lg = LG[:, :, 0:8]
                        mx_, sec = t2[:, :, 0], t2[:, :, 1]
                        link(nc.vector.tensor_reduce(mx_, lg, AX, ALU.max))
                        link(nc.vector.tensor_tensor(t1[:, :, :], lg, b3(mx_, 8), ALU.subtract))
                        link(nc.vector.tensor_scalar(t3[:, :, :], t1[:, :, :], 0.0, NEG, ALU.is_ge, ALU.mult))
                        link(nc.vector.tensor_tensor(t3[:, :, :], t3[:, :, :], t1[:, :, :], ALU.add))
                        link(nc.vector.tensor_reduce(sec, t3[:, :, :], AX, ALU.max))
                        link(nc.vector.tensor_tensor(t3[:, :, :], t1[:, :, :], b3(sec, 8), ALU.is_ge))
                        dv.wait_ge(S["route_exp"].sem, S["route_exp"].base + 1)
                        link(nc.vector.tensor_reduce(mx_, t4[:, :, :], AX, ALU.add))
                        link(nc.vector.reciprocal(mx_, mx_))
                        link(nc.vector.tensor_tensor(t3[:, :, :], t3[:, :, :], t4[:, :, :], ALU.mult))
                        link(nc.vector.tensor_tensor(gate[:, :, :], t3[:, :, :], b3(mx_, 8), ALU.mult))
                        for k in range(3):
                            link(nc.vector.tensor_copy(part[:, :, :], gate[:, :, :]))
                            link(nc.vector.tensor_copy(gate3[:, :, k, :], part[:, :, :]))
                            if k < 2:
                                link(nc.vector.tensor_tensor(gate[:, :, :], gate[:, :, :], gate3[:, :, k, :], ALU.subtract))
                        link(nc.vector.tensor_copy(SEL[:, :, :], SEL32[:, :, :]))
                    else:
                        gl, el = LG[:, :, 0:4], LG[:, :, 4:12]
                        mg, sg_ = t2[:, :, 0], t2[:, :, 1]
                        m2, s2 = t2[:, :, 4:8], t3[:, :, 0:4]
                        pair = lambda ap: ap.rearrange("p t (g e) -> p (t g) e", e=2)
                        flat = lambda ap: ap.rearrange("p t g -> p (t g)")
                        link(nc.vector.tensor_reduce(mg, gl, AX, ALU.max))
                        el4 = el.rearrange("p t (g e) -> p t g e", e=2)
                        link(nc.vector.tensor_tensor(m2, el4[:, :, :, 0], el4[:, :, :, 1], ALU.max))
                        link(nc.vector.tensor_tensor(t1[:, :, 0:4], gl, b3(mg, 4), ALU.subtract))
                        for j in range(2):
                            dst = t4[:, :, :].rearrange("p t (g e) -> p t g e", e=2)[:, :, :, j]
                            link(nc.vector.tensor_tensor(dst, el4[:, :, :, j], m2, ALU.subtract))
                        link(nc.vector.tensor_scalar(gate[:, :, :], t4[:, :, :], 0.0, None, ALU.is_ge))
                        link(nc.vector.tensor_scalar(t3[:, :, 4:8], t1[:, :, 0:4], 0.0, None, ALU.is_ge))
                        dv.wait_ge(S["route_exp"].sem, S["route_exp"].base + 1)
                        link(nc.vector.tensor_reduce(sg_, t1[:, :, 0:4], AX, ALU.add))
                        t44 = t4[:, :, :].rearrange("p t (g e) -> p t g e", e=2)
                        link(nc.vector.tensor_tensor(s2, t44[:, :, :, 0], t44[:, :, :, 1], ALU.add))
                        link(nc.vector.tensor_tensor(s2, s2, b3(sg_, 4), ALU.mult))
                        link(nc.vector.reciprocal(s2, s2))
                        link(nc.vector.tensor_tensor(s2, s2, t3[:, :, 4:8], ALU.mult))
                        for j in range(2):
                            dst = gate[:, :, :].rearrange("p t (g e) -> p t g e", e=2)[:, :, :, j]
                            link(nc.vector.tensor_tensor(dst, dst, s2, ALU.mult))

                @block.scalar
                def _(act):
                    if gated:
                        act.wait_ge(S["route"].sem, S["route"].base + 2)
                        nc.scalar.activation(t4[:, :, :], t1[:, :, :], ACT.Exp).then_inc(S["route_exp"].sem, 1)
                    else:
                        act.wait_ge(S["route"].sem, S["route"].base + 7)
                        nc.scalar.activation(t4[:, :, :], t4[:, :, :], ACT.Exp)
                        nc.scalar.activation(t1[:, :, 0:4], t1[:, :, 0:4], ACT.Exp).then_inc(S["route_exp"].sem, 1)
                S.advance(dict(route_exp=1))
            S.advance(dict(route=cnt[0]))

            if gated:
                packed_experts(L, NCH, W1, W2, XS, XT, SG, G, ACC, st, ag, rt, psX, psY, psG, psO, gate3, G3S, G3T, SEL)
                mem.close()
                return

            with nc.Block() as block:
                @block.gpsimd
                def _(g):
                    def slot(B):
                        if B.ok:
                            if after(B.b - 1):
                                g.wait_ge(S["turned"].sem, S["turned"].base + B.b - 1)
                            if after(B.b - 1):
                                g.wait_ge(S["gt_turned"].sem, S["gt_turned"].base + B.b - 1)
                            nc.gpsimd.tensor_copy(GS[:, B.u], gate[:, B.tiles(), :])
                            nc.gpsimd.tensor_copy(XS[:, B.u], X[:, B.tiles(), :]).then_inc(S["xs"].sem, 1)
                        A = B - 1
                        if A.ok:
                            g.wait_ge(S["stats"].sem, S["stats"].base + 2 * A.b + 1)
                            nc.gpsimd.tensor_tensor(rt[:, A.u, 0, :], ag[:, A.u, :, 1], eps[:, 0:TB], ALU.add).then_inc(S["var_eps"].sem, 1)
                            g.wait_ge(S["var_eps"].sem, S["var_eps"].base + 2 * A.b + 1)
                            nc.gpsimd.tensor_tensor(rt[:, A.u, 1, :], rt[:, A.u, 0, :], half[:, 0:TB], ALU.pow).then_inc(S["rstd"].sem, 1)
                            k = 2
                            g.wait_ge(S["stats"].sem, S["stats"].base + k * A.b + k)
                            if after(A.b - 1):
                                g.wait_ge(S["out_rows"].sem, S["out_rows"].base + A.b - 1)
                            nc.gpsimd.tensor_tensor(rt[:, A.u, 0, :], ag[:, A.u, :, 1], eps[:, 0:TB], ALU.add).then_inc(S["var_eps"].sem, 1)
                            g.wait_ge(S["var_eps"].sem, S["var_eps"].base + k * A.b + k)
                            nc.gpsimd.tensor_tensor(rt[:, A.u, 1, :], rt[:, A.u, 0, :], half[:, 0:TB], ALU.pow).then_inc(S["rstd"].sem, 1)
                    batches(g, slot, 1)

                @block.tensor
                def _(pe):
                    def products(B, m):
                        n = B.b * (ne + 1) + m
                        pe.wait_ge(S["g_ready"].sem, S["g_ready"].base + B.b * steps + (m + 1) * fc)
                        if after(n - 1):
                            pe.wait_ge(S["o_added"].sem, S["o_added"].base + n - 1)
                        ob = (m + B.u) % 2
                        for j in range(TB):
                            for c in range(fc):
                                i_ = nc.tensor.matmul(psO[:, ob, j, :], G[:, m % 2, c, j * P:(j + 1) * P], W2[:, m, c, :], start=c == 0, stop=c == fc - 1)
                        i_.then_inc(S["o_done"].sem, 1)

                    def turn_rows(B):
                        pe.wait_ge(S["xs"].sem, S["xs"].base + B.b + 1)
                        if after(B.b):
                            pe.wait_ge(S["xt_out"].sem, S["xt_out"].base + B.b)
                        for j in range(TB):
                            i_ = nc.tensor.transpose(psX[:, j * P:(j + 1) * P], XS[:, B.u, j, :], ident)
                        i_.then_inc(S["turned"].sem, 1)

                    def slot(B):
                        if B.c == 0 and B.i is None:
                            turn_rows(B)
                        for m in range(ne):
                            if m == 6 and Bat(B.i, B.c + 1).ok:
                                turn_rows(Bat(B.i, B.c + 1))
                            for c in range(fc):
                                if m == 0 and c == 0:
                                    pe.wait_ge(S["xt_out"].sem, S["xt_out"].base + B.b + 1)
                                n = B.b * steps + m * fc + c
                                yb = (m * fc + c) % 2
                                if after(n - 1):
                                    pe.wait_ge(S["g_ready"].sem, S["g_ready"].base + n - 1)
                                i_ = nc.tensor.matmul(psY[0:fw, yb, 0, :], W1[:, m, c * fw:(c + 1) * fw], XT[:, B.u, :], start=True, stop=True)
                                i_.then_inc(S["hidden"].sem, 1)
                            if m == ne - 1:
                                if after(B.b):
                                    pe.wait_ge(S["gt_out"].sem, S["gt_out"].base + B.b)
                                for j in range(TB):
                                    i_ = nc.tensor.transpose(psL[0:ne, j, :], GS[:, B.u, j, :], ident)
                                i_.then_inc(S["gt_turned"].sem, 1)
                            if m:
                                products(B, m - 1)
                        products(B, ne - 1)
                        pe.wait_ge(S["gt_out"].sem, S["gt_out"].base + B.b + 1)
                        pe.wait_ge(S["o_added"].sem, S["o_added"].base + B.b * (ne + 1) + ne - 1)
                        for j in range(TB):
                            i_ = nc.tensor.matmul(psO[:, B.u, j, :], GT[:, B.u, j * P:(j + 1) * P], B2[:, :], start=True, stop=True)
                        i_.then_inc(S["o_done"].sem, 1)
                    batches(pe, slot, 0, 1)

                @block.scalar
                def _(act):
                    def rows(B):
                        act.wait_ge(S["turned"].sem, S["turned"].base + B.b + 1)
                        nc.scalar.activation(XT[:, B.u, :], psX[:, :], ACT.Copy).then_inc(S["xt_out"].sem, 1)

                    def slot(B):
                        if B.c == 0 and B.i is None:
                            rows(B)
                        for m in range(ne):
                            if m == 6 and Bat(B.i, B.c + 1).ok:
                                rows(Bat(B.i, B.c + 1))
                            for c in range(fc):
                                n = B.b * steps + m * fc + c
                                yb = (m * fc + c) % 2
                                act.wait_ge(S["hidden"].sem, S["hidden"].base + n + 1)
                                if after(B.b * (ne + 1) + m - 1):
                                    act.wait_ge(S["o_done"].sem, S["o_done"].base + B.b * (ne + 1) + m - 1)
                                nc.scalar.activation(G[:, m % 2, c, :], psY[0:fw, yb, 0, :], ACT.Relu, bias=B1[:, m, c:c + 1]).then_inc(S["g_ready"].sem, 1)
                        act.wait_ge(S["gt_turned"].sem, S["gt_turned"].base + B.b + 1)
                        if after((B.b - 1) * (ne + 1)):
                            act.wait_ge(S["o_done"].sem, S["o_done"].base + (B.b - 1) * (ne + 1))
                        nc.scalar.activation(GT[:, B.u, :], psL[0:ne, :, :].rearrange("p t k -> p (t k)"), ACT.Copy).then_inc(S["gt_out"].sem, 1)
                    batches(act, slot, 0, 1)

                @block.vector
                def _(dv):
                    def slot(B):
                        if B.ok:
                            for m in range(ne + 1):
                                if m == 2:
                                    tail(B - 1)
                                if m:
                                    add(B, m - 1)
                            e = B.b * (ne + 1) + ne
                            dv.wait_ge(S["o_done"].sem, S["o_done"].base + e + 1)
                            dv.wait_ge(S["o_added"].sem, S["o_added"].base + e)
                            nc.vector.tensor_tensor(ACC[:, B.u], ACC[:, B.u], psO[:, B.u], ALU.add).then_inc(S["o_added"].sem, 1)
                            dv.wait_ge(S["o_added"].sem, S["o_added"].base + e + 1)
                            stats(B, 0)
                        else:
                            tail(B - 1)

                    def add(B, m):
                        e = B.b * (ne + 1) + m
                        ob = (m + B.u) % 2
                        dv.wait_ge(S["o_done"].sem, S["o_done"].base + e + 1)
                        if after(e):
                            dv.wait_ge(S["o_added"].sem, S["o_added"].base + e)
                        if m == 0:
                            if after(B.b - 1):
                                dv.wait_ge(S["out_rows"].sem, S["out_rows"].base + B.b - 1)
                        for j in range(TB):
                            t_ = bass.ds(B.b * TB + j, 1)
                            base_ = X[:, t_, :].rearrange("p a d -> p (a d)") if m == 0 else ACC[:, B.u, j, :]
                            i_ = nc.vector.scalar_tensor_tensor(ACC[:, B.u, j, :], psO[:, ob, j, :], gate[:, t_, m:m + 1].rearrange("p a e -> p (a e)"), base_, ALU.mult, ALU.add)
                        i_.then_inc(S["o_added"].sem, 1)

                    def stats(B, second):
                        k = 2
                        n = k * B.b + second
                        if second == 0:
                            dv.wait_ge(S["o_added"].sem, S["o_added"].base + (B.b + 1) * (ne + 1))
                        for j in range(TB):
                            i_ = nc.vector.bn_stats(st[:, B.u, j, :], ACC[:, B.u, j, :])
                        i_.then_inc(S["bn"].sem, 1)
                        dv.wait_ge(S["bn"].sem, S["bn"].base + n + 1)
                        pace(nc.vector, S)
                        for j in range(TB):
                            i_ = nc.vector.bn_aggr(ag[:, B.u, j, :], st[:, B.u, j, :])
                        i_.then_inc(S["stats"].sem, 1)

                    def tail(A):
                        if not A.ok:
                            return
                        dv.wait_ge(S["rstd"].sem, S["rstd"].base + 2 * A.b + 1)
                        for j in range(TB):
                            i_ = nc.vector.tensor_scalar(ACC[:, A.u, j, :], ACC[:, A.u, j, :], ag[:, A.u, j, 0:1], rt[:, A.u, 1, j:j + 1], ALU.subtract, ALU.mult)
                        i_.then_inc(S["own"].sem, 1)
                        k = 3 * A.b
                        dv.wait_ge(S["own"].sem, S["own"].base + k + 1)
                        nc.vector.tensor_tensor(ACC[:, A.u], ACC[:, A.u], R("g2").unsqueeze(1).to_broadcast([P, TB, D]), ALU.mult).then_inc(S["own"].sem, 1)
                        dv.wait_ge(S["own"].sem, S["own"].base + k + 2)
                        nc.vector.tensor_tensor(ACC[:, A.u], ACC[:, A.u], XO[:, A.tiles(), :], ALU.add).then_inc(S["own"].sem, 1)
                        dv.wait_ge(S["own"].sem, S["own"].base + k + 3)
                        stats(A, 1)
                        dv.wait_ge(S["rstd"].sem, S["rstd"].base + 2 * A.b + 2)
                        for j in range(TB):
                            i_ = nc.vector.tensor_scalar(X[:, bass.ds(A.b * TB + j, 1), :].rearrange("p a d -> p (a d)"), ACC[:, A.u, j, :],
                                                         ag[:, A.u, j, 0:1], rt[:, A.u, 1, j:j + 1], ALU.subtract, ALU.mult)
                        i_.then_inc(S["out_rows"].sem, 1)
                    batches(dv, slot, 1)
            k = 2
            S.advance(dict.fromkeys(("xs", "turned", "xt_out", "out_rows"), NBATCH))
            S.advance(dict.fromkeys(("hidden", "g_ready"), NBATCH * steps))
            S.advance(dict.fromkeys(("bn", "stats", "var_eps", "rstd"), k * NBATCH))
            S.advance(dict.fromkeys(("o_done", "o_added"), NBATCH * (ne + 1)))
            S.advance(dict(own=3 * NBATCH, gt_turned=NBATCH, gt_out=NBATCH))
            mem.close()

        def row_stats(B, src, st, ag):
            for j in range(TB):
                m = nc.vector.bn_stats(st[:, B.u, j, :], src[:, B.u, j, :])
            m.then_inc(S["bn"].sem, 1)
            nc.vector.wait_ge(S["bn"].sem, S["bn"].base + B.b + 1)
            pace(nc.vector, S)
            for j in range(TB):
                m = nc.vector.bn_aggr(ag[:, B.u, j, :], st[:, B.u, j, :])
            m.then_inc(S["stats"].sem, 1)

        def row_root(B, ag, rt):
            nc.gpsimd.wait_ge(S["stats"].sem, S["stats"].base + B.b + 1)
            nc.gpsimd.tensor_tensor(rt[:, B.u, 0, :], ag[:, B.u, :, 1], eps[:, 0:TB], ALU.add).then_inc(S["var_eps"].sem, 1)
            nc.gpsimd.wait_ge(S["var_eps"].sem, S["var_eps"].base + B.b + 1)
            nc.gpsimd.tensor_tensor(rt[:, B.u, 1, :], rt[:, B.u, 0, :], half[:, 0:TB], ALU.pow).then_inc(S["rstd"].sem, 1)

        def row_out(B, src, ag, rt):
            nc.vector.wait_ge(S["rstd"].sem, S["rstd"].base + B.b + 1)
            for j in range(TB):
                m = nc.vector.tensor_scalar(X[:, bass.ds(B.t0 + j, 1), :].rearrange("p a d -> p (a d)"), src[:, B.u, j, :],
                                            ag[:, B.u, j, 0:1], rt[:, B.u, 1, j:j + 1], ALU.subtract, ALU.mult)
            m.then_inc(S["out_rows"].sem, 1)

        class Micro(Bat):

            def __init__(self, i, c):
                super().__init__(i, c)
                self.e = c // 2 if i is None else i + c // 2
                self.t0 = (self.u * (NBATCH // 2) + self.e) * TB
                self.rows = bass.ds(self.t0, TB)

            def __sub__(self, k):
                return Micro(self.i, self.c - k)

            def __add__(self, k):
                return Micro(self.i, self.c + k)

        def micros(eng, slot, ahead=0):
            turns = NBATCH // 2 - 1 - ahead
            for c in range(-ahead, 2):
                slot(Micro(None, c))
            with eng.Fori(0, turns) as i:
                for c in range(2):
                    slot(Micro(i, 2 + c))
            for c in range(2 + 2 * turns, NBATCH + 1):
                slot(Micro(None, c))

        FLAT = "p t k -> p (t k)"

        def expert_blocks():
            FC = 4
            mem = Memory(nc, "L2f")
            W1, W2 = mem.sb("W1", [P, 2, FC * D]), mem.sb("W2", [P, 2, FC, D])
            B1, B2 = mem.sb("B1", [P, 2, FC]), mem.sb("B2", [P, 8])
            XS, XN = mem.sb("XS", [P, 2, TB, D]), mem.sb("XN", [P, 2, TB, D])
            XT, XNT, XA = mem.sb("XT", [P, 2, BATCH]), mem.sb("XNT", [P, 2, BATCH]), mem.sb("XA", [P, 2, BATCH])
            H = mem.sb("H", [P, 2, FC, BATCH])
            EO, F = mem.sb("EO", [P, 2, BATCH]), mem.sb("F", [P, 2, BATCH])
            RB = mem.sb("RB", [P, 2, TB, D])
            sti, agi, rti = mem.sb("sti", [P, 2, TB, 6]), mem.sb("agi", [P, 2, TB, 2]), mem.sb("rti", [P, 2, 2, TB])
            st, ag, rt = mem.sb("st", [P, 2, TB, 6]), mem.sb("ag", [P, 2, TB, 2]), mem.sb("rt", [P, 2, 2, TB])
            ps = mem.pb("ps", [P, 2, 4, BATCH])

            with nc.Block() as block:
                @block.sync
                def _(sp):
                    sp.dma_start(B2[:, :], io["b2c"]).then_inc(S["weights_in"].sem, 16)
                    sp.wait_ge(S["weights_in"].sem, S["weights_in"].base + 16)
            S.advance(dict(weights_in=16))

            with nc.Block() as block:
                @block.sync
                def _(sp):
                    def slot(B):
                        if B.ok:
                            if after(B.b - 1):
                                sp.wait_ge(S["expert"].sem, S["expert"].base + B.b - 1)
                            got = (S["w_in0"] if B.u == 0 else S["w_in1"]).sem
                            sp.dma_start(B1[:, B.u, :], io["b1c"][bass.ds(B.e * P, P), :]).then_inc(got, 16)
                            sp.dma_start(W1[:, B.u, :], io["w1c"][bass.ds(B.e * D, D), :]).then_inc(got, 16)
                            sp.dma_start(W2[:, B.u, :, :], io["w2c"][bass.ds(B.e * FC * D, FC * D), :].rearrange("(c p) d -> p c d", p=P)).then_inc(got, 16)
                    micros(sp, slot)

                @block.gpsimd
                def _(g):
                    def slot(B):
                        A, N = B - 1, B + 1
                        if N.ok:
                            if after(N.b - 1):
                                g.wait_ge(S["turned"].sem, S["turned"].base + N.b - 1)
                            nc.gpsimd.tensor_copy(XS[:, N.u], X[:, N.rows, :]).then_inc(S["xs"].sem, 1)
                            g.wait_ge(S["in_stats"].sem, S["in_stats"].base + N.b + 1)
                            nc.gpsimd.tensor_tensor(rti[:, N.u, 0, :], agi[:, N.u, :, 1], eps[:, 0:TB], ALU.add).then_inc(S["in_eps"].sem, 1)
                            g.wait_ge(S["in_eps"].sem, S["in_eps"].base + N.b + 1)
                            nc.gpsimd.tensor_tensor(rti[:, N.u, 1, :], rti[:, N.u, 0, :], half[:, 0:TB], ALU.pow).then_inc(S["in_rstd"].sem, 1)
                        if A.ok:
                            if after(A.b - 1):
                                g.wait_ge(S["out_rows"].sem, S["out_rows"].base + A.b - 1)
                            row_root(A, ag, rt)
                    micros(g, slot, 1)

                @block.tensor
                def _(pe):
                    def slot(B):
                        A = B - 1
                        if B.ok:
                            if after(B.b - 1):
                                pe.wait_ge(S["out_rows"].sem, S["out_rows"].base + B.b - 1)
                            pe.wait_ge(S["xs"].sem, S["xs"].base + B.b + 1)
                            for j in range(TB):
                                nc.tensor.transpose(ps[:, B.u, 0, j * P:(j + 1) * P], XS[:, B.u, j, :], ident)
                            pe.wait_ge(S["xn"].sem, S["xn"].base + B.b + 1)
                            for j in range(TB):
                                m = nc.tensor.transpose(ps[:, B.u, 1, j * P:(j + 1) * P], XN[:, B.u, j, :], ident)
                            m.then_inc(S["turned"].sem, 1)
                        if A.ok:
                            pe.wait_ge(S["gelu"].sem, S["gelu"].base + FC * A.b + FC)
                            for c in range(FC):
                                m = nc.tensor.matmul(ps[:, A.u, 2, :], W2[:, A.u, c, :], H[:, A.u, c, :], start=c == 0, stop=c == FC - 1)
                            m.then_inc(S["expert"].sem, 1)
                        if B.ok:
                            pe.wait_ge(S["xnt_out"].sem, S["xnt_out"].base + B.b + 1)
                            nc.tensor.matmul(ps[:, B.u, 2, :], Wm("L2fa"), XNT[:, B.u, :], start=True, stop=True).then_inc(S["attn"].sem, 1)
                        if A.ok:
                            pe.wait_ge(S["expert_out"].sem, S["expert_out"].base + A.b + 1)
                            nc.tensor.matmul(ps[:, A.u, 3, :], Wm("L2fn"), EO[:, A.u, :], start=True, stop=True).then_inc(S["next"].sem, 1)
                        if B.ok:
                            pe.wait_ge(S["xa"].sem, S["xa"].base + B.b + 1)
                            pe.wait_ge((S["w_in0"] if B.u == 0 else S["w_in1"]).sem, (S["w_in0"] if B.u == 0 else S["w_in1"]).base + 48 * (B.e + 1))
                            for c in range(FC):
                                if after(FC * B.b + c - 1 if c > 1 else 0):
                                    pe.wait_ge(S["gelu"].sem, S["gelu"].base + (FC * B.b + c - 1 if c > 1 else 0))
                                nc.tensor.matmul(ps[:, B.u, c % 2, :], W1[:, B.u, c * D:(c + 1) * D], XA[:, B.u, :], start=True, stop=True).then_inc(S["hidden"].sem, 1)
                                if c == 1 and A.ok:
                                    pe.wait_ge(S["next_out"].sem, S["next_out"].base + A.b + 1)
                                    for j in range(TB):
                                        m = nc.tensor.transpose(ps[:, A.u, 2, j * P:(j + 1) * P], F[:, A.u, j * P:(j + 1) * P], ident)
                                    m.then_inc(S["back"].sem, 1)
                        elif A.ok:
                            pe.wait_ge(S["next_out"].sem, S["next_out"].base + A.b + 1)
                            for j in range(TB):
                                m = nc.tensor.transpose(ps[:, A.u, 2, j * P:(j + 1) * P], F[:, A.u, j * P:(j + 1) * P], ident)
                            m.then_inc(S["back"].sem, 1)
                    micros(pe, slot, 1)

                @block.scalar
                def _(act):
                    def slot(B):
                        A = B - 1
                        if B.ok:
                            act.wait_ge(S["turned"].sem, S["turned"].base + B.b + 1)
                            nc.scalar.activation(XNT[:, B.u, :], ps[:, B.u, 1, :], ACT.Identity, scale=C("L2g"), bias=C("L2b")).then_inc(S["xnt_out"].sem, 1)
                        if A.ok:
                            act.wait_ge(S["next"].sem, S["next"].base + A.b + 1)
                            nc.scalar.activation(F[:, A.u, :], ps[:, A.u, 3, :], ACT.Gelu, bias=C("L2fnb")).then_inc(S["next_out"].sem, 1)
                        if B.ok:
                            for c in range(FC):
                                act.wait_ge(S["hidden"].sem, S["hidden"].base + FC * B.b + c + 1)
                                nc.scalar.activation(H[:, B.u, c, :], ps[:, B.u, c % 2, :], ACT.Gelu,
                                                     bias=B1[:, B.u, c:c + 1]).then_inc(S["gelu"].sem, 1)
                    micros(act, slot, 1)

                @block.vector
                def _(dv):
                    def slot(B):
                        A, N = B - 1, B + 1
                        if A.ok:
                            dv.wait_ge(S["expert"].sem, S["expert"].base + A.b + 1)
                            nc.vector.tensor_scalar(EO[:, A.u, :], ps[:, A.u, 2, :], B2[:, bass.ds(A.e, 1)], None, ALU.add).then_inc(S["expert_out"].sem, 1)
                        if B.ok:
                            dv.wait_ge(S["turned"].sem, S["turned"].base + B.b + 1)
                            nc.vector.tensor_scalar(XT[:, B.u, :], ps[:, B.u, 0, :], C("L2fab"), None, ALU.add).then_inc(S["xt_out"].sem, 1)
                            dv.wait_ge(S["attn"].sem, S["attn"].base + B.b + 1)
                            dv.wait_ge(S["xt_out"].sem, S["xt_out"].base + B.b + 1)
                            nc.vector.tensor_tensor(XA[:, B.u, :], ps[:, B.u, 2, :], XT[:, B.u, :], ALU.add).then_inc(S["xa"].sem, 1)
                        if N.ok:
                            if after(N.b - 1):
                                dv.wait_ge(S["xn"].sem, S["xn"].base + N.b - 1)
                            for j in range(TB):
                                m = nc.vector.bn_stats(sti[:, N.u, j, :], X[:, bass.ds(N.t0 + j, 1), :].rearrange("p a d -> p (a d)"))
                            m.then_inc(S["in_bn"].sem, 1)
                            dv.wait_ge(S["in_bn"].sem, S["in_bn"].base + N.b + 1)
                            pace(nc.vector, S)
                            for j in range(TB):
                                m = nc.vector.bn_aggr(agi[:, N.u, j, :], sti[:, N.u, j, :])
                            m.then_inc(S["in_stats"].sem, 1)
                        if A.ok:
                            dv.wait_ge(S["back"].sem, S["back"].base + A.b + 1)
                            if after(A.b - 1):
                                dv.wait_ge(S["out_rows"].sem, S["out_rows"].base + A.b - 1)
                            nc.vector.tensor_tensor(RB[:, A.u], ps[:, A.u, 2, :].rearrange("p (t d) -> p t d", d=D), X[:, A.rows, :], ALU.add).then_inc(S["res"].sem, 1)
                            dv.wait_ge(S["res"].sem, S["res"].base + A.b + 1)
                            row_stats(A, RB, st, ag)
                        if N.ok:
                            if after(N.b - 1):
                                dv.wait_ge(S["turned"].sem, S["turned"].base + N.b - 1)
                            dv.wait_ge(S["in_rstd"].sem, S["in_rstd"].base + N.b + 1)
                            dv.wait_ge(S["xs"].sem, S["xs"].base + N.b + 1)
                            for j in range(TB):
                                m = nc.vector.tensor_scalar(XN[:, N.u, j, :], XS[:, N.u, j, :], agi[:, N.u, j, 0:1], rti[:, N.u, 1, j:j + 1], ALU.subtract, ALU.mult)
                            m.then_inc(S["xn"].sem, 1)
                        if A.ok:
                            row_out(A, RB, ag, rt)
                    micros(dv, slot, 1)
            S.advance(dict.fromkeys(("expert", "xs", "in_bn", "in_stats", "in_eps", "in_rstd", "xn", "turned", "xnt_out", "attn", "expert_out", "next", "xa",
                                     "next_out", "back", "xt_out", "res", "bn", "stats", "var_eps", "rstd", "out_rows"), NBATCH))
            S.advance(dict(hidden=FC * NBATCH, gelu=FC * NBATCH, w_in0=24 * NBATCH, w_in1=24 * NBATCH))
            mem.close()

        def channel_mix():
            mem = Memory(nc, "L3f")
            NSEQ = BATCH // SEQ
            XS = mem.sb("XS", [P, 2, TB, D])
            XP = mem.sb("XP", [P, 2, NSEQ, SEQ + 1])
            mu1 = mem.sb("mu1", [P, 2])
            T1, T2 = mem.sb("T1", [P, 2, BATCH]), mem.sb("T2", [P, 2, BATCH])
            XR, XK = mem.sb("XR", [P, 2, BATCH]), mem.sb("XK", [P, 2, BATCH])
            KA = mem.sb("KA", [P, 2, BATCH])
            RG, RB = mem.sb("RG", [P, 2, TB, D]), mem.sb("RB", [P, 2, TB, D])
            st, ag, rt = mem.sb("st", [P, 2, TB, 6]), mem.sb("ag", [P, 2, TB, 2]), mem.sb("rt", [P, 2, 2, TB])
            ps = mem.pb("ps", [P, 2, 4, BATCH])
            with nc.Block() as block:
                @block.vector
                def _(dv):
                    nc.vector.memset(XP[:, :, :, :], 0.0)
                    nc.vector.tensor_scalar(mu1[:, 0:1], C("mur"), -1.0, 1.0, ALU.mult, ALU.add)
                    nc.vector.tensor_scalar(mu1[:, 1:2], C("muk"), -1.0, 1.0, ALU.mult, ALU.add)
            seqs = lambda ap: ap.rearrange("p (s k) -> p s k", k=SEQ)
            with nc.Block() as block:
                @block.gpsimd
                def _(g):
                    def slot(B):
                        A, N = B - 1, B + 1
                        if N.ok:
                            if after(N.b - 1):
                                g.wait_ge(S["turned"].sem, S["turned"].base + N.b - 1)
                            nc.gpsimd.tensor_copy(XS[:, N.u], X[:, N.rows, :]).then_inc(S["xs"].sem, 1)
                        if A.ok:
                            if after(A.b - 1):
                                g.wait_ge(S["out_rows"].sem, S["out_rows"].base + A.b - 1)
                            row_root(A, ag, rt)
                    micros(g, slot, 1)

                @block.tensor
                def _(pe):
                    def slot(B):
                        A = B - 1
                        if B.ok:
                            if after(B.b - 1):
                                pe.wait_ge(S["out_rows"].sem, S["out_rows"].base + B.b - 1)
                            pe.wait_ge(S["xs"].sem, S["xs"].base + B.b + 1)
                            for j in range(TB):
                                m = nc.tensor.transpose(ps[:, B.u, 0, j * P:(j + 1) * P], XS[:, B.u, j, :], ident)
                            m.then_inc(S["turned"].sem, 1)
                        if A.ok:
                            pe.wait_ge(S["ka"].sem, S["ka"].base + A.b + 1)
                            for j in range(TB):
                                m = nc.tensor.matmul(ps[:, A.u, 3, j * P:(j + 1) * P], KA[:, A.u, j * P:(j + 1) * P], Wm("L3fv"), start=True, stop=True)
                            m.then_inc(S["back"].sem, 1)
                        if B.ok:
                            pe.wait_ge(S["xk"].sem, S["xk"].base + B.b + 1)
                            nc.tensor.matmul(ps[:, B.u, 1, :], Wm("L3fk"), XK[:, B.u, :], start=True, stop=True).then_inc(S["hidden"].sem, 1)
                            pe.wait_ge(S["xr"].sem, S["xr"].base + B.b + 1)
                            for j in range(TB):
                                m = nc.tensor.matmul(ps[:, B.u, 2, j * P:(j + 1) * P], XR[:, B.u, j * P:(j + 1) * P], Wm("L3fr"), start=True, stop=True)
                            m.then_inc(S["attn"].sem, 1)
                    micros(pe, slot, 1)

                @block.scalar
                def _(act):
                    def slot(B):
                        A = B - 1
                        if B.ok:
                            act.wait_ge(S["turned"].sem, S["turned"].base + B.b + 1)
                            nc.scalar.activation(XP[:, B.u, :, 1:SEQ + 1], seqs(ps[:, B.u, 0, :]), ACT.Copy).then_inc(S["xt_out"].sem, 1)
                            act.wait_ge(S["xt_out"].sem, S["xt_out"].base + B.b + 1)
                            nc.scalar.activation(seqs(T1[:, B.u, :]), XP[:, B.u, :, 0:SEQ], ACT.Copy, scale=mu1[:, 1:2])
                            nc.scalar.activation(seqs(T2[:, B.u, :]), XP[:, B.u, :, 0:SEQ], ACT.Copy, scale=mu1[:, 0:1]).then_inc(S["prev"].sem, 1)
                            act.wait_ge(S["attn"].sem, S["attn"].base + B.b + 1)
                            nc.scalar.activation(RG[:, B.u].rearrange(FLAT), ps[:, B.u, 2, :], ACT.Sigmoid).then_inc(S["gelu"].sem, 1)
                    micros(act, slot, 1)

                @block.vector
                def _(dv):
                    def slot(B):
                        A = B - 1
                        if B.ok:
                            dv.wait_ge(S["prev"].sem, S["prev"].base + B.b + 1)
                            nc.vector.scalar_tensor_tensor(seqs(XK[:, B.u, :]), XP[:, B.u, :, 1:SEQ + 1], C("muk"), seqs(T1[:, B.u, :]), ALU.mult, ALU.add).then_inc(S["xk"].sem, 1)
                            nc.vector.scalar_tensor_tensor(seqs(XR[:, B.u, :]), XP[:, B.u, :, 1:SEQ + 1], C("mur"), seqs(T2[:, B.u, :]), ALU.mult, ALU.add).then_inc(S["xr"].sem, 1)
                        if A.ok:
                            dv.wait_ge(S["back"].sem, S["back"].base + A.b + 1)
                            dv.wait_ge(S["gelu"].sem, S["gelu"].base + A.b + 1)
                            nc.vector.tensor_tensor(RB[:, A.u].rearrange(FLAT), ps[:, A.u, 3, :], RG[:, A.u].rearrange(FLAT), ALU.mult).then_inc(S["next"].sem, 1)
                        if B.ok:
                            dv.wait_ge(S["hidden"].sem, S["hidden"].base + B.b + 1)
                            nc.vector.tensor_scalar(T1[:, B.u, :], ps[:, B.u, 1, :], 0.0, None, ALU.max).then_inc(S["next_out"].sem, 1)
                            dv.wait_ge(S["next_out"].sem, S["next_out"].base + B.b + 1)
                            nc.vector.tensor_tensor(KA[:, B.u, :], T1[:, B.u, :], T1[:, B.u, :], ALU.mult).then_inc(S["ka"].sem, 1)
                        if A.ok:
                            dv.wait_ge(S["next"].sem, S["next"].base + A.b + 1)
                            nc.vector.tensor_tensor(RB[:, A.u], RB[:, A.u], X[:, A.rows, :], ALU.add).then_inc(S["res"].sem, 1)
                            dv.wait_ge(S["res"].sem, S["res"].base + A.b + 1)
                            row_stats(A, RB, st, ag)
                            row_out(A, RB, ag, rt)
                    micros(dv, slot, 1)
            S.advance(dict.fromkeys(("xs", "turned", "attn", "hidden", "gelu", "next", "next_out", "ka", "xr", "xk", "prev", "back", "xt_out", "res",
                                     "bn", "stats", "var_eps", "rstd", "out_rows"), NBATCH))
            mem.close()

        def recurrent_block():
            FC, CK = 4, 4
            NSEQ = BATCH // SEQ
            RMS3_EPS = 1e-6
            mem = Memory(nc, "L3a")
            WG, WU, WD = mem.sb("WG", [P, FC * D]), mem.sb("WU", [P, FC * D]), mem.sb("WD", [P, FC, D])
            decay, dtmp = mem.sb("decay", [P, 1]), mem.sb("dtmp", [P, 4])
            eps3, nw = mem.sb("eps3", [P, TB]), mem.sb("nw", [P, 2])
            SQR = mem.sb("SQR", [P, 2, TB, D])
            ms, ms2 = mem.sb("ms", [P, 2, 2, TB]), mem.sb("ms2", [P, 2, 2, TB])
            XN, XT = mem.sb("XN", [P, 2, TB, D]), mem.sb("XT", [P, 2, BATCH])
            XP = mem.sb("XP", [P, 2, NSEQ, SEQ + CK - 1])
            YB, XC, RG, IG = (mem.sb(n, [P, 2, BATCH]) for n in ("YB", "XC", "RG", "IG"))
            A1, A2, HS = mem.sb("A1", [P, 2, BATCH]), mem.sb("A2", [P, 2, BATCH]), mem.sb("HS", [P, 2, BATCH])
            H1 = mem.sb("H1", [P, 2, TB, D])
            GG, G2 = mem.sb("GG", [P, 2, BATCH]), mem.sb("G2", [P, FC, BATCH])
            RB = mem.sb("RB", [P, 2, TB, D])
            st, ag, rt = mem.sb("st", [P, 2, TB, 6]), mem.sb("ag", [P, 2, TB, 2]), mem.sb("rt", [P, 2, 2, TB])
            ps = mem.pb("ps", [P, 2, 4, BATCH])
            seqs = lambda ap: ap.rearrange("p (s k) -> p s k", k=SEQ)
            flat = lambda ap: ap.rearrange("p t k -> p (t k)")

            with nc.Block() as block:
                @block.sync
                def _(sp):
                    for d, s_ in ((WG[:, :], io["wg"]), (WU[:, :], io["wu"]), (WD[:, :, :], io["wd"])):
                        sp.dma_start(d, s_).then_inc(S["weights_in"].sem, 16)
                    sp.wait_ge(S["weights_in"].sem, S["weights_in"].base + 48)

                @block.vector
                def _(dv):
                    nc.vector.memset(XP[:, :, :, :], 0.0)
                    nc.vector.memset(eps3[:, :], D * RMS3_EPS)
                    nc.vector.tensor_scalar(nw[:, 0:1], C("n1"), float(np.sqrt(D)), None, ALU.mult)
                    nc.vector.tensor_scalar(nw[:, 1:2], C("n2"), float(np.sqrt(D)), None, ALU.mult)
                    nc.vector.tensor_scalar(dtmp[:, 0:1], C("lam"), -1.0, None, ALU.mult).then_inc(S["prep"].sem, 1)
                    nc.vector.tensor_scalar(dtmp[:, 3:4], C("lam"), 0.0, None, ALU.max)
                    dv.wait_ge(S["prep"].sem, S["prep"].base + 1)
                    nc.vector.tensor_tensor(dtmp[:, 1:2], dtmp[:, 0:1], C("lam"), ALU.min).then_inc(S["prep"].sem, 1)
                    dv.wait_ge(S["prep_act"].sem, S["prep_act"].base + 1)
                    nc.vector.tensor_tensor(dtmp[:, 3:4], dtmp[:, 3:4], dtmp[:, 2:3], ALU.add).then_inc(S["prep"].sem, 1)
                    dv.wait_ge(S["prep"].sem, S["prep"].base + 3)
                    nc.vector.tensor_scalar(decay[:, :], dtmp[:, 3:4], -8.0, None, ALU.mult)

                @block.scalar
                def _(act):
                    act.wait_ge(S["prep"].sem, S["prep"].base + 2)
                    nc.scalar.activation(dtmp[:, 2:3], dtmp[:, 1:2], ACT.Exp).then_inc(S["prep_exp"].sem, 1)
                    act.wait_ge(S["prep_exp"].sem, S["prep_exp"].base + 1)
                    nc.scalar.activation(dtmp[:, 2:3], dtmp[:, 2:3], ACT.Ln, bias=1.0).then_inc(S["prep_act"].sem, 1)
            S.advance(dict(weights_in=48, prep=3, prep_exp=1, prep_act=1))

            with nc.Block() as block:
                @block.gpsimd
                def _(g):
                    def root(B, ms_, means, eps, done):
                        g.wait_ge(means.sem, means.base + B.b + 1)
                        nc.gpsimd.tensor_tensor(ms_[:, B.u, 1, :], ms_[:, B.u, 0, :], eps3[:, :], ALU.add).then_inc(eps.sem, 1)
                        g.wait_ge(eps.sem, eps.base + B.b + 1)
                        nc.gpsimd.tensor_tensor(ms_[:, B.u, 0, :], ms_[:, B.u, 1, :], half[:, 0:TB], ALU.pow).then_inc(done.sem, 1)

                    def slot(B):
                        A, N = B - 1, B + 1
                        if A.ok:
                            g.wait_ge(S["h1"].sem, S["h1"].base + A.b + 1)
                            nc.gpsimd.tensor_tensor(SQR[:, A.u], H1[:, A.u], H1[:, A.u], ALU.mult).then_inc(S["squares2"].sem, 1)
                            root(A, ms2, S["means2"], S["h_eps"], S["h_rstd"])
                        if N.ok:
                            if after(N.b - 1):
                                g.wait_ge(S["means2"].sem, S["means2"].base + N.b - 1)
                            if after(N.b - 1):
                                g.wait_ge(S["xn"].sem, S["xn"].base + N.b - 1)
                            pace(g, S)
                            nc.gpsimd.tensor_tensor(SQR[:, N.u], X[:, N.rows, :], X[:, N.rows, :], ALU.mult).then_inc(S["squares"].sem, 1)
                            root(N, ms, S["means"], S["in_eps"], S["in_rstd"])
                        if A.ok:
                            g.wait_ge(S["un"].sem, S["un"].base + A.b + 1)
                            pace(g, S)
                            nc.gpsimd.tensor_tensor(H1[:, A.u], H1[:, A.u], X[:, A.rows, :], ALU.add).then_inc(S["h1_x"].sem, 1)
                        if B.ok:
                            g.wait_ge(S["gates_out"].sem, S["gates_out"].base + B.b + 1)
                            nc.gpsimd.tensor_tensor(IG[:, B.u, :], IG[:, B.u, :], XC[:, B.u, :], ALU.mult).then_inc(S["ix"].sem, 1)
                        if A.ok:
                            if after(A.b - 1):
                                g.wait_ge(S["out_rows"].sem, S["out_rows"].base + A.b - 1)
                            row_root(A, ag, rt)
                    micros(g, slot, 1)

                @block.tensor
                def _(pe):
                    def turn(B, bank, src, ready, done):
                        pe.wait_ge(ready.sem, ready.base + B.b + 1)
                        for j in range(TB):
                            m = nc.tensor.transpose(ps[:, B.u, bank, j * P:(j + 1) * P], src[:, B.u, j, :], ident)
                        m.then_inc(done.sem, 1)

                    def hidden(A, c):
                        b1, b2 = ((3, 0), (1, 2))[c % 2]
                        if after(FC * A.b + c - 1 if c > 1 else 0):
                            pe.wait_ge(S["gg"].sem, S["gg"].base + (FC * A.b + c - 1 if c > 1 else 0))
                        if c == 0:
                            pe.wait_ge(S["u_out"].sem, S["u_out"].base + A.b + 1)
                        nc.tensor.matmul(ps[:, A.u, b1, :], WG[:, c * D:(c + 1) * D], XT[:, A.u, :], start=True, stop=True)
                        nc.tensor.matmul(ps[:, A.u, b2, :], WU[:, c * D:(c + 1) * D], XT[:, A.u, :], start=True, stop=True).then_inc(S["hidden"].sem, 1)

                    def slot(B):
                        A = B - 1
                        if B.ok:
                            if after(B.b - 1):
                                pe.wait_ge(S["out_rows"].sem, S["out_rows"].base + B.b - 1)
                            turn(B, 0, XN, S["xn"], S["turned"])
                        if A.ok:
                            pe.wait_ge(S["hy"].sem, S["hy"].base + A.b + 1)
                            for j in range(TB):
                                m = nc.tensor.matmul(ps[:, A.u, 1, j * P:(j + 1) * P], HS[:, A.u, j * P:(j + 1) * P], Wm("L3Wo"), start=True, stop=True)
                            m.then_inc(S["mix"].sem, 1)
                        if B.ok:
                            pe.wait_ge(S["xt_out"].sem, S["xt_out"].base + B.b + 1)
                            nc.tensor.matmul(ps[:, B.u, 1, :], Wm("L3Wx"), XT[:, B.u, :], start=True, stop=True).then_inc(S["xb"].sem, 1)
                            nc.tensor.matmul(ps[:, B.u, 2, :], Wm("L3Wy"), XT[:, B.u, :], start=True, stop=True).then_inc(S["yb"].sem, 1)
                        if A.ok:
                            turn(A, 2, RB, S["un"], S["turned2"])
                            hidden(A, 0)
                            hidden(A, 1)
                        if B.ok:
                            pe.wait_ge(S["conv"].sem, S["conv"].base + 5 * (B.b + 1))
                            nc.tensor.matmul(ps[:, B.u, 3, :], Wm("L3Wa"), XC[:, B.u, :], start=True, stop=True)
                            nc.tensor.matmul(ps[:, B.u, 0, :], Wm("L3Wi"), XC[:, B.u, :], start=True, stop=True).then_inc(S["gates"].sem, 1)
                        if A.ok:
                            hidden(A, 2)
                            hidden(A, 3)
                            pe.wait_ge(S["gg"].sem, S["gg"].base + FC * (A.b + 1))
                            for j in range(TB):
                                for c in range(FC):
                                    m = nc.tensor.matmul(ps[:, A.u, 3, j * P:(j + 1) * P], G2[:, c, j * P:(j + 1) * P], WD[:, c, :], start=c == 0, stop=c == FC - 1)
                            m.then_inc(S["back"].sem, 1)
                    micros(pe, slot, 1)

                @block.scalar
                def _(act):
                    def gelu(A, c):
                        act.wait_ge(S["hidden"].sem, S["hidden"].base + FC * A.b + c + 1)
                        if after(FC * A.b + c - 1):
                            act.wait_ge(S["gg"].sem, S["gg"].base + FC * A.b + c - 1)
                        nc.scalar.activation(GG[:, c % 2, :], ps[:, A.u, (3, 1)[c % 2], :], ACT.Gelu_apprx_tanh).then_inc(S["gelu"].sem, 1)

                    def slot(B):
                        A = B - 1
                        if B.ok:
                            act.wait_ge(S["turned"].sem, S["turned"].base + B.b + 1)
                            nc.scalar.activation(XT[:, B.u, :], ps[:, B.u, 0, :], ACT.Copy, scale=nw[:, 0:1]).then_inc(S["xt_out"].sem, 1)
                            act.wait_ge(S["yb"].sem, S["yb"].base + B.b + 1)
                            nc.scalar.activation(YB[:, B.u, :], ps[:, B.u, 2, :], ACT.Gelu_apprx_tanh).then_inc(S["yb_out"].sem, 1)
                        if A.ok:
                            act.wait_ge(S["turned2"].sem, S["turned2"].base + A.b + 1)
                            nc.scalar.activation(XT[:, A.u, :], ps[:, A.u, 2, :], ACT.Copy, scale=nw[:, 1:2]).then_inc(S["u_out"].sem, 1)
                            for c in range(FC):
                                gelu(A, c)
                        if B.ok:
                            act.wait_ge(S["gates"].sem, S["gates"].base + B.b + 1)
                            nc.scalar.activation(RG[:, B.u, :], ps[:, B.u, 3, :], ACT.Sigmoid)
                            nc.scalar.activation(IG[:, B.u, :], ps[:, B.u, 0, :], ACT.Sigmoid).then_inc(S["gates_out"].sem, 1)
                            act.wait_ge(S["gates_out"].sem, S["gates_out"].base + B.b + 1)
                            nc.scalar.activation(A1[:, B.u, :], RG[:, B.u, :], ACT.Exp, scale=decay[:, 0:1]).then_inc(S["a_out"].sem, 1)
                            act.wait_ge(S["floored"].sem, S["floored"].base + B.b + 1)
                            nc.scalar.activation(A2[:, B.u, :], A2[:, B.u, :], ACT.Sqrt).then_inc(S["m_root"].sem, 1)
                    micros(act, slot, 1)

                @block.vector
                def _(dv):
                    def mean_square(B, squares, ms_, done):
                        dv.wait_ge(squares.sem, squares.base + B.b + 1)
                        nc.vector.tensor_reduce(ms_[:, B.u, 0, :], SQR[:, B.u], AX, ALU.add).then_inc(done.sem, 1)

                    def scaled(B, dst, src, ms_, ready, done):
                        dv.wait_ge(ready.sem, ready.base + B.b + 1)
                        nc.vector.tensor_tensor(dst[:, B.u], src, ms_[:, B.u, 0, :].unsqueeze(2).to_broadcast([P, TB, D]), ALU.mult).then_inc(done.sem, 1)

                    def gated(A, c):
                        dv.wait_ge(S["gelu"].sem, S["gelu"].base + FC * A.b + c + 1)
                        if c == 0:
                            if after(A.b):
                                dv.wait_ge(S["back"].sem, S["back"].base + A.b)
                        nc.vector.tensor_tensor(G2[:, c, :], GG[:, c % 2, :], ps[:, A.u, (0, 2)[c % 2], :], ALU.mult).then_inc(S["gg"].sem, 1)

                    def slot(B):
                        A, N = B - 1, B + 1
                        if A.ok:
                            if after(A.b - 1):
                                dv.wait_ge(S["out_rows"].sem, S["out_rows"].base + A.b - 1)
                            dv.wait_ge(S["mix"].sem, S["mix"].base + A.b + 1)
                            nc.vector.tensor_tensor(H1[:, A.u], ps[:, A.u, 1, :].rearrange("p (t d) -> p t d", d=D), X[:, A.rows, :], ALU.add).then_inc(S["h1"].sem, 1)
                        if B.ok:
                            dv.wait_ge(S["xb"].sem, S["xb"].base + B.b + 1)
                            nc.vector.tensor_copy(XP[:, B.u, :, CK - 1:], seqs(ps[:, B.u, 1, :])).then_inc(S["conv"].sem, 1)
                        if A.ok:
                            mean_square(A, S["squares2"], ms2, S["means2"])
                        if B.ok:
                            xc = seqs(XC[:, B.u, :])
                            dv.wait_ge(S["conv"].sem, S["conv"].base + 5 * B.b + 1)
                            nc.vector.tensor_scalar(xc, XP[:, B.u, :, 0:SEQ], C("c0"), C("cb"), ALU.mult, ALU.add).then_inc(S["conv"].sem, 1)
                        if A.ok:
                            dv.wait_ge(S["h1"].sem, S["h1"].base + A.b + 1)
                            scaled(A, RB, H1[:, A.u], ms2, S["h_rstd"], S["un"])
                        if N.ok:
                            mean_square(N, S["squares"], ms, S["means"])
                        if B.ok:
                            for k in range(1, CK):
                                dv.wait_ge(S["conv"].sem, S["conv"].base + 5 * B.b + 1 + k)
                                nc.vector.scalar_tensor_tensor(xc, XP[:, B.u, :, k:k + SEQ], C(f"c{k}"), xc, ALU.mult, ALU.add).then_inc(S["conv"].sem, 1)
                        if A.ok:
                            gated(A, 0)
                            gated(A, 1)
                        if N.ok:
                            if after(N.b - 1):
                                dv.wait_ge(S["turned"].sem, S["turned"].base + N.b - 1)
                            scaled(N, XN, X[:, N.rows, :], ms, S["in_rstd"], S["xn"])
                        if A.ok:
                            gated(A, 2)
                            gated(A, 3)
                        if B.ok:
                            dv.wait_ge(S["a_out"].sem, S["a_out"].base + B.b + 1)
                            nc.vector.tensor_tensor(A2[:, B.u, :], A1[:, B.u, :], A1[:, B.u, :], ALU.mult).then_inc(S["a_squared"].sem, 1)
                            dv.wait_ge(S["a_squared"].sem, S["a_squared"].base + B.b + 1)
                            nc.vector.tensor_scalar(A2[:, B.u, :], A2[:, B.u, :], -1.0, 1.0, ALU.mult, ALU.add).then_inc(S["one_less"].sem, 1)
                            nc.vector.memset(seqs(A1[:, B.u, :])[:, :, 0:1], 0.0).then_inc(S["cut"].sem, 1)
                            dv.wait_ge(S["one_less"].sem, S["one_less"].base + B.b + 1)
                            nc.vector.tensor_scalar(A2[:, B.u, :], A2[:, B.u, :], 1e-12, None, ALU.max).then_inc(S["floored"].sem, 1)
                        if A.ok:
                            dv.wait_ge(S["back"].sem, S["back"].base + A.b + 1)
                            dv.wait_ge(S["h1_x"].sem, S["h1_x"].base + A.b + 1)
                            nc.vector.tensor_tensor(RB[:, A.u], ps[:, A.u, 3, :].rearrange("p (t d) -> p t d", d=D), H1[:, A.u], ALU.add).then_inc(S["res"].sem, 1)
                            dv.wait_ge(S["res"].sem, S["res"].base + A.b + 1)
                            row_stats(A, RB, st, ag)
                        if B.ok:
                            dv.wait_ge(S["m_root"].sem, S["m_root"].base + B.b + 1)
                            dv.wait_ge(S["ix"].sem, S["ix"].base + B.b + 1)
                            nc.vector.tensor_tensor(A2[:, B.u, :], A2[:, B.u, :], IG[:, B.u, :], ALU.mult).then_inc(S["b_out"].sem, 1)
                            dv.wait_ge(S["b_out"].sem, S["b_out"].base + B.b + 1)
                            dv.wait_ge(S["cut"].sem, S["cut"].base + B.b + 1)
                            nc.vector.tensor_tensor_scan(HS[:, B.u, :], A1[:, B.u, :], A2[:, B.u, :], 0.0, ALU.mult, ALU.add).then_inc(S["scanned"].sem, 1)
                            dv.wait_ge(S["scanned"].sem, S["scanned"].base + B.b + 1)
                            dv.wait_ge(S["yb_out"].sem, S["yb_out"].base + B.b + 1)
                            nc.vector.tensor_tensor(HS[:, B.u, :], HS[:, B.u, :], YB[:, B.u, :], ALU.mult).then_inc(S["hy"].sem, 1)
                        if A.ok:
                            row_out(A, RB, ag, rt)
                    micros(dv, slot, 1)
            S.advance(dict.fromkeys(("squares", "squares2", "means", "means2", "in_eps", "in_rstd", "h_eps", "h_rstd", "un", "h1_x", "gates_out", "ix", "xn", "turned",
                                     "hy", "mix", "xt_out", "xb", "yb", "turned2", "u_out", "gates", "back", "yb_out", "a_out", "floored", "m_root", "h1",
                                     "a_squared", "one_less", "cut", "res", "b_out", "scanned", "bn", "stats", "var_eps", "rstd", "out_rows"), NBATCH))
            S.advance(dict(conv=5 * NBATCH, hidden=FC * NBATCH, gelu=FC * NBATCH, gg=FC * NBATCH))
            mem.close()

        def grouped_attention():
            QC = HEADS // 2
            mem = Memory(nc, "L1a")
            WQ, WK, WV = mem.sb("WQ", [P, QC, P]), mem.sb("WK", [P, KVH, 2, GD]), mem.sb("WV", [P, KVH * GD])
            WO = mem.sb("WO", [P, QC, D])
            XS, XT = mem.sb("XS", [P, 2, 2, D]), mem.sb("XT", [P, 2, 2 * P])
            QT = mem.sb("QT", [P, 2, QC, 2 * P])
            KB = mem.sb("KB", [P, 2, 4, KVH, 2, SEQ])
            VB = mem.sb("VB", [P, 2, 4, KVH, 2, GD])
            PR, PT = mem.sb("PR", [P, 2, HEADS, SEQ]), mem.sb("PT", [P, QC, P])
            mx, rden = mem.sb("mx", [P, 2, HEADS]), mem.sb("rden", [P, 2, 2, HEADS])
            ON, OT = mem.sb("ON", [P, QC, P]), mem.sb("OT", [P, QC, P])
            RB, st, ag, rs = mem.sb("RB", [P, 2, D]), mem.sb("st", [P, 2, 6]), mem.sb("ag", [P, 2, 2]), mem.sb("rs", [P, 2, 2])
            psF, psS = mem.pb("psF", [P, 2, 512]), mem.pb("psS", [P, 2, 8, SEQ])
            psP, psO = mem.pb("psP", [P, 2, 4, P]), mem.pb("psO", [P, 2, 4, P])
            psJ = psO[:, 0, 0, :]
            scale = GD ** -0.5

            FILLS = [("x", 0), ("k", 0), ("k", 1), ("q", 0), ("q", 1), ("q", 2), ("q", 3), ("v", 0), ("v", 1)]
            NFILL = len(FILLS)
            by_act = [1, 1, 1, 0, 1, 0, 1, 1, 1]
            by_dve = [0, 1, 1, 1, 0, 1, 0, 1, 1]
            NA, ND = sum(by_act), sum(by_dve)
            PLACES = (((0,), (1, 2), (3, 4)), ((5,), (6, 7), (8,)))

            def copied(eng, p, n, also=None):
                q, k = (p, n) if n >= 0 else (p - 1, n + NFILL)
                if also is not None and n < also:
                    eng.wait_ge(S["out_a"].sem, S["out_a"].base + p * NA + sum(by_act[:also + 1]))
                else:
                    if after(q * NA + sum(by_act[:k + 1])):
                        eng.wait_ge(S["out_a"].sem, S["out_a"].base + q * NA + sum(by_act[:k + 1]))
                if after(q * ND + sum(by_dve[:k + 1])):
                    eng.wait_ge(S["out_d"].sem, S["out_d"].base + q * ND + sum(by_dve[:k + 1]))

            with nc.Block() as block:
                @block.sync
                def _(sp):
                    for d, s_ in ((WQ[:, :, :], io["wq"]), (WK[:, :, :, :], io["wk"]), (WV[:, :], io["wv"]), (WO[:, :, :], io["wo"])):
                        sp.dma_start(d, s_).then_inc(S["weights_in"].sem, 16)
                    sp.wait_ge(S["weights_in"].sem, S["weights_in"].base + 64)

                @block.vector
                def _(dv):
                    nc.vector.memset(KB[:, :, :, :, :, :], 0.0)

                @block.gpsimd
                def _(g):
                    nc.gpsimd.memset(VB[:, :, :, :, :, :], 0.0)
            S.advance(dict(weights_in=64))

            def copy_out(eng, N, n):
                kind, k = FILLS[n]
                act = eng is nc.scalar
                bank = psF[:, (N.u + n) % 2, :]
                eng.wait_ge(S["front"].sem, S["front"].base + N.p * NFILL + n + 1)
                half_ = slice(0, 64) if act else slice(64, 128)
                h = 0 if act else 1
                if kind == "x":
                    dst, src = XT[:, N.u, :], bank[:, 0:256]
                elif kind == "q":
                    if after(2 * N.p - 2):
                        eng.wait_ge(S["scores"].sem, S["scores"].base + 2 * N.p - 2)
                    dst, src = QT[:, N.u, 2 * k:2 * k + 2, :].rearrange("p c t -> p (c t)"), bank
                elif kind == "k":
                    if after(2 * N.p - 2):
                        eng.wait_ge(S["scores"].sem, S["scores"].base + 2 * N.p - 2)
                    dst = KB[half_, N.u, :, 2 * k:2 * k + 2, h, :]
                    src = bank[half_, :].rearrange("p (j s k) -> p s j k", j=2, k=SEQ)
                else:
                    if after(2 * N.p - 2):
                        eng.wait_ge(S["pv"].sem, S["pv"].base + 2 * N.p - 2)
                    dst = VB[half_, N.u, 2 * k:2 * k + 2, :, h, :]
                    src = bank[half_, :].rearrange("p (s j k) -> p s j k", s=2, k=GD)
                if act:
                    nc.scalar.activation(dst, src, ACT.Copy).then_inc(S["out_a"].sem, 1)
                else:
                    nc.vector.tensor_copy(dst, src).then_inc(S["out_d"].sem, 1)

            def copies(eng, T, place):
                N = T + 2 if T.par == 0 else T + 1
                if N.ok:
                    for n in PLACES[T.par][place]:
                        if (by_act if eng is nc.scalar else by_dve)[n]:
                            copy_out(eng, N, n)

            with nc.Block() as block:
                @block.gpsimd
                def _(g):
                    def slot(T):
                        N, A = T + 2, T - 1
                        if T.par == 0 and N.ok:
                            if after((N.p - 2) * NFILL + 1):
                                g.wait_ge(S["front"].sem, S["front"].base + (N.p - 2) * NFILL + 1)
                            nc.gpsimd.tensor_copy(XS[:, N.u], X[:, bass.ds(N.t, 2), :]).then_inc(S["xs"].sem, 1)
                        if A.ok:
                            g.wait_ge(S["stats"].sem, S["stats"].base + A.t + 1)
                            if after(A.t - 1):
                                g.wait_ge(S["out_rows"].sem, S["out_rows"].base + A.t - 1)
                            nc.gpsimd.tensor_tensor(rs[:, A.par, 0:1], ag[:, A.par, 1:2], eps[:, 0:1], ALU.add).then_inc(S["var_eps"].sem, 1)
                            g.wait_ge(S["var_eps"].sem, S["var_eps"].base + A.t + 1)
                            nc.gpsimd.tensor_tensor(rs[:, A.par, 1:2], rs[:, A.par, 0:1], half[:, 0:1], ALU.pow).then_inc(S["rstd"].sem, 1)
                    pipeline(g, slot, 2)

                @block.tensor
                def _(pe):
                    def fill(N, n):
                        kind, k = FILLS[n]
                        bank = psF[:, (N.u + n) % 2, :]
                        copied(pe, N.p, n - 2, 0 if n else None)
                        if kind == "x":
                            pe.wait_ge(S["xs"].sem, S["xs"].base + N.p + 1)
                            for a in range(2):
                                m = nc.tensor.transpose(bank[:, a * P:a * P + P], XS[:, N.u, a, :], ident)
                        if kind == "k":
                            for j in range(2):
                                m = nc.tensor.matmul(bank[:, 256 * j:256 * j + 256], WK[:, 2 * k + j, :, :].rearrange("p h d -> p (h d)"), XT[:, N.u, :], start=True, stop=True)
                        if kind == "q":
                            for j in range(2):
                                m = nc.tensor.matmul(bank[:, 256 * j:256 * j + 256], WQ[:, 2 * k + j, :], XT[:, N.u, :], start=True, stop=True)
                        if kind == "v":
                            for s in range(2):
                                for a in range(2):
                                    q4 = 2 * k + s
                                    m = nc.tensor.matmul(bank[64 * a:64 * a + 64, 256 * s:256 * s + 256], XT[:, N.u, q4 * SEQ:(q4 + 1) * SEQ], WV[:, :], start=True, stop=True)
                        m.then_inc(S["front"].sem, 1)

                    def fills(T, place):
                        N = T + 2 if T.par == 0 else T + 1
                        if N.ok:
                            for n in PLACES[T.par][place]:
                                fill(N, n)

                    def slot(T):
                        A = T - 1
                        if A.ok:
                            pe.wait_ge(S["probs"].sem, S["probs"].base + A.t + 1)
                            for hb, free, done in ((0, S["ot_a"], S["turned_a"]), (1, S["ot_b"], S["turned_b"])):
                                if after(A.t):
                                    pe.wait_ge(free.sem, free.base + A.t)
                                for j in range(4):
                                    b = hb * 4 + j
                                    m = nc.tensor.transpose(psP[:, hb, j, :], PR[:, A.par, 2 * b:2 * b + 2, :].rearrange("p h k -> p (h k)"), ident)
                                m.then_inc(done.sem, 1)
                        if T.ok:
                            copied(pe, T.p, NFILL - 1)
                            if after(T.t):
                                pe.wait_ge(S["shifted"].sem, S["shifted"].base + T.t)
                            for hh in range(2):
                                nc.tensor.matmul(psS[:, hh], idb[:, :], causal[:, :].unsqueeze(1).to_broadcast([P, 8, SEQ]), start=True, stop=False, skip_group_check=True)
                            for c in range(QC):
                                for s in range(2):
                                    q4 = 2 * T.par + s
                                    m = nc.tensor.matmul(psS[64 * s:64 * s + 64, c // 4, 2 * (c % 4):2 * (c % 4) + 2, :], QT[:, T.u, c, q4 * SEQ:(q4 + 1) * SEQ],
                                                         KB[:, T.u, q4, c // 2, :, :], start=False, stop=True, skip_group_check=True)
                            m.then_inc(S["scores"].sem, 1)
                        fills(T, 0)
                        if A.ok:
                            pe.wait_ge(S["pt_a"].sem, S["pt_a"].base + A.t + 1)
                            pe.wait_ge(S["pt_b"].sem, S["pt_b"].base + A.t + 1)
                            if after(A.t):
                                pe.wait_ge(S["res"].sem, S["res"].base + A.t)
                            for c in range(QC):
                                for s in range(2):
                                    m = nc.tensor.matmul(psO[64 * s:64 * s + 64, c // 4, c % 4, :], PT[:, c, 64 * s:64 * s + 64],
                                                         VB[:, A.u, 2 * A.par + s, c // 2, :, :], start=True, stop=True)
                            m.then_inc(S["pv"].sem, 1)
                        fills(T, 1)
                        if A.ok:
                            pe.wait_ge(S["normed"].sem, S["normed"].base + A.t + 1)
                            for hb, done in ((0, S["o_turned_a"]), (1, S["o_turned_b"])):
                                for j in range(4):
                                    m = nc.tensor.transpose(psP[:, hb, j, :], ON[:, 4 * hb + j, :], ident)
                                m.then_inc(done.sem, 1)
                        fills(T, 2)
                        if A.ok:
                            pe.wait_ge(S["ot_a"].sem, S["ot_a"].base + A.t + 1)
                            pe.wait_ge(S["ot_b"].sem, S["ot_b"].base + A.t + 1)
                            for c in range(QC):
                                m = nc.tensor.matmul(psJ, OT[:, c, :], WO[:, c, :], start=c == 0, stop=c == QC - 1)
                            m.then_inc(S["proj"].sem, 1)
                    pipeline(pe, slot, 2)

                @block.scalar
                def _(act):
                    def slot(T):
                        A = T - 1
                        if A.ok:
                            act.wait_ge(S["turned_a"].sem, S["turned_a"].base + A.t + 1)
                            if after(A.t):
                                act.wait_ge(S["pv"].sem, S["pv"].base + A.t)
                            nc.scalar.activation(PT[:, 0:4, :], psP[:, 0], ACT.Copy).then_inc(S["pt_a"].sem, 1)
                        copies(act, T, 0)
                        if T.ok:
                            act.wait_ge(S["shifted"].sem, S["shifted"].base + T.t + 1)
                            nc.scalar.activation(PR[:, T.par], PR[:, T.par], ACT.Exp, scale=scale).then_inc(S["probs"].sem, 1)
                        copies(act, T, 1)
                        if A.ok:
                            act.wait_ge(S["o_turned_a"].sem, S["o_turned_a"].base + A.t + 1)
                            if after(A.t):
                                act.wait_ge(S["proj"].sem, S["proj"].base + A.t)
                            nc.scalar.activation(OT[:, 0:4, :], psP[:, 0], ACT.Copy).then_inc(S["ot_a"].sem, 1)
                        copies(act, T, 2)
                    pipeline(act, slot, 2)

                @block.vector
                def _(dv):
                    def slot(T):
                        A, E = T - 1, T - 2
                        if A.ok:
                            dv.wait_ge(S["turned_b"].sem, S["turned_b"].base + A.t + 1)
                            if after(A.t):
                                dv.wait_ge(S["pv"].sem, S["pv"].base + A.t)
                            nc.vector.tensor_copy(PT[:, 4:8, :], psP[:, 1]).then_inc(S["pt_b"].sem, 1)
                        if T.ok:
                            sc = psS[:, :, :, :].rearrange("p b h k -> p (b h) k")
                            dv.wait_ge(S["scores"].sem, S["scores"].base + T.t + 1)
                            nc.vector.tensor_reduce(mx[:, T.par, :], sc, AX, ALU.max).then_inc(S["maxed"].sem, 1)
                            dv.wait_ge(S["maxed"].sem, S["maxed"].base + T.t + 1)
                            if after(T.t - 1):
                                dv.wait_ge(S["turned_b"].sem, S["turned_b"].base + T.t - 1)
                            nc.vector.tensor_tensor(PR[:, T.par], sc, mx[:, T.par, :].unsqueeze(2).to_broadcast([P, HEADS, SEQ]), ALU.subtract).then_inc(S["shifted"].sem, 1)
                        copies(dv, T, 0)
                        if A.ok:
                            dv.wait_ge(S["pv"].sem, S["pv"].base + A.t + 1)
                            dv.wait_ge(S["recip"].sem, S["recip"].base + A.t + 1)
                            if after(A.t):
                                dv.wait_ge(S["o_turned_b"].sem, S["o_turned_b"].base + A.t)
                            nc.vector.tensor_tensor(ON[:, :, :].rearrange("p c (h d) -> p (c h) d", d=GD), psO[:, :, :, :].rearrange("p b c (h d) -> p (b c h) d", d=GD),
                                                    rden[:, A.par, 1, :].unsqueeze(2).to_broadcast([P, HEADS, GD]), ALU.mult).then_inc(S["normed"].sem, 1)
                        copies(dv, T, 1)
                        if A.ok:
                            dv.wait_ge(S["o_turned_b"].sem, S["o_turned_b"].base + A.t + 1)
                            if after(A.t):
                                dv.wait_ge(S["proj"].sem, S["proj"].base + A.t)
                            nc.vector.tensor_copy(OT[:, 4:8, :], psP[:, 1]).then_inc(S["ot_b"].sem, 1)
                        copies(dv, T, 2)
                        if T.ok:
                            dv.wait_ge(S["probs"].sem, S["probs"].base + T.t + 1)
                            if after(T.t - 1):
                                dv.wait_ge(S["normed"].sem, S["normed"].base + T.t - 1)
                            nc.vector.tensor_reduce(rden[:, T.par, 0, :], PR[:, T.par], AX, ALU.add).then_inc(S["summed"].sem, 1)
                            dv.wait_ge(S["summed"].sem, S["summed"].base + T.t + 1)
                            nc.vector.reciprocal(rden[:, T.par, 1, :], rden[:, T.par, 0, :]).then_inc(S["recip"].sem, 1)
                        if E.ok:
                            dv.wait_ge(S["rstd"].sem, S["rstd"].base + E.t + 1)
                            nc.vector.tensor_scalar(X[:, bass.ds(E.t, 1), :].rearrange("p a d -> p (a d)"), RB[:, E.par, :],
                                                    ag[:, E.par, 0:1], rs[:, E.par, 1:2], ALU.subtract, ALU.mult).then_inc(S["out_rows"].sem, 1)
                        if A.ok:
                            dv.wait_ge(S["proj"].sem, S["proj"].base + A.t + 1)
                            if after(A.t - 1):
                                dv.wait_ge(S["out_rows"].sem, S["out_rows"].base + A.t - 1)
                            nc.vector.tensor_tensor(RB[:, A.par, :], psJ, X[:, bass.ds(A.t, 1), :].rearrange("p a d -> p (a d)"), ALU.add).then_inc(S["res"].sem, 1)
                            dv.wait_ge(S["res"].sem, S["res"].base + A.t + 1)
                            nc.vector.bn_stats(st[:, A.par, :], RB[:, A.par, :]).then_inc(S["bn"].sem, 1)
                            dv.wait_ge(S["bn"].sem, S["bn"].base + A.t + 1)
                            pace(nc.vector, S)
                            nc.vector.bn_aggr(ag[:, A.par, :], st[:, A.par, :]).then_inc(S["stats"].sem, 1)
                    pipeline(dv, slot, 2)
            S.advance(dict.fromkeys(("scores", "maxed", "shifted", "probs", "turned_a", "turned_b", "pt_a", "pt_b", "pv", "normed", "o_turned_a", "o_turned_b",
                                     "ot_a", "ot_b", "proj", "res", "bn", "stats", "var_eps", "rstd", "out_rows", "summed", "recip"), TILES))
            S.advance(dict(front=NFILL * PAIRS, out_a=NA * PAIRS, out_d=ND * PAIRS, xs=PAIRS))
            mem.close()

        static = lambda T: causal[:, :]
        per_tile = lambda T: maskk[:, bass.ds(T.t, 1), :].rearrange("p a k -> p (a k)")
        attention("L0a", Wm("L0q"), Wm("L0k"), Wm("L0v"), Wm("L0o"), qs=Wm("L0qs"), ks=Wm("L0ks"), mask=static)
        source_stats("rms")
        attention("L0x", ident, ident, ident, Wm("L0xo"), qs=Wm("SWAP"), ks=Wm("SWAP"), gq=C("qn"), gqs=C("qns"), gk=C("kn"), gks=C("kns"),
                  bo=R("L0xb"), cross=True, norm="rms")
        moe("L0f", 8, 2, 88, True, "w1a", "w2a", dict(rw="rwa"))
        grouped_attention()
        key_masks("mask")
        attention("L1x", Wm("L1xq"), Wm("L1xk"), Wm("L1xv"), Wm("L1xo"), bq=C("L1bq"), bk=C("L1bk"), bv=C("L1bv"), bo=R("L1xb"),
                  cross=True, mask=per_tile, keymask=True)
        keep = Memory(nc, "keep")
        XO = keep.sb("XO", [P, TILES, D])
        with nc.Block() as block:
            @block.vector
            def _(dv):
                nc.vector.tensor_tensor(XO[:, :, :], X[:, :, :], R("b2").unsqueeze(1).to_broadcast([P, TILES, D]), ALU.add)
        attention("L1f", Wm("L1fq"), Wm("L1fk"), Wm("L1fv"), Wm("L1fo"), bq=C("L1fbq"), bk=C("L1fbk"), bv=C("L1fbv"), bo=R("L1fb"),
                  affine=(R("g1"), R("b1")))
        moe("L1m", 8, 2, 128, False, "w1b", "w2b", dict(rw="rwb", rb="rbb", b1="b1b", b2="b2b"), XO)
        keep.close()
        attention("L2a", Wm("L2q"), Wm("L2k"), Wm("L2v"), Wm("L2o"), qs=Wm("L2qs"), ks=Wm("L2ks"), bq=C("L2bq"), bqs=C("L2bqs"),
                  bk=C("L2bk"), bks=C("L2bks"), bv=C("L2bv"), bo=R("L2b"), cq=2, ck=2, mask=static)
        attention("L2x", Wm("L2xq"), Wm("L2xk"), Wm("L2xv"), Wm("L2xo"), bq=C("L2xbq"), bk=C("L2xbk"), bv=C("L2xbv"), bo=R("L2xb"), cross=True)
        expert_blocks()
        recurrent_block()
        key_masks("cell")
        source_stats("ln")
        fold_norms()
        attention("L3x", wp[:, 0, :], wp[:, 2, :], wp[:, 4, :], wp[:, 5, :], qs=wp[:, 1, :], ks=wp[:, 3, :], bq=colx[:, 0:1], bqs=colx[:, 1:2],
                  bk=colx[:, 2:3], bks=colx[:, 3:4], cq=4, ck=0, cross=True, norm="ln", mask=per_tile, ln_o=True)
        channel_mix()
        store()


def _swap(w, kind):
    n = w.shape[-1]
    order = np.arange(n) ^ 1 if kind == "pairs" else (np.arange(n) + n // 2) % n
    return w[..., order]


def _rope_tables():
    def table(power, pos, sign):
        inv = (np.float32(1.0) / np.float32(10000.0) ** power.astype(np.float32)).astype(np.float32)
        ang = (inv[:, None] * pos[None, :].astype(np.float32)).astype(np.float32)
        return np.cos(ang).astype(np.float32), (sign[:, None] * np.sin(ang)).astype(np.float32)

    f = np.arange(D)
    pairs = ((f % HD) // 2 * 2 / np.float32(HD))
    psign = np.where(f % 2 == 0, -1.0, 1.0).astype(np.float32)
    halves = (f % (D // 2)) / np.float32(D // 2)
    hsign = np.where(f < D // 2, -1.0, 1.0).astype(np.float32)
    pos = np.arange(SEQ)
    t = [*table(pairs, pos, psign), *table(halves, pos, hsign), *table(pairs, pos - SEQ // 2, psign)]
    return np.ascontiguousarray(np.stack(t, 1))


def kernel(**inputs):
    import concourse.bacc as bacc
    from concourse.bass_utils import run_bass_kernel_spmd

    a = {k: np.asarray(v) for k, v in inputs.items()}
    T = lambda n: a[n].T
    ipw, ipb = a["L1_ffn_in_proj_w"], a["L1_ffn_in_proj_b"]
    eye = np.eye(D, dtype=np.float32)
    w = {"I": eye, "SWAP": _swap(eye, "pairs"),
         "L0q": T("L0_attn_wq"), "L0qs": _swap(T("L0_attn_wq"), "pairs"), "L0k": T("L0_attn_wk"), "L0ks": _swap(T("L0_attn_wk"), "pairs"),
         "L0v": T("L0_attn_wv"), "L0o": T("L0_attn_wo"), "L0xo": T("L0_xattn_proj_w"),
         "L1xq": T("L1_xattn_Wq"), "L1xk": T("L1_xattn_Wk"), "L1xv": T("L1_xattn_Wv"), "L1xo": T("L1_xattn_Wo"),
         "L1fq": ipw[0:D].T, "L1fk": ipw[D:2 * D].T, "L1fv": ipw[2 * D:].T, "L1fo": T("L1_ffn_out_proj_w"),
         "L2q": T("L2_attn_Wq"), "L2qs": _swap(T("L2_attn_Wq"), "halves"), "L2k": T("L2_attn_Wk"), "L2ks": _swap(T("L2_attn_Wk"), "halves"),
         "L2v": T("L2_attn_Wv"), "L2o": T("L2_attn_Wo"),
         "L2xq": T("L2_xattn_Wq"), "L2xk": T("L2_xattn_Wk"), "L2xv": T("L2_xattn_Wv"), "L2xo": T("L2_xattn_Wo"),
         "L3xq": T("L3_xattn_w_q"), "L3xqs": _swap(T("L3_xattn_w_q"), "pairs"), "L3xk": T("L3_xattn_w_k"), "L3xks": _swap(T("L3_xattn_w_k"), "pairs"),
         "L3xv": T("L3_xattn_w_v"), "L3xo": T("L3_xattn_w_o"),
         "L2fa": T("L2_ffn_attn_w"), "L2fn": T("L2_ffn_next_w"), "L3Wx": a["L3_attn_Wx"], "L3Wy": a["L3_attn_Wy"], "L3Wi": a["L3_attn_Wi"],
         "L3Wa": a["L3_attn_Wa"], "L3Wo": a["L3_attn_Wo"], "L3fr": T("L3_ffn_W_r"), "L3fk": T("L3_ffn_W_k"), "L3fv": T("L3_ffn_W_v")}
    qn, kn = np.tile(a["L0_xattn_q_norm_w"], HEADS), np.tile(a["L0_xattn_k_norm_w"], HEADS)
    c = {"qn": qn, "qns": _swap(qn, "pairs"), "kn": kn, "kns": _swap(kn, "pairs"),
         "L1bq": a["L1_xattn_bq"], "L1bk": a["L1_xattn_bk"], "L1bv": a["L1_xattn_bv"], "L1fbq": ipb[0:D], "L1fbk": ipb[D:2 * D], "L1fbv": ipb[2 * D:],
         "L2bq": a["L2_attn_bq"], "L2bqs": _swap(a["L2_attn_bq"], "halves"), "L2bk": a["L2_attn_bk"], "L2bks": _swap(a["L2_attn_bk"], "halves"),
         "L2bv": a["L2_attn_bv"], "L2xbq": a["L2_xattn_bq"], "L2xbk": a["L2_xattn_bk"], "L2xbv": a["L2_xattn_bv"],
         "L3bq": a["L3_xattn_b_q"], "L3bqs": _swap(a["L3_xattn_b_q"], "pairs"), "L3bk": a["L3_xattn_b_k"], "L3bks": _swap(a["L3_xattn_b_k"], "pairs"),
         "L3gq": a["L3_xattn_ln_q_w"], "L3aq": a["L3_xattn_ln_q_b"], "L3gk": a["L3_xattn_ln_k_w"], "L3ak": a["L3_xattn_ln_k_b"],
         "L3gv": a["L3_xattn_ln_v_w"], "L3av": a["L3_xattn_ln_v_b"], "L3go": a["L3_xattn_ln_o_w"], "L3ao": a["L3_xattn_ln_o_b"], "L3bv": a["L3_xattn_b_v"],
         "L2fab": a["L2_ffn_attn_b"], "L2fnb": a["L2_ffn_next_b"], "n1": a["L3_attn_norm1_w"], "n2": a["L3_attn_norm2_w"], "cb": a["L3_attn_conv_b"],
         "lam": a["L3_attn_lam"], **{f"c{k}": a["L3_attn_conv_w"][k] for k in range(4)}, "mur": a["L3_ffn_mu_r"], "muk": a["L3_ffn_mu_k"],
         "L2g": a["L2_ffn_ln_scale"], "L2b": a["L2_ffn_ln_bias"]}
    r = {"L0xb": a["L0_xattn_proj_b"], "L1xb": a["L1_xattn_bo"], "L1fb": a["L1_ffn_out_proj_b"], "L2b": a["L2_attn_bo"], "L2xb": a["L2_xattn_bo"],
         "L3b": a["L3_xattn_b_o"], "g1": a["L1_ffn_ln1_g"], "b1": a["L1_ffn_ln1_b"], "g2": a["L1_ffn_ln2_g"], "b2": a["L1_ffn_ln2_b"]}
    q, k = np.arange(P)[:, None] % SEQ, np.arange(SEQ)[None, :]
    arrays = {
        "x": a["x"].reshape(TOK, D), "ctx": a["ctx_1024"].reshape(TOK, D), "ctxT": a["ctx_1024"].reshape(TOK, D).T,
        "mask": a["mask_BxS2_ik0"].reshape(TOK), "cell": a["itok_Bx1xSx1_0_63"].reshape(TOK), "cellT": a["itok_Bx1xSx1_0_63"].reshape(TILES, P).T,
        "W": np.stack([w[n] for n in SQ], 1), "col": np.stack([c[n] for n in COL], 1), "row": np.stack([r[n] for n in ROW], 0),
        "rope": _rope_tables(),
        "causal": np.where(k <= q, np.float32(0.0), np.float32(NEG)),
    }
    arrays |= {
        "w1a": a["L0_ffn_w1"].reshape(8, D, 2, 176).transpose(1, 2, 0, 3).reshape(D, 2, 11, 128), "w2a": a["L0_ffn_w2"].reshape(11, 128, D).transpose(1, 0, 2),
        "sel": np.tile((np.arange(8 * 176) // 176 == np.arange(8)[:, None]).astype(np.float32), (3, 1)).reshape(24, 11, 128), "rwa": a["L0_ffn_router_weight"],
        "w1b": a["L1_ffn_w1"].transpose(1, 0, 2), "w2b": a["L1_ffn_w2"].reshape(8, 2, 128, D).transpose(2, 0, 1, 3),
        "b1b": a["L1_ffn_b1"].reshape(8, 2, 128).transpose(2, 0, 1), "b2b": a["L1_ffn_b2"],
        "rwb": np.concatenate([a["L1_ffn_w_group"], a["L1_ffn_w_expert"].transpose(1, 0, 2).reshape(D, 8)], 1),
        "rbb": np.concatenate([a["L1_ffn_b_group"], a["L1_ffn_b_expert"].reshape(8)])}
    arrays |= {"w1c": a["L2_ffn_w1"].reshape(8 * D, 512), "w2c": a["L2_ffn_w2"].reshape(8 * 512, D),
               "b1c": a["L2_ffn_b1"].reshape(8, 4, 128).transpose(0, 2, 1).reshape(8 * 128, 4), "b2c": a["L2_ffn_b2"].T}
    arrays |= {"wg": a["L3_attn_Wg"], "wu": a["L3_attn_Wu"], "wd": a["L3_attn_Wd"].reshape(4, 128, D).transpose(1, 0, 2)}
    wk = a["L1_attn_Wk"].T.reshape(D, 4, 1, 64)
    arrays |= {"wq": a["L1_attn_Wq"].T.reshape(D, 8, 128), "wk": np.concatenate([wk, wk], 2), "wv": a["L1_attn_Wv"].T,
               "wo": a["L1_attn_Wo"].T.reshape(8, 128, D).transpose(1, 0, 2)}
    nc = bacc.Bacc("TRN2", target_bir_lowering=False, num_devices=1)
    arrays = {n: np.ascontiguousarray(v) for n, v in arrays.items()}
    io = {n: nc.dram_tensor("in_" + n, v.shape, mybir.dt.from_np(v.dtype), kind="ExternalInput").ap() for n, v in arrays.items()}
    out = nc.dram_tensor("out", (TOK, D), F32, kind="ExternalOutput").ap()
    build(nc, io, out)
    res = run_bass_kernel_spmd(nc, [{"in_" + n: v for n, v in arrays.items()}], core_ids=[0])
    return res.results[0]["out"].reshape(NB, SEQ, D)
```
